# Optimizing a Trainium2 kernel written in Bass

```python
import numpy as np
import jax
import jax.numpy as jnp

def _softmax(x, axis=-1):
    return jax.nn.softmax(x, axis=axis)

def _gelu(x):
    return jax.nn.gelu(x, approximate=True)

def _silu(x):
    return jax.nn.silu(x)

def _sigmoid(x):
    return jax.nn.sigmoid(x)

def _layernorm(x, axis=-1, eps=1e-05):
    m = jnp.mean(x, axis=axis, keepdims=True)
    v = jnp.var(x, axis=axis, keepdims=True)
    return (x - m) / jnp.sqrt(v + eps)

def _scatter_add(tgt, idx, src, axis=0):
    return tgt.at[idx].add(src)

def _segment_sum(src, seg, n):
    return jax.ops.segment_sum(src, seg, n)
kernel_name = 'mk_adj_ffn_d2_adj_r2_99be3e'

def setup_inputs(seed: int=0):
    np.random.seed(seed)
    _w = jnp.asarray

    def _rec_inputs():
        import jax
        import jax.numpy as jnp
        _gk = jax.random.key(seed)
        x = -0.0003929 + 0.9999 * jax.random.normal(jax.random.fold_in(_gk, 1), (32, 256, 128), jnp.float32)
        _a = jax.random.bernoulli(jax.random.fold_in(_gk, 2), 0.0078125, (256, 256))
        _af = _a.astype(jnp.float32)
        _af = _af / jnp.maximum(_af.sum(-1, keepdims=True), 1.0)
        adj = _af
        return (x, adj)
    x, adj = _rec_inputs()

    def _L0_gnn_setup():
        import jax, jax.numpy as jnp
        import numpy as np
        B, N, D = (128, 256, 128)

        def _make_adj(k):
            a = jax.random.uniform(k, (N, N), dtype=jnp.float32)
            mask = (jax.random.uniform(jax.random.fold_in(k, 1), (N, N)) < 4.0 / N).astype(jnp.float32)
            a = a * mask
            return a / (a.sum(axis=1, keepdims=True) + 1e-08)
        key = jax.random.key(seed)
        ks = jax.random.split(key, 8)
        x = jax.random.normal(ks[0], (B, N, D), dtype=jnp.float32)
        adj_in = _make_adj(ks[1])
        adj_out = _make_adj(ks[2])
        bias_in = jax.random.normal(ks[3], (N, D), dtype=jnp.float32) * 0.02
        bias_out = jax.random.normal(ks[4], (N, D), dtype=jnp.float32) * 0.02
        gate_w_in = jax.random.normal(ks[5], (D, 1), dtype=jnp.float32) * 0.02
        gate_b_in = jnp.zeros((N, 1), dtype=jnp.float32)
        gate_w_out = jax.random.normal(ks[6], (D, 1), dtype=jnp.float32) * 0.02
        gate_b_out = jnp.zeros((N, 1), dtype=jnp.float32)
        loop_gate = jax.random.normal(ks[7], (D, 1), dtype=jnp.float32) * 0.02
        return {'x': x, 'adj_in': adj_in, 'adj_out': adj_out, 'bias_in': bias_in, 'bias_out': bias_out, 'gate_w_in': gate_w_in, 'gate_b_in': gate_b_in, 'gate_w_out': gate_w_out, 'gate_b_out': gate_b_out, 'loop_gate': loop_gate}
    _L0_gnn_all = _L0_gnn_setup()
    _L0_gnn_in = {k: v for k, v in _L0_gnn_all.items() if k in ('bias_in', 'bias_out', 'gate_w_in', 'gate_b_in', 'gate_w_out', 'gate_b_out', 'loop_gate')}
    del _L0_gnn_all

    def _L0_ffn_setup():
        import jax, jax.numpy as jnp
        import numpy as np
        C = 128
        HID = 512
        E = 8
        TEMP = 1.0
        key = jax.random.key(seed)
        ks = jax.random.split(key, 7)
        x = jax.random.normal(ks[0], (8, 8192, C), dtype=jnp.float32)
        W1 = jax.random.normal(ks[1], (C, HID), dtype=jnp.float32) * 0.02
        b1 = jnp.zeros((HID,), dtype=jnp.float32)
        Wg = jax.random.normal(ks[2], (HID, E), dtype=jnp.float32) * 0.02
        bg = jnp.zeros((E,), dtype=jnp.float32)
        Wd = jax.random.normal(ks[3], (E, HID, C), dtype=jnp.float32) * 0.02
        bd = jnp.zeros((E, C), dtype=jnp.float32)
        return {'x': x, 'W1': W1, 'b1': b1, 'Wg': Wg, 'bg': bg, 'Wd': Wd, 'bd': bd}
    _L0_ffn_all = _L0_ffn_setup()
    _L0_ffn_in = {k: v for k, v in _L0_ffn_all.items() if k in ('W1', 'b1', 'Wg', 'bg', 'Wd', 'bd')}
    del _L0_ffn_all

    def _L1_gnn_setup():
        import jax, jax.numpy as jnp
        import numpy as np
        B, T, D, H = (64, 1024, 128, 128)
        MAX_SKIP = 4

        def _lstm_last(Wih, Whh, bih, bhh, xs):
            N, _, Hd = xs.shape
            bias = bih + bhh

            def step(carry, x_t):
                h, c = carry
                g = x_t @ Wih.T + h @ Whh.T + bias
                i, f, gg, o = jnp.split(g, 4, axis=-1)
                c = jax.nn.sigmoid(f) * c + jax.nn.sigmoid(i) * jnp.tanh(gg)
                h = jax.nn.sigmoid(o) * jnp.tanh(c)
                return ((h, c), None)
            init = (jnp.zeros((N, Hd), xs.dtype), jnp.zeros((N, Hd), xs.dtype))
            (h_last, _), _ = jax.lax.scan(step, init, jnp.swapaxes(xs, 0, 1))
            return h_last
        key = jax.random.key(seed)
        ks = jax.random.split(key, 8)
        s = 0.05
        x = jax.random.normal(ks[0], (B, T, D), jnp.float32)
        adj = jax.random.uniform(ks[1], (T, T), jnp.float32) / T
        Wg0 = jax.random.normal(ks[2], (D, H), jnp.float32) * s
        bg0 = jnp.zeros((H,), jnp.float32)
        Wg1 = jax.random.normal(ks[3], (H, H), jnp.float32) * s
        bg1 = jnp.zeros((H,), jnp.float32)
        Wih = jax.random.normal(ks[4], (MAX_SKIP, 4 * H, H), jnp.float32) * s
        Whh = jax.random.normal(ks[5], (MAX_SKIP, 4 * H, H), jnp.float32) * s
        bih = jax.random.normal(ks[6], (MAX_SKIP, 4 * H), jnp.float32) * s
        bhh = jax.random.normal(ks[7], (MAX_SKIP, 4 * H), jnp.float32) * s
        return dict(x=x, adj=adj, Wg0=Wg0, bg0=bg0, Wg1=Wg1, bg1=bg1, Wih=Wih, Whh=Whh, bih=bih, bhh=bhh)
    _L1_gnn_all = _L1_gnn_setup()
    _L1_gnn_in = {k: v for k, v in _L1_gnn_all.items() if k in ('Wg0', 'bg0', 'Wg1', 'bg1', 'Wih', 'Whh', 'bih', 'bhh')}
    del _L1_gnn_all

    def _L1_ffn_setup():
        import jax, jax.numpy as jnp
        import numpy as np
        N_EXPERTS = 8
        TOP_K = 2
        key = jax.random.key(seed)
        ks = jax.random.split(key, 5)
        B, T, C, E, H = (8, 1024, 128, 8, 341)
        scale = 1.0 / np.sqrt(C)
        return {'x': jax.random.normal(ks[0], (B, T, C), dtype=jnp.float32), 'router_w': jax.random.normal(ks[1], (E, C), dtype=jnp.float32) * scale, 'w1': jax.random.normal(ks[2], (E, H, C), dtype=jnp.float32) * scale, 'w2': jax.random.normal(ks[3], (E, C, H), dtype=jnp.float32) * (1.0 / np.sqrt(H)), 'w3': jax.random.normal(ks[4], (E, H, C), dtype=jnp.float32) * scale}
    _L1_ffn_all = _L1_ffn_setup()
    _L1_ffn_in = {k: v for k, v in _L1_ffn_all.items() if k in ('router_w', 'w1', 'w2', 'w3')}
    del _L1_ffn_all
    return {'x': x, 'adj': adj, 'L0_gnn_bias_in': _L0_gnn_in['bias_in'], 'L0_gnn_bias_out': _L0_gnn_in['bias_out'], 'L0_gnn_gate_w_in': _L0_gnn_in['gate_w_in'], 'L0_gnn_gate_b_in': _L0_gnn_in['gate_b_in'], 'L0_gnn_gate_w_out': _L0_gnn_in['gate_w_out'], 'L0_gnn_gate_b_out': _L0_gnn_in['gate_b_out'], 'L0_gnn_loop_gate': _L0_gnn_in['loop_gate'], 'L0_ffn_W1': _L0_ffn_in['W1'], 'L0_ffn_b1': _L0_ffn_in['b1'], 'L0_ffn_Wg': _L0_ffn_in['Wg'], 'L0_ffn_bg': _L0_ffn_in['bg'], 'L0_ffn_Wd': _L0_ffn_in['Wd'], 'L0_ffn_bd': _L0_ffn_in['bd'], 'L1_gnn_Wg0': _L1_gnn_in['Wg0'], 'L1_gnn_bg0': _L1_gnn_in['bg0'], 'L1_gnn_Wg1': _L1_gnn_in['Wg1'], 'L1_gnn_bg1': _L1_gnn_in['bg1'], 'L1_gnn_Wih': _L1_gnn_in['Wih'], 'L1_gnn_Whh': _L1_gnn_in['Whh'], 'L1_gnn_bih': _L1_gnn_in['bih'], 'L1_gnn_bhh': _L1_gnn_in['bhh'], 'L1_ffn_router_w': _L1_ffn_in['router_w'], 'L1_ffn_w1': _L1_ffn_in['w1'], 'L1_ffn_w2': _L1_ffn_in['w2'], 'L1_ffn_w3': _L1_ffn_in['w3']}

def reference(x, adj, L0_gnn_bias_in, L0_gnn_bias_out, L0_gnn_gate_w_in, L0_gnn_gate_b_in, L0_gnn_gate_w_out, L0_gnn_gate_b_out, L0_gnn_loop_gate, L0_ffn_W1, L0_ffn_b1, L0_ffn_Wg, L0_ffn_bg, L0_ffn_Wd, L0_ffn_bd, L1_gnn_Wg0, L1_gnn_bg0, L1_gnn_Wg1, L1_gnn_bg1, L1_gnn_Wih, L1_gnn_Whh, L1_gnn_bih, L1_gnn_bhh, L1_ffn_router_w, L1_ffn_w1, L1_ffn_w2, L1_ffn_w3):
    import jax
    import jax.numpy as jnp

    def _L0_gnn_ref(x, adj_in, adj_out, bias_in, bias_out, gate_w_in, gate_b_in, gate_w_out, gate_b_out, loop_gate):
        import jax, jax.numpy as jnp
        import numpy as np
        B, N, D = (128, 256, 128)

        def _make_adj(k):
            a = jax.random.uniform(k, (N, N), dtype=jnp.float32)
            mask = (jax.random.uniform(jax.random.fold_in(k, 1), (N, N)) < 4.0 / N).astype(jnp.float32)
            a = a * mask
            return a / (a.sum(axis=1, keepdims=True) + 1e-08)
        msg_in = (jnp.einsum('nm,bmd->bnd', adj_in, x) + bias_in) * jax.nn.sigmoid(x @ gate_w_in + gate_b_in)
        msg_out = (jnp.einsum('nm,bmd->bnd', adj_out, x) + bias_out) * jax.nn.sigmoid(x @ gate_w_out + gate_b_out)
        msg_loop = x * jax.nn.sigmoid(x @ loop_gate)
        return jax.nn.relu(msg_in + msg_out + msg_loop)

    def _L0_ffn_ref(x, W1, b1, Wg, bg, Wd, bd):
        import jax, jax.numpy as jnp
        import numpy as np
        C = 128
        HID = 512
        E = 8
        TEMP = 1.0
        orig_shape = x.shape
        xf = x.reshape(-1, orig_shape[-1])
        H = jax.nn.gelu(xf @ W1 + b1, approximate=False)
        probs = jax.nn.softmax((H @ Wg + bg) / TEMP, axis=-1)
        assign = jnp.argmax(probs, axis=-1)
        out = jnp.zeros_like(xf)
        for e in range(Wd.shape[0]):
            y = H @ Wd[e] + bd[e]
            sel = (assign == e)[:, None]
            out = out + jnp.where(sel, probs[:, e:e + 1] * y, 0.0)
        return out.reshape(orig_shape)

    def _L1_gnn_ref(x, adj, Wg0, bg0, Wg1, bg1, Wih, Whh, bih, bhh):
        import jax, jax.numpy as jnp
        import numpy as np
        B, T, D, H = (64, 1024, 128, 128)
        MAX_SKIP = 4

        def _lstm_last(Wih, Whh, bih, bhh, xs):
            N, _, Hd = xs.shape
            bias = bih + bhh

            def step(carry, x_t):
                h, c = carry
                g = x_t @ Wih.T + h @ Whh.T + bias
                i, f, gg, o = jnp.split(g, 4, axis=-1)
                c = jax.nn.sigmoid(f) * c + jax.nn.sigmoid(i) * jnp.tanh(gg)
                h = jax.nn.sigmoid(o) * jnp.tanh(c)
                return ((h, c), None)
            init = (jnp.zeros((N, Hd), xs.dtype), jnp.zeros((N, Hd), xs.dtype))
            (h_last, _), _ = jax.lax.scan(step, init, jnp.swapaxes(xs, 0, 1))
            return h_last
        h = jax.nn.relu(jnp.einsum('ts,bsh->bth', adj, x @ Wg0 + bg0))
        h = jax.nn.relu(jnp.einsum('ts,bsh->bth', adj, h @ Wg1 + bg1))
        Bv, Tv, Hd = h.shape
        for p in range(1, MAX_SKIP + 1):
            nw = Tv // p
            wins = h[:, :nw * p, :].reshape(Bv * nw, p, Hd)
            last = _lstm_last(Wih[p - 1], Whh[p - 1], bih[p - 1], bhh[p - 1], wins)
            idx = jnp.arange(nw) * p + (p - 1)
            h = h.at[:, idx, :].set(last.reshape(Bv, nw, Hd))
        return h

    def _L1_ffn_ref(x, router_w, w1, w2, w3):
        import jax, jax.numpy as jnp
        import numpy as np
        N_EXPERTS = 8
        TOP_K = 2
        B, T, C = x.shape
        flat = x.reshape(-1, C)
        logits = flat @ router_w.T
        probs = jax.nn.softmax(logits, axis=-1)
        topk_probs, topk_idx = jax.lax.top_k(probs, TOP_K)
        topk_probs = topk_probs / (jnp.sum(topk_probs, axis=-1, keepdims=True) + 1e-09)
        onehot = jax.nn.one_hot(topk_idx, N_EXPERTS, dtype=flat.dtype)
        gates = jnp.einsum('nk,nke->ne', topk_probs, onehot)
        h1 = jnp.einsum('nc,ehc->neh', flat, w1)
        h3 = jnp.einsum('nc,ehc->neh', flat, w3)
        h = jax.nn.silu(h1) * h3
        y = jnp.einsum('neh,ech->nec', h, w2)
        out = jnp.einsum('ne,nec->nc', gates, y)
        return out.reshape(B, T, C)
    x = x + _L0_gnn_ref(_layernorm(x, axis=-1), adj, adj, L0_gnn_bias_in, L0_gnn_bias_out, L0_gnn_gate_w_in, L0_gnn_gate_b_in, L0_gnn_gate_w_out, L0_gnn_gate_b_out, L0_gnn_loop_gate)
    x = x + _L0_ffn_ref(_layernorm(x, axis=-1), L0_ffn_W1, L0_ffn_b1, L0_ffn_Wg, L0_ffn_bg, L0_ffn_Wd, L0_ffn_bd)
    x = x + _L1_gnn_ref(_layernorm(x, axis=-1), adj, L1_gnn_Wg0, L1_gnn_bg0, L1_gnn_Wg1, L1_gnn_bg1, L1_gnn_Wih, L1_gnn_Whh, L1_gnn_bih, L1_gnn_bhh)
    x = x + _L1_ffn_ref(_layernorm(x, axis=-1), L1_ffn_router_w, L1_ffn_w1, L1_ffn_w2, L1_ffn_w3)
    return x

_drawn_inputs = setup_inputs


def setup_inputs(seed=0):
    import zlib

    import numpy as np

    out = dict(_drawn_inputs(seed))
    spreads = {'L0_gnn_gate_b_in': (0.0, 0.422),
     'L0_gnn_gate_b_out': (0.0, 0.38),
     'L0_ffn_b1': (0.0, 0.44),
     'L0_ffn_bg': (0.0, 0.1),
     'L0_ffn_bd': (0.0, 0.298),
     'L1_gnn_bg0': (0.0, 0.8),
     'L1_gnn_bg1': (0.0, 0.694)}
    factors = {'L0_gnn_bias_in': 3.59,
     'L0_gnn_bias_out': 3.659,
     'L0_ffn_W1': 2.837,
     'L0_ffn_Wg': 2.819,
     'L0_ffn_Wd': 3.15,
     'L1_gnn_Wg0': 5.395,
     'L1_gnn_Wg1': 4.782,
     'L1_gnn_Wih': 3.279,
     'L1_gnn_Whh': 7.125}
    for name, (base, spread) in spreads.items():
        noise = np.random.default_rng([zlib.crc32(name.encode()), seed]).standard_normal(out[name].shape)
        drawn = base * np.exp(spread * noise) if base else spread * noise
        out[name] = jnp.asarray(drawn.astype(out[name].dtype))
    for name, factor in factors.items():
        out[name] = (out[name] * factor).astype(out[name].dtype)
    return out
```

```python
from contextlib import ExitStack, contextmanager

import concourse.bass as bass
from concourse import mybir

P = 128
F32 = mybir.dt.float32
I32 = mybir.dt.int32
U32 = mybir.dt.uint32
ALU = mybir.AluOpType
ACT = mybir.ActivationFunctionType
AX_X = mybir.AxisListType.X
PE_ENGINE = mybir.EngineType.PE
DVE_ENGINE = mybir.EngineType.DVE
LN_EPS = 1e-5
RSQRT_MAGIC = 0x5F3759DF
TOPK_EPS = 1e-9
BANK = 512


def bcast(ap, axis, n):
    v = ap.unsqueeze(axis)
    shape = list(v.shape)
    shape[axis] = n
    return v.broadcast_to(shape)


class HiddenSems:

    def __init__(self, tr, xt, h, act, lg):
        self.tr, self.xt, self.h, self.act, self.lg = tr, xt, h, act, lg


class RouteSems(HiddenSems):

    def __init__(self, xn, tr, xt, h, act, lg, st, mx, ix, copied, flat, ranks, places, mask, tiles):
        super().__init__(tr, xt, h, act, lg)
        self.xn, self.st, self.mx, self.ix, self.copied = xn, st, mx, ix, copied
        self.flat, self.ranks, self.places, self.mask, self.tiles = flat, ranks, places, mask, tiles


@contextmanager
def pairs(eng, first, end):
    with eng.Fori(0, (end - first) // 2) as h:
        yield 2 * h + first


def build(nc, x, adj_t, bias_io, gate_w, gate_b, w1, b1, wg, bg, wd, bd, g0_w, g0_b, g1_w, g1_b, wih_t, whh_t, bih, bhh,
          router_t, up_t, down_t, out):
    TOK, D = x.shape
    NTILE = TOK // P
    N = adj_t.shape[0]
    MC = N // P
    E = router_t.shape[1]
    HID = w1.shape[1]
    KH = HID // P
    UP = up_t.shape[2] // 2
    KU = -(-UP // P)
    MAX_SKIP = wih_t.shape[0]
    GATES = 4
    assert D == P and E == 8 and MC == 2 and MAX_SKIP == 4

    NSLOT0 = -(-(NTILE + E - 1) // 4) * 4
    NSLOT1 = -(-(2 * NTILE + E - 1) // 8) * 8

    with ExitStack() as ctx:
        def sb(name, shape, dt=F32):
            return ctx.enter_context(nc.sbuf_tensor("sb_" + name, shape, dt))

        def sem(name):
            return ctx.enter_context(nc.semaphore(name))

        sorted_in = nc.dram_tensor("sorted_in", [NSLOT1 * P, D], F32, kind="Internal").ap()
        sorted_out = nc.dram_tensor("sorted_out", [NSLOT1 * P, D], F32, kind="Internal").ap()

        X = sb("X", [P, NTILE, D])
        R1 = sb("R1", [P, NTILE * D])
        R2 = sb("R2", [P, NTILE * D])
        XN = R1[:, :].rearrange("p (t d) -> p t d", d=D)
        xn = [sb(f"xn{u}", [P, 8, D]) for u in range(2)]
        xt = [sb(f"xt{u}", [P, 8 * P]) for u in range(2)]
        ident = sb("ident", [P, P])
        before = sb("before", [P, P])
        ones = sb("ones", [P, P])
        ones_row = sb("ones_row", [P, BANK])
        iota_e = sb("iota_e", [P, E])
        iota_t = sb("iota_t", [P, NTILE])
        iota_s = sb("iota_s", [1, NSLOT1])
        adj_sb = sb("adj_sb", [P, MC, N])
        bias_sb = sb("bias_sb", [P, MC, 2, D])
        gw_sb = sb("gw_sb", [P, 3])
        gb_sb = sb("gb_sb", [P, MC, 3])
        w1_sb = sb("w1_sb", [P, HID])
        b1_sb = sb("b1_sb", [P, KH])
        wg_sb = sb("wg_sb", [P, KH, E])
        bg_sb = sb("bg_sb", [P, E])
        BIG = sb("BIG", [P, E * (2 * UP + KU * D)])
        wd_sb = BIG[:, 0:KH * E * D].rearrange("p (k n) -> p k n", k=KH)
        bd_sb = BIG[:, KH * E * D:(KH + 1) * E * D]
        up_sb = BIG[:, 0:E * 2 * UP]
        down_sb = BIG[:, E * 2 * UP:E * (2 * UP + KU * D)]
        g0_sb = sb("g0_sb", [P, D])
        g1_sb = sb("g1_sb", [P, D])
        g0b_sb = sb("g0b_sb", [P, 1])
        g1b_sb = sb("g1b_sb", [P, D])
        bga_sb = sb("bga_sb", [P, N])
        wih_sb = sb("wih_sb", [P, MAX_SKIP, GATES * P])
        whh_sb = sb("whh_sb", [P, MAX_SKIP, GATES * P])
        bih_sb = sb("bih_sb", [P, MAX_SKIP * GATES])
        bhh_sb = sb("bhh_sb", [P, MAX_SKIP * GATES])
        lb_sb = sb("lb_sb", [P, MAX_SKIP * GATES])
        rt_sb = sb("rt_sb", [P, E])
        ST = sb("ST", [P, NTILE, 6])
        MEAN = sb("MEAN", [P, NTILE])
        RSTD = sb("RSTD", [P, NTILE])
        ln_t = sb("ln_t", [P, 4, NTILE])
        ln_i = sb("ln_i", [P, 2, NTILE], I32)
        MX = sb("MX", [P, NTILE, E])
        IX = sb("IX", [P, NTILE, E])
        lg_st = [sb(f"lg_st{u}", [P, 4, E]) for u in range(2)]
        mx_st = [sb(f"mx_st{u}", [P, 4, E]) for u in range(2)]
        ix_st = [sb(f"ix_st{u}", [P, 4, E], U32) for u in range(2)]
        wait_c = [sb(f"wait_c{u}", [P, 2]) for u in range(2)]
        GT = sb("GT", [P, 2, NTILE])
        dest_i = sb("dest_i", [P, 2, NTILE], I32)
        tile_e = sb("tile_e", [1, NSLOT1], I32)
        yo = [sb(f"yo{u}", [P, 8, D]) for u in range(2)]

        bank = [ctx.enter_context(nc.psum_tensor(f"bank{i}", [P, BANK], F32)) for i in range(8)]

        def view(region, at, *shape):
            n = 1
            for s in shape:
                n *= s
            names = "abcd"[:len(shape)]
            v = region[:, at:at + n]
            if len(shape) == 1:
                return v
            return v.rearrange(f"p ({' '.join(names)}) -> p {' '.join(names)}", **dict(zip(names, shape)))

        block = ctx.enter_context(nc.Block())

        NX = 8
        x_in = [sem(f"x_in{i}") for i in range(NX)]
        w_in = sem("w_in")
        w_in_n = [0]
        up_in = sem("up_in")
        const_ready = sem("const_ready")
        zero_ready = sem("zero_ready")
        zeroed = sem("zeroed")

        loads_w = [
            (adj_sb[:, :, :], adj_t.rearrange("(c p) n -> p c n", p=P)),
            (bias_sb[:, :, :, :].rearrange("p c i d -> p c (i d)"), bias_io.rearrange("(c p) n -> p c n", p=P)),
            (gw_sb[:, :], gate_w),
            (gb_sb[:, :, :], gate_b.rearrange("(c p) n -> p c n", p=P)),
            (w1_sb[:, :], w1),
            (b1_sb[:, :], b1),
            (wg_sb[:, :, :], wg.rearrange("(k p) e -> p k e", p=P)),
            (bg_sb[:, :], bg.partition_broadcast(P)),
            (wd_sb, wd.rearrange("(k p) n -> p k n", p=P)),
            (bd_sb, bd.partition_broadcast(P)),
            (g0_sb[:, :], g0_w), (g1_sb[:, :], g1_w), (g0b_sb[:, :], g0_b),
            (g1b_sb[:, :], g1_b.partition_broadcast(P)),
            (wih_sb[:, :, :], wih_t.rearrange("s p n -> p s n")),
            (whh_sb[:, :, :], whh_t.rearrange("s p n -> p s n")),
            (bih_sb[:, :], bih), (bhh_sb[:, :], bhh), (rt_sb[:, :], router_t),
        ]
        W_ALL = 16 * len(loads_w)

        NA = NTILE // 8
        a_xn, a_tr, a_xt, a_z, a_ax, a_zb, a_th, a_s, a_q, a_t1, a_x = (
            sem("a_" + n) for n in "normed transposed copied z mixed zbias tanh gate bias scaled done".split())
        zb = [view(R2, u * 24, 8, 3) for u in range(2)]
        th = [view(R2, 64 + u * 24, 8, 3) for u in range(2)]
        sg = [view(R2, 128 + u * 24, 8, 3) for u in range(2)]
        us = [view(R2, 192 + u * 8, 8) for u in range(2)]
        q1 = [view(R2, 512 + u * 1024, 8, D) for u in range(2)]
        q2 = view(R2, 2560, 8, D)
        q3 = view(R2, 3584, 8, D)
        t1 = view(R2, 4608, 8, D)
        ZW = 17 * D
        zero = view(R2, 5632, ZW)

        row_sums = sem("row_sums")
        dve_step = sem("dve_step")
        pool_step = sem("pool_step")
        n_dve = [0]
        n_pool = [0]

        def link(eng, ins):
            ins.then_inc(dve_step, 1)
            n_dve[0] += 1
            eng.wait_ge(dve_step, n_dve[0])

        def route_sems(tag):
            return RouteSems(*(sem(f"{tag}_{n}") for n in (
                "normed", "transposed", "copied", "hidden", "gelu", "logits", "staged", "sorted", "chosen", "indexed",
                "softmax", "ranks", "places", "mask", "tiles")))

        rb, rd = route_sems("b1"), route_sems("d1")
        NG = NTILE // 4
        Ht = [view(R2, u * KH * BANK, KH, BANK) for u in range(2)]
        RW = 2 * KH * BANK
        oh = [view(R2, RW + k * BANK, E, NTILE) for k in range(2)]
        mask = view(R2, RW + 2 * BANK, E, NTILE)
        tot = view(R2, RW + 3 * BANK, E, NTILE)
        cum = view(R2, RW + 4 * BANK, E, NTILE)
        rw1 = view(R2, RW + 5 * BANK, E, NTILE)
        rw2 = view(R2, RW + 6 * BANK, E, NTILE)
        small = view(R2, RW + 7 * BANK, 16, E)
        dest_f = view(R2, RW + 7 * BANK + 128, 2, NTILE)
        tcmp = view(R2, 0, NSLOT1, E)

        s_scat = {0: sem("b_scattered"), 1: sem("d_scattered")}
        s_gath = {0: [sem(f"b_gathered{i}") for i in range(NX)], 1: [sem(f"d_gathered{i}") for i in range(NX)]}
        b2_in = [sem("b2_in0"), sem("b2_in1")]
        b2_tr, b2_xt, b2_h, b2_act, b2_y, b2_yo = (sem("b2_" + n) for n in "tr xt h act y yo".split())
        b2_out = [sem("b2_out0"), sem("b2_out1")]
        xs = xn
        NB2 = NSLOT0 // 4
        b3_x, b3_t = sem("b3_x"), sem("b3_t")

        c1_xn, c1_ax, c1_axc, c1_h, c1_hb, c1_hr, c1_z, c1_zc, c1_g, c1_f = (
            sem("g_" + n) for n in "normed mixed mixed_sb h0 h0_biased h0_relu z1 z1_sb h1 done".split())
        F = R2
        axt = [view(R1, u * BANK, BANK) for u in range(2)]
        hb = [view(R1, (2 + u) * BANK, BANK) for u in range(2)]
        h1 = [view(R1, (4 + u) * BANK, BANK) for u in range(2)]
        zs = [view(R1, (6 + u) * BANK, 4, P) for u in range(2)]

        l_x, l_g, l_act, l_ig, l_fc, l_c, l_tc, l_h = (sem("l_" + n) for n in "x g act ig fc c tc h".split())
        gb = [[view(R1, (u * GATES + k) * BANK, BANK) for k in range(GATES)] for u in range(2)]
        cst = [view(R1, (8 + u) * BANK, BANK) for u in range(2)]
        tcs = [view(R1, (10 + u) * BANK, BANK) for u in range(2)]
        hst = [view(R1, (12 + u) * BANK, BANK) for u in range(2)]

        t_st, t_tr, t_x, t_ln = (sem("t_" + n) for n in "st tr x ln".split())

        ND2 = NSLOT1 // 8
        d2_in = [sem("d2_in0"), sem("d2_in1")]
        d2_tr, d2_xt, d2_h, d2_silu, d2_m, d2_tt, d2_tc, d2_y, d2_yo = (
            sem("d2_" + n) for n in "tr xt h silu m tt tc y yo".split())
        d2_out = [sem("d2_out0"), sem("d2_out1")]
        sl = [view(R2, u * 384, UP) for u in range(2)]
        hm = [view(R2, 768 + u * 384, UP) for u in range(2)]
        ht = [view(R2, 1536 + u * 384, KU, P) for u in range(2)]
        Y1 = view(R2, 0, NTILE, D)
        d3_x, d3_t = sem("d3_x"), sem("d3_t")
        out_sem = sem("out_sem")

        lstm_steps = []
        NSUP = 4
        for half in range(2):
            for s in range(2):
                lstm_steps.append((1, 0, s, NSUP * s + 2 * half, 2))
        for p in range(2, MAX_SKIP + 1):
            for t in range(p):
                for s in range(2):
                    lstm_steps.append((p, t, s, NSUP * s, NSUP))
        NL = len(lstm_steps)
        LB = TOK // (2 * NSUP * N)

        @block.sync
        def _(sp):
            for g in range(NX):
                sp.dma_start(X[:, 8 * g:8 * g + 8, :],
                             x.rearrange("(t p) d -> p t d", p=P)[:, 8 * g:8 * g + 8, :]).then_inc(x_in[g], 16)
                if g == 0:
                    for dst, src in loads_w[:4]:
                        sp.dma_start(dst, src).then_inc(w_in, 16)
            for dst, src in loads_w[4:]:
                sp.dma_start(dst, src).then_inc(w_in, 16)
            sp.wait_ge(zero_ready, 1)
            zv = sorted_in.rearrange("(p n) d -> p (n d)", p=P)
            for i in range(NSLOT1 * D // ZW):
                sp.dma_start(zv[:, i * ZW:(i + 1) * ZW], zero).then_inc(zeroed, 16)

            def b2_body(g, u):
                sp.wait_ge(b2_tr, g - 1) if not isinstance(g, int) or g >= 2 else None
                sp.dma_start(xs[u][:, 0:4, :], sorted_in[bass.ds(g * 4 * P, 4 * P), :].rearrange(
                    "(t p) d -> p t d", p=P)).then_inc(b2_in[u], 16)

            def b2_store(g, u):
                sp.wait_ge(b2_yo, g + 1)
                sp.dma_start(sorted_out[bass.ds(g * 4 * P, 4 * P), :].rearrange("(t p) d -> p t d", p=P),
                             yo[u][:, 0:4, :]).then_inc(b2_out[u], 16)

            sp.wait_ge(s_scat[0], 16 * NTILE)
            b2_body(0, 0)
            b2_body(1, 1)
            with pairs(sp, 2, NB2) as g:
                for u in range(2):
                    b2_body(g + u, u)
                    b2_store(g + u - 2, u)
            b2_store(NB2 - 2, 0)
            b2_store(NB2 - 1, 1)
            sp.wait_ge(b2_y, NB2)
            sp.wait_ge(b2_yo, NB2)
            sp.dma_start(up_sb, up_t.rearrange("e p n -> p e n")).then_inc(up_in, 16)
            dv = down_sb.rearrange("p (e k d) -> p e k d", k=KU, d=D)
            for k in range(KU):
                kk = min(P, UP - k * P)
                sp.dma_start(dv[0:kk, :, k, :], down_t[:, k * P:k * P + kk, :].rearrange("e p d -> p e d")).then_inc(up_in, 16)

            def d2_body(g, u):
                if not isinstance(g, int) or g >= 2:
                    sp.wait_ge(d2_tr, g - 1)
                sp.dma_start(xs[u][:, :, :], sorted_in[bass.ds(g * 8 * P, 8 * P), :].rearrange(
                    "(t p) d -> p t d", p=P)).then_inc(d2_in[u], 16)

            def d2_store(g, u):
                sp.wait_ge(d2_yo, 8 * g + 8)
                sp.dma_start(sorted_out[bass.ds(g * 8 * P, 8 * P), :].rearrange("(t p) d -> p t d", p=P),
                             yo[u][:, :, :]).then_inc(d2_out[u], 16)

            sp.wait_ge(s_scat[1], 32 * NTILE)
            d2_body(0, 0)
            d2_body(1, 1)
            nb = (ND2 - 2) // 2 * 2
            with pairs(sp, 2, 2 + nb) as g:
                for u in range(2):
                    d2_body(g + u, u)
                    d2_store(g + u - 2, u)
            for g in range(2 + nb, ND2):
                d2_body(g, g % 2)
                d2_store(g - 2, g % 2)
            for g in range(ND2 - 2, ND2):
                d2_store(g, g % 2)
            for g in range(NX):
                sp.wait_ge(d3_x, 16 * (g + 1))
                sp.dma_start(out.rearrange("(t p) d -> p t d", p=P)[:, 8 * g:8 * g + 8, :],
                             X[:, 8 * g:8 * g + 8, :]).then_inc(out_sem, 16)
            sp.wait_ge(out_sem, 16 * NX)
        @block.gpsimd
        def _(pool):
            def step(ins):
                ins.then_inc(pool_step, 1)
                n_pool[0] += 1
                pool.wait_ge(pool_step, n_pool[0])

            pool.memset(zero, 0.0).then_inc(zero_ready, 1)
            step(pool.memset(ident[:, :], 0.0))
            step(pool.affine_select(out=ident[:, :], in_=ident[:, :], compare_op=ALU.not_equal, fill=1.0, base=0,
                                    pattern=[[-1, P]], channel_multiplier=1))
            pool.memset(ones_row[:, :], 1.0)
            step(pool.memset(ones[:, :], 1.0))
            step(pool.affine_select(out=before[:, :], in_=ones[:, :], compare_op=ALU.is_gt, fill=0.0, base=0,
                                    pattern=[[1, P]], channel_multiplier=-1))
            pool.iota(iota_e[:, :], [[1, E]], base=0, channel_multiplier=0, allow_small_or_imprecise_dtypes=True)
            pool.iota(iota_t[:, :], [[P, NTILE]], base=0, channel_multiplier=0, allow_small_or_imprecise_dtypes=True)
            pool.iota(iota_s[:, :], [[1, NSLOT1]], base=0, channel_multiplier=0,
                      allow_small_or_imprecise_dtypes=True).then_inc(const_ready, 1)

            pool.wait_ge(w_in, W_ALL)
            p0 = n_pool[0]
            with pairs(pool, 0, NA) as g0:
                for u in range(2):
                    g = g0 + u
                    pool.wait_ge(a_s, g + 1)
                    pool.wait_ge(a_q, g)
                    xv = xn[u][:, :, :]
                    for q, src, k in ((q1[u], bias_sb, 0), (q2, bias_sb, 1), (q3, None, 2)):
                        s = sg[u][:, :, k]
                        if src is None:
                            ins = pool.tensor_tensor(q, xv, bcast(s, 2, D), ALU.mult)
                        else:
                            if k == 0:
                                pool.wait_ge(a_t1, g)
                            ins = pool.tensor_tensor(
                                q.rearrange("p (b c) d -> p b c d", c=MC), bcast(src[:, :, k, :], 1, 8 // MC),
                                bcast(s.rearrange("p (b c) -> p b c", c=MC), 3, D), ALU.mult)
                        ins.then_inc(pool_step, 1)
                    pool.wait_ge(pool_step, p0 + 4 * g + 3)
                    pool.tensor_tensor(q1[u], q1[u], q2, ALU.add).then_inc(pool_step, 1)
                    pool.wait_ge(pool_step, p0 + 4 * g + 4)
                    pool.tensor_tensor(q1[u], q1[u], q3, ALU.add).then_inc(a_q, 1)

            def scatter(layer, places, K):
                pool.wait_ge(places, 1)
                pool.wait_ge(zeroed, 16 * (NSLOT1 * D // ZW))
                for t in range(NTILE):
                    for k in range(K):
                        pool.indirect_dma_start(
                            out=sorted_in, out_offset=bass.IndirectOffsetOnAxis(ap=dest_i[:, k, t:t + 1], axis=0),
                            in_=XN[:, t, :], in_offset=None).then_inc(s_scat[layer], 16)

            scatter(0, rb.places, 1)
            pool.wait_ge(b2_out[0], 16 * (NB2 - NB2 // 2))
            pool.wait_ge(b2_out[1], 16 * (NB2 // 2))
            pool.wait_ge(s_scat[0], 16 * NTILE)
            for t in range(NTILE):
                pool.indirect_dma_start(
                    out=XN[:, t, :], out_offset=None, in_=sorted_out[0:NSLOT0 * P, :],
                    in_offset=bass.IndirectOffsetOnAxis(ap=dest_i[:, 0, t:t + 1], axis=0)).then_inc(s_gath[0][t // 8], 16)
            scatter(1, rd.places, 2)
            pool.wait_ge(d2_out[0], 16 * (ND2 - ND2 // 2))
            pool.wait_ge(d2_out[1], 16 * (ND2 // 2))
            pool.wait_ge(s_scat[1], 32 * NTILE)
            for t in range(NTILE):
                for k in range(2):
                    dst = XN[:, t, :] if k == 0 else Y1[:, t, :]
                    pool.indirect_dma_start(
                        out=dst, out_offset=None, in_=sorted_out,
                        in_offset=bass.IndirectOffsetOnAxis(ap=dest_i[:, k, t:t + 1], axis=0)).then_inc(s_gath[1][t // 8], 16)

        @block.scalar
        def _(act):
            act.wait_ge(w_in, W_ALL)
            with pairs(act, 0, NA) as g0:
                for u in range(2):
                    g = g0 + u
                    act.wait_ge(a_tr, g + 1)
                    for h in range(2):
                        ins = act.activation(xt[u][:, h * BANK:(h + 1) * BANK], bank[h][:, :], ACT.Copy)
                    ins.then_inc(a_xt, 1)
                    act.wait_ge(a_zb, g + 1)
                    act.activation(th[u], zb[u], ACT.Tanh, scale=0.5).then_inc(a_th, 1)

            def b_act(r, g, u, last):
                for k in range(KH):
                    act.wait_ge(r.h, KH * g + k + 1)
                    if k == 0 and (not isinstance(g, int) or g >= 2):
                        act.wait_ge(r.lg, g - 1)
                    act.activation(Ht[u][:, k, :], bank[2 + k][:, :], ACT.Gelu, bias=b1_sb[:, k:k + 1]).then_inc(r.act, 1)
                if not last:
                    copy_xt(r, g + 1, 1 - u)

            def copy_xt(r, g, u, gelu=True):
                act.wait_ge(r.tr, g + 1)
                act.activation(xt[u][:, 0:BANK], bank[u][:, :], ACT.Copy).then_inc(r.xt, 1)

            def hidden_loop(r, NGR):
                copy_xt(r, 0, 0)
                b_act(r, 0, 0, False)
                b_act(r, 1, 1, False)
                with pairs(act, 2, NGR - 2) as g:
                    for u in range(2):
                        b_act(r, g + u, u, False)
                b_act(r, NGR - 2, 0, False)
                b_act(r, NGR - 1, 1, True)

            hidden_loop(rb, NG)
            act.wait_ge(rb.flat, 1)
            act.activation(rw1, rw2, ACT.Exp).then_inc(rb.flat, 1)
            r2 = HiddenSems(b2_tr, b2_xt, b2_h, b2_act, b2_y)
            hidden_loop(r2, NB2)

            with pairs(act, 0, NG) as g0:
                for u in range(2):
                    g = g0 + u
                    act.wait_ge(c1_ax, g + 1)
                    act.wait_ge(b3_x, NTILE)
                    act.activation(axt[u], bank[4 * u][:, :], ACT.Copy).then_inc(c1_axc, 1)
                for u in range(2):
                    g = g0 + u
                    act.wait_ge(c1_hb, g + 1)
                    act.activation(h1[u], hb[u], ACT.Relu).then_inc(c1_hr, 1)
                for u in range(2):
                    g = g0 + u
                    act.wait_ge(c1_g, g + 1)
                    act.activation(F[:, bass.ds(g * BANK, BANK)], bank[4 * u + 3][:, :], ACT.Relu).then_inc(c1_f, 1)

            funcs = (ACT.Sigmoid, ACT.Sigmoid, ACT.Tanh, ACT.Sigmoid)
            act.wait_ge(c1_f, NG)
            act.wait_ge(c1_zc, NG)
            with act.Fori(0, LB) as it:
                for n, (p, t, s, b0, nb) in enumerate(lstm_steps):
                    c = nb * (N // p)
                    act.wait_ge(l_g, it * NL + n + 1)
                    if n >= 2:
                        act.wait_ge(l_h, it * NL + n - 1)
                    else:
                        act.wait_ge(l_h, it * NL)
                    for k in (0, 2, 1, 3):
                        if k == 1 and t == 0:
                            continue
                        act.activation(gb[s][k][:, 0:c], bank[4 * s + k][:, 0:c], funcs[k],
                                       bias=lb_sb[:, (p - 1) * GATES + k:(p - 1) * GATES + k + 1]).then_inc(l_act, 1)
                    act.wait_ge(l_c, it * NL + n + 1)
                    act.activation(tcs[s][:, 0:c], cst[s][:, 0:c], ACT.Tanh).then_inc(l_tc, 1)
            act.wait_ge(l_h, LB * NL)
            with pairs(act, 0, NG) as g0:
                for u in range(2):
                    g = g0 + u
                    act.wait_ge(t_tr, g0)
                    act.activation(xt[u][:, 0:BANK], F[:, bass.ds(g * BANK, BANK)], ACT.Copy).then_inc(t_st, 1)
            with pairs(act, 0, NG) as g0:
                for u in range(2):
                    g = g0 + u
                    act.wait_ge(rd.tr, g + 1)
                    act.wait_ge(rd.lg, g0)
                    act.wait_ge(t_x, NG)
                    act.activation(xt[u][:, 0:BANK], bank[u][:, :], ACT.Copy).then_inc(rd.xt, 1)
            act.wait_ge(rd.flat, 1)
            act.activation(rw1, rw2, ACT.Exp).then_inc(rd.flat, 1)

            def d2_group(g, u, first):
                act.wait_ge(d2_tr, g + 1)
                if not first:
                    act.wait_ge(d2_h, 8 * g)
                for h in range(2):
                    ins = act.activation(xt[u][:, h * BANK:(h + 1) * BANK], bank[h][:, :], ACT.Copy)
                ins.then_inc(d2_xt, 1)

            def d2_tile(i, j):
                act.wait_ge(d2_h, i + 1)
                if not (isinstance(i, int) and i < 2):
                    act.wait_ge(d2_m, i - 1)
                act.activation(sl[j % 2], bank[2 + 2 * (j % 2)][:, 0:UP], ACT.Silu).then_inc(d2_silu, 1)

            def d2_tcopy(i, j):
                act.wait_ge(d2_tt, i + 1)
                if not (isinstance(i, int) and i < 2):
                    act.wait_ge(d2_y, i - 1)
                kf = UP // P
                act.activation(ht[j % 2][:, 0:kf, :], bank[6][:, 0:kf * P].rearrange("p (k n) -> p k n", n=P), ACT.Copy)
                act.activation(ht[j % 2][0:UP - kf * P, kf, :], bank[6][0:UP - kf * P, kf * P:(kf + 1) * P],
                               ACT.Copy).then_inc(d2_tc, 1)

            def d2_body_act(g, u, first, last):
                for j in range(10):
                    if j < 8:
                        d2_tile(8 * g + j, j)
                    if 1 <= j < 9:
                        d2_tcopy(8 * g + j - 1, j - 1)
                if not last:
                    d2_group(g + 1, 1 - u, False)

            act.wait_ge(rd.ix, NG)
            act.wait_ge(rd.places, 1)
            d2_group(0, 0, True)
            d2_body_act(0, 0, True, False)
            nb = (ND2 - 2) // 2 * 2
            with pairs(act, 1, 1 + nb) as g:
                d2_body_act(g, 1, False, False)
                d2_body_act(g + 1, 0, False, False)
            for g in range(1 + nb, ND2):
                d2_body_act(g, g % 2, False, g == ND2 - 1)

        @block.tensor
        def _(pe):
            def load_experts(first, n):
                _, r = nc.values_load_multi_w_load_instructions(
                    tile_e[0:1, bass.ds(first, n)], engines=[PE_ENGINE], min_val=0, max_val=E - 1,
                    skip_runtime_bounds_check_because="clamped to the last expert where it is computed")
                return r

            pe.wait_ge(const_ready, 1)
            pe.wait_ge(w_in, W_ALL)
            for m in range(MC):
                mm = pe.matmul(bank[3][:, 0:N], ones[:, :], adj_sb[:, m, :], start=(m == 0), stop=(m == MC - 1))
            mm.then_inc(row_sums, 1)
            with pairs(pe, 0, NA) as g0:
                for u in range(2):
                    g = g0 + u
                    pe.wait_ge(a_xn, g + 1)
                    for j in range(8):
                        tr = pe.transpose(bank[j // 4][:, (j % 4) * P:(j % 4 + 1) * P], xn[u][:, j, :], ident[:, :])
                    tr.then_inc(a_tr, 1)
                    xv = xn[u][:, :, :].rearrange("p (b c) d -> p b c d", c=MC)
                    pe.wait_ge(a_t1, g0)
                    for nch in range(MC):
                        for m in range(MC):
                            mm = pe.matmul(bank[4 + 2 * u + nch][:, :].rearrange("p (b d) -> p b d", d=D),
                                           adj_sb[:, m, nch * P:(nch + 1) * P], xv[:, :, m, :],
                                           start=(m == 0), stop=(m == MC - 1))
                    mm.then_inc(a_ax, 1)
                    pe.wait_ge(a_xt, g + 1)
                    pe.wait_ge(a_zb, g)
                    for j in range(8):
                        mm = pe.matmul(bank[2][:, 3 * j:3 * j + 3], xt[u][:, j * P:(j + 1) * P], gw_sb[:, :],
                                       start=True, stop=True)
                    mm.then_inc(a_z, 1)

            def transposes4(src, dst, s):
                for j in range(4):
                    tr = pe.transpose(dst[:, j * P:(j + 1) * P], src[:, j, :], ident[:, :])
                tr.then_inc(s, 1)

            def b1_t(r, g, u, xsem):
                pe.wait_ge(*xsem)
                if not (isinstance(g, int) and g < 2):
                    pe.wait_ge(r.xt, g - 1)
                transposes4(xn[u], bank[u], r.tr)

            def w1_mm(r, g, u):
                pe.wait_ge(r.xt, g + 1)
                for k in range(KH):
                    if not (isinstance(g, int) and g < 1):
                        pe.wait_ge(r.act, KH * (g - 1) + k + 1)
                    pe.matmul(bank[2 + k][:, :], w1_sb[:, k * P:(k + 1) * P], xt[u][:, 0:BANK],
                              start=True, stop=True).then_inc(r.h, 1)

            def b1_logits(r, g, u):
                if not (isinstance(g, int) and g < 2):
                    pe.wait_ge(r.st, g - 1)
                for k in range(KH):
                    pe.wait_ge(r.act, KH * g + k + 1)
                    for j in range(4):
                        mm = pe.matmul(bank[6 + u][:, j * E:(j + 1) * E], Ht[u][:, k, j * P:(j + 1) * P], wg_sb[:, k, :],
                                       start=(k == 0 and j == 0), stop=(k == KH - 1), skip_group_check=True)
                mm.then_inc(r.lg, 1)

            def b1_body(g, u, last):
                w1_mm(rb, g, u)
                if not last:
                    b1_t(rb, g + 1, 1 - u, (rb.xn, g + 2))
                b1_logits(rb, g, u)

            pe.wait_ge(a_x, NA)
            b1_t(rb, 0, 0, (rb.xn, 1))
            b1_body(0, 0, False)
            b1_body(1, 1, False)
            with pairs(pe, 2, NG - 2) as g:
                for u in range(2):
                    b1_body(g + u, u, False)
            b1_body(NG - 2, 0, False)
            b1_body(NG - 1, 1, True)

            def rank(r):
                pe.wait_ge(r.mask, 1)
                flat = mask.rearrange("p e t -> p (e t)")
                pe.matmul(bank[0][:, :], before[:, :], flat, start=True, stop=True)
                pe.matmul(bank[1][:, :], ones[:, :], flat, start=True, stop=True).then_inc(r.ranks, 1)

            rank(rb)

            def b2_t(g, u):
                pe.wait_ge(b2_in[u], 16 * (g // 2 + 1) if isinstance(g, int) else 0)

            def y_mm(g, u):
                er = load_experts(4 * g, 4)
                if not (isinstance(g, int) and g < 2):
                    pe.wait_ge(b2_yo, g - 1)
                for k in range(KH):
                    pe.wait_ge(b2_act, KH * g + k + 1)
                    for j in range(4):
                        mm = pe.matmul(bank[6 + u][:, j * P:(j + 1) * P], Ht[u][:, k, j * P:(j + 1) * P],
                                       wd_sb[:, k, bass.ds(er[j] * D, D)],
                                       start=(k == 0 and j == 0), stop=(k == KH - 1), skip_group_check=True)
                mm.then_inc(b2_y, 1)

            r2 = HiddenSems(b2_tr, b2_xt, b2_h, b2_act, b2_y)
            pe.wait_ge(rb.tiles, 1)
            b1_t(r2, 0, 0, (b2_in[0], 16))

            def b2_pe(g, u, g2, last):
                w1_mm(r2, g, u)
                if not last:
                    b1_t(r2, g + 1, 1 - u, (b2_in[1 - u], 16 * g2))
                y_mm(g, u)

            b2_pe(0, 0, 1, False)
            b2_pe(1, 1, 2, False)
            with pe.Fori(1, NB2 // 2 - 1) as h:
                b2_pe(2 * h, 0, h + 1, False)
                b2_pe(2 * h + 1, 1, h + 2, False)
            b2_pe(NB2 - 2, 0, NB2 // 2, False)
            b2_pe(NB2 - 1, 1, 0, True)

            pe.wait_ge(b2_yo, NB2)
            with pairs(pe, 0, NG) as g0:
                for u in range(2):
                    g = g0 + u
                    pe.wait_ge(c1_xn, g + 1)
                    for b in range(2):
                        for m in range(MC):
                            mm = pe.matmul(bank[4 * u][:, b * N:(b + 1) * N], xn[u][:, MC * b + m, :], adj_sb[:, m, :],
                                           start=(m == 0), stop=(m == MC - 1))
                    mm.then_inc(c1_ax, 1)
                for u in range(2):
                    g = g0 + u
                    pe.wait_ge(c1_axc, g + 1)
                    pe.matmul(bank[4 * u + 1][:, :], g0_sb[:, :], axt[u], start=True, stop=True).then_inc(c1_h, 1)
                for u in range(2):
                    g = g0 + u
                    pe.wait_ge(c1_hr, g + 1)
                    for j in range(4):
                        mm = pe.matmul(bank[4 * u + 2][:, j * P:(j + 1) * P], h1[u][:, j * P:(j + 1) * P], g1_sb[:, :],
                                       start=True, stop=True)
                    mm.then_inc(c1_z, 1)
                for u in range(2):
                    g = g0 + u
                    pe.wait_ge(c1_zc, g + 1)
                    pe.wait_ge(c1_f, g0)
                    for b in range(2):
                        for m in range(MC):
                            mm = pe.matmul(bank[4 * u + 3][:, b * N:(b + 1) * N], zs[u][:, MC * b + m, :], adj_sb[:, m, :],
                                           start=(m == 0), stop=(m == MC - 1))
                    mm.then_inc(c1_g, 1)

            pe.wait_ge(c1_f, NG)
            pe.wait_ge(c1_zc, NG)
            with pe.Fori(0, LB) as it:
                for n, (p, t, s, b0, nb) in enumerate(lstm_steps):
                    nw = N // p
                    c = nb * nw
                    xin = F[:, bass.ds(it * (2 * NSUP * N) + b0 * N, nb * N)].rearrange(
                        "p (b n) -> p b n", n=N)[:, :, t:t + (nw - 1) * p + 1:p]
                    pe.wait_ge(l_h, it * NL + (n - 1 if n >= 2 else 0))
                    for k in range(GATES):
                        if k == 1 and t == 0:
                            continue
                        ps = bank[4 * s + k][:, 0:c]
                        mm = pe.matmul(ps.rearrange("p (b n) -> p b n", n=nw), wih_sb[:, p - 1, k * P:(k + 1) * P], xin,
                                       start=True, stop=(t == 0))
                        if t > 0:
                            mm = pe.matmul(ps, whh_sb[:, p - 1, k * P:(k + 1) * P], hst[s][:, 0:c],
                                           start=False, stop=True)
                    mm.then_inc(l_g, 1)

            with pairs(pe, 0, NG) as g0:
                for u in range(2):
                    g = g0 + u
                    pe.wait_ge(t_st, g + 1)
                    pe.wait_ge(t_x, g0)
                    for j in range(4):
                        tr = pe.transpose(bank[u][:, j * P:(j + 1) * P], xt[u][:, j * P:(j + 1) * P], ident[:, :])
                    tr.then_inc(t_tr, 1)
            pe.wait_ge(t_x, NG)
            with pairs(pe, 0, NG) as g0:
                for u in range(2):
                    g = g0 + u
                    pe.wait_ge(rd.xn, g + 1)
                    pe.wait_ge(rd.xt, g0)
                    transposes4(xn[u], bank[u], rd.tr)
                    pe.wait_ge(rd.xt, g + 1)
                    pe.wait_ge(rd.st, g0)
                    for j in range(4):
                        mm = pe.matmul(bank[6 + u][:, j * E:(j + 1) * E], xt[u][:, j * P:(j + 1) * P], rt_sb[:, :],
                                       start=True, stop=True)
                    mm.then_inc(rd.lg, 1)
            rank(rd)

            def d2_tr8(g, u, n_in):
                pe.wait_ge(d2_in[u], 16 * n_in)
                if not (isinstance(g, int) and g < 1):
                    pe.wait_ge(d2_xt, g)
                for j in range(8):
                    tr = pe.transpose(bank[j // 4][:, (j % 4) * P:(j % 4 + 1) * P], xs[u][:, j, :], ident[:, :])
                tr.then_inc(d2_tr, 1)

            def d2_pe(g, u, n_in, last):
                er = load_experts(8 * g, 8)
                pe.wait_ge(d2_xt, g + 1)
                early = isinstance(g, int) and g == 0
                for j in range(10):
                    if j < 8:
                        i = 8 * g + j
                        if not (early and j < 2):
                            pe.wait_ge(d2_m, i - 1)
                        for half in range(2):
                            mm = pe.matmul(bank[2 + 2 * (j % 2) + half][:, 0:UP], xt[u][:, j * P:(j + 1) * P],
                                           up_sb[:, bass.ds(er[j] * (2 * UP) + half * UP, UP)], start=True, stop=True)
                        mm.then_inc(d2_h, 1)
                    if 1 <= j < 9:
                        i = 8 * g + j - 1
                        pe.wait_ge(d2_m, i + 1)
                        if not (early and j == 1):
                            pe.wait_ge(d2_tc, i)
                        for k in range(KU):
                            kk = min(P, UP - k * P)
                            mm = pe.transpose(bank[6][0:kk, k * P:(k + 1) * P], hm[(j - 1) % 2][:, k * P:k * P + kk],
                                              ident[:, :])
                        mm.then_inc(d2_tt, 1)
                    if j >= 2:
                        i = 8 * g + j - 2
                        pe.wait_ge(d2_tc, i + 1)
                        pe.wait_ge(d2_yo, i)
                        for k in range(KU):
                            kk = min(P, UP - k * P)
                            mm = pe.matmul(bank[7][:, ((j - 2) % 4) * P:((j - 2) % 4 + 1) * P], ht[j % 2][0:kk, k, :],
                                           down_sb[0:kk, bass.ds(er[j - 2] * (KU * D) + k * D, D)],
                                           start=(k == 0), stop=(k == KU - 1), skip_group_check=True)
                        mm.then_inc(d2_y, 1)
                    if j == 8 and not last:
                        d2_tr8(g + 1, 1 - u, n_in)

            pe.wait_ge(rd.tiles, 1)
            pe.wait_ge(up_in, 16 * (1 + KU))
            d2_tr8(0, 0, 1)
            d2_pe(0, 0, 1, False)
            nb = (ND2 - 2) // 2
            with pe.Fori(0, nb) as h:
                d2_pe(2 * h + 1, 1, h + 2, False)
                d2_pe(2 * h + 2, 0, h + 2, False)
            for g in range(1 + 2 * nb, ND2):
                d2_pe(g, g % 2, (g + 1) // 2 + 1, g == ND2 - 1)

        @block.vector
        def _(dve):
            def L(ins):
                link(dve, ins)

            def stats(t, group_sem=None):
                return dve.bn_stats(ST[:, t, :], X[:, t, :])

            def ln_finish():
                me, ve, mo, vo = (ST[:, :, i] for i in (1, 2, 4, 5))
                s, d, v, t = (ln_t[:, i, :] for i in range(4))
                L(dve.tensor_tensor(s, me, mo, ALU.add))
                L(dve.tensor_tensor(d, me, mo, ALU.subtract))
                L(dve.tensor_tensor(v, ve, vo, ALU.add))
                L(dve.tensor_scalar(MEAN[:, :], s, 0.5, None, ALU.mult))
                L(dve.tensor_scalar(v, v, 1.0 / D, LN_EPS, ALU.mult, ALU.add))
                L(dve.tensor_tensor(d, d, d, ALU.mult))
                L(dve.scalar_tensor_tensor(v, d, 0.25, v, ALU.mult, ALU.add))
                L(dve.tensor_scalar(ln_i[:, 0, :], v.bitcast(I32), 1, None, ALU.arith_shift_right))
                L(dve.tensor_scalar(ln_i[:, 1, :], ln_i[:, 0, :], -1.0, float(RSQRT_MAGIC), ALU.mult, ALU.add))
                y = ln_i[:, 1, :].bitcast(F32)
                for i in range(3):
                    L(dve.tensor_tensor(t, y, y, ALU.mult))
                    L(dve.scalar_tensor_tensor(t, t, -0.5, v, ALU.mult, ALU.mult))
                    L(dve.scalar_tensor_tensor(RSTD[:, :], t, 1.5, y, ALU.add, ALU.mult))
                    y = RSTD[:, :]

            dve.wait_ge(const_ready, 1)

            def norm_steps(g, n, dst, done, step_sem, count):
                dve.tensor_tensor(dst, X[:, bass.ds(g * n, n), :], bcast(MEAN[:, bass.ds(g * n, n)], 2, D),
                                  ALU.subtract).then_inc(step_sem, 1)
                dve.wait_ge(step_sem, count + 1)
                dve.tensor_tensor(dst, dst, bcast(RSTD[:, bass.ds(g * n, n)], 2, D), ALU.mult).then_inc(done, 1)

            a_ns = sem("a_norm_step")
            a_st = sem("a_stats")
            for g in range(NX):
                dve.wait_ge(x_in[g], 16)
                for t in range(8 * g, 8 * g + 8):
                    dve.bn_stats(ST[:, t, :], X[:, t, :]).then_inc(a_st, 1)
            dve.wait_ge(a_st, NTILE)
            ln_finish()
            dve.wait_ge(w_in, W_ALL)
            dve.wait_ge(row_sums, 1)
            L(dve.tensor_scalar(bga_sb[:, :], bank[3][:, 0:N], g0b_sb[:, 0:1], None, ALU.mult))
            norm_steps(0, 8, xn[0][:, :, :], a_xn, a_ns, 0)
            a_s2 = sem("a_steps")

            def a_body(g, u, last):
                if not last:
                    dve.wait_ge(a_z, g)
                    dve.wait_ge(a_ax, g)
                    dve.wait_ge(a_q, g)
                    norm_steps(g + 1, 8, xn[1 - u][:, :, :], a_xn, a_ns, g + 1)
                dve.wait_ge(a_z, g + 1)
                if not (isinstance(g, int) and g < 2):
                    dve.wait_ge(a_th, g - 1)
                dve.tensor_tensor(zb[u].rearrange("p (b c) k -> p b c k", c=MC),
                                  bank[2][:, 0:24].rearrange("p (b c k) -> p b c k", c=MC, k=3),
                                  bcast(gb_sb[:, :, :], 1, 4), ALU.add).then_inc(a_zb, 1)
                dve.wait_ge(a_th, g + 1)
                dve.wait_ge(a_q, g - 1) if not (isinstance(g, int) and g < 1) else None
                dve.tensor_scalar(sg[u], th[u], 0.5, 0.5, ALU.mult, ALU.add).then_inc(a_s, 1)
                dve.wait_ge(a_s, g + 1)
                dve.tensor_tensor(us[u], sg[u][:, :, 0], sg[u][:, :, 1], ALU.add).then_inc(a_s2, 1)
                dve.wait_ge(a_ax, g + 1)
                dve.wait_ge(a_s2, 5 * g + 1)
                uv = us[u].rearrange("p (b c) -> p b c", c=MC)
                tv = t1.rearrange("p (b c) d -> p b c d", c=MC)
                for c in range(MC):
                    ins = dve.tensor_tensor(tv[:, :, c, :], bank[4 + 2 * u + c][:, :].rearrange("p (b d) -> p b d", d=D),
                                            bcast(uv[:, :, c], 2, D), ALU.mult)
                    ins.then_inc(a_s2, 1)
                dve.wait_ge(a_s2, 5 * g + 3)
                dve.wait_ge(a_q, g + 1)
                dve.tensor_tensor(t1, t1, q1[u], ALU.add).then_inc(a_t1, 1)
                dve.wait_ge(a_t1, g + 1)
                xv = X[:, bass.ds(8 * g, 8), :]
                dve.scalar_tensor_tensor(xv, t1, 0.0, xv, ALU.max, ALU.add).then_inc(a_s2, 1)
                dve.wait_ge(a_s2, 5 * g + 4)
                for j in range(8):
                    ins = dve.bn_stats(ST[:, bass.ds(8 * g + j, 1), :].rearrange("p a k -> p (a k)"),
                                       X[:, bass.ds(8 * g + j, 1), :].rearrange("p a k -> p (a k)"))
                ins.then_inc(a_s2, 1)
                dve.sem_inc(a_x, 1)

            a_body(0, 0, False)
            with pairs(dve, 1, NA - 1) as g:
                a_body(g, 1, False)
                a_body(g + 1, 0, False)
            a_body(NA - 1, 1, True)
            dve.wait_ge(a_s2, 5 * NA)

            def norm_rows(r, g, u, ns):
                norm_steps(g, 4, xn[u][:, 0:4, :], r.xn, ns, 2 * g)
                dve.wait_ge(r.xn, g + 1)
                dve.tensor_copy(XN[:, bass.ds(4 * g, 4), :], xn[u][:, 0:4, :]).then_inc(ns, 1)

            def choose(r, g, u, bias, cs):
                dve.wait_ge(r.lg, g + 1)
                src = bank[6 + u][:, 0:4 * E].rearrange("p (j e) -> p j e", e=E)
                if bias is not None:
                    dve.tensor_tensor(lg_st[u][:, :, :], src, bcast(bias, 1, 4), ALU.add).then_inc(r.st, 1)
                else:
                    dve.tensor_copy(lg_st[u][:, :, :], src).then_inc(r.st, 1)
                dve.wait_ge(r.st, g + 1)
                dve.tensor_copy(wait_c[u][:, 0:1], lg_st[u][:, 0, 0:1])
                for j in range(4):
                    dve.max(mx_st[u][:, j, :], lg_st[u][:, j, :]).then_inc(r.mx, 1)
                dve.wait_ge(r.mx, 4 * g + 4)
                dve.tensor_copy(wait_c[u][:, 1:2], mx_st[u][:, 0, 0:1])
                for j in range(4):
                    ins = dve.max_index(ix_st[u][:, j, :], mx_st[u][:, j, :], lg_st[u][:, j, :])
                    ins.then_inc(r.copied, 1)
                dve.tensor_copy(MX[:, bass.ds(4 * g, 4), :], mx_st[u][:, :, :]).then_inc(cs, 1)
                dve.wait_ge(r.copied, 4 * g + 4)
                dve.tensor_copy(IX[:, bass.ds(4 * g, 4), :], ix_st[u][:, :, :]).then_inc(r.ix, 1)

            def places(r, K, nslot, bank_r, bank_t):
                dve.wait_ge(r.ix, NG)
                for k in range(K):
                    L(dve.tensor_tensor(oh[k], bcast(iota_e[:, :], 2, NTILE), bcast(IX[:, :, k], 1, E), ALU.is_equal))
                if K == 2:
                    ins = dve.tensor_tensor(mask, oh[0], oh[1], ALU.add)
                else:
                    ins = dve.tensor_copy(mask, oh[0])
                ins.then_inc(r.mask, 1)
                L(dve.tensor_tensor(rw2.rearrange("p e t -> p (e t)").rearrange("p (t e) -> p t e", e=E), MX[:, :, :],
                                    bcast(MX[:, :, 0], 2, E), ALU.subtract))
                dve.sem_inc(r.flat, 1)
                dve.wait_ge(r.flat, 2)
                ex = rw1.rearrange("p e t -> p (e t)").rearrange("p (t e) -> p t e", e=E)
                den = ln_t[:, 0, :]
                L(dve.tensor_reduce(den, ex, AX_X, ALU.add))
                L(dve.reciprocal(ln_t[:, 1, :], den))
                if K == 1:
                    L(dve.tensor_copy(GT[:, 0, :], ln_t[:, 1, :]))
                else:
                    p1, p2 = ln_t[:, 1, :], ln_t[:, 2, :]
                    L(dve.tensor_tensor(p2, ex[:, :, 1], p1, ALU.mult))
                    L(dve.scalar_tensor_tensor(ln_t[:, 3, :], p1, TOPK_EPS, p2, ALU.add, ALU.add))
                    L(dve.reciprocal(den, ln_t[:, 3, :]))
                    L(dve.tensor_tensor(GT[:, 0, :], p1, den, ALU.mult))
                    L(dve.tensor_tensor(GT[:, 1, :], p2, den, ALU.mult))
                dve.wait_ge(r.ranks, 1)
                flat = lambda v: v.rearrange("p e t -> p (e t)")
                L(dve.tensor_copy(flat(tot), bank_t[:, :]))
                L(dve.tensor_tensor_scan(flat(cum), ones_row[:, :], flat(tot), 0.0, ALU.mult, ALU.add))
                L(dve.tensor_tensor(rw1, cum, tot, ALU.subtract))
                start, count, ntile, end, corr, tmp = (small[:, i, :] for i in range(6))
                L(dve.tensor_copy(start, rw1[:, :, 0]))
                L(dve.tensor_tensor(count, cum[:, :, NTILE - 1], start, ALU.subtract))
                L(dve.tensor_tensor(rw2, bcast(count, 2, NTILE), bcast(iota_t[:, :], 1, E), ALU.is_gt))
                L(dve.tensor_reduce(ntile, rw2, AX_X, ALU.add))
                L(dve.tensor_tensor_scan(end, ones_row[:, 0:E], ntile, 0.0, ALU.mult, ALU.add))
                L(dve.tensor_tensor(tmp, end, ntile, ALU.subtract))
                L(dve.scalar_tensor_tensor(corr, tmp, float(P), start, ALU.mult, ALU.subtract))
                L(dve.tensor_tensor(rw1, rw1, bcast(corr, 2, NTILE), ALU.add))
                L(dve.tensor_tensor(flat(rw1), bank_r[:, :], flat(rw1), ALU.add))
                for k in range(K):
                    L(dve.tensor_tensor(rw2, oh[k], rw1, ALU.mult))
                    L(dve.tensor_reduce(dest_f[:, k, :], rw2.rearrange("p e t -> p t e"), AX_X, ALU.add))
                L(dve.tensor_copy(dest_i[:, 0:K, :], dest_f[:, 0:K, :]))
                dve.sem_inc(r.places, 1)
                L(dve.tensor_tensor(tcmp[0:1, 0:nslot, :], bcast(iota_s[0:1, 0:nslot], 2, E),
                                    bcast(end[0:1, :], 1, nslot), ALU.is_ge))
                te = view(R2, NSLOT1 * E, NSLOT1)
                L(dve.tensor_reduce(te[0:1, 0:nslot], tcmp[0:1, 0:nslot, :], AX_X, ALU.add))
                L(dve.tensor_scalar(tile_e[:, 0:nslot], te[0:1, 0:nslot], float(E - 1), None, ALU.min))
                dve.sem_inc(r.tiles, 1)

            ln_finish()
            nsb, csb = sem("b1_norm_step"), sem("b1_choose_step")
            dve.wait_ge(zeroed, 16 * (NSLOT1 * D // ZW))
            norm_rows(rb, 0, 0, nsb)

            def b1_dve(g, u, last):
                if not last:
                    if not (isinstance(g, int) and g < 1):
                        dve.wait_ge(rb.tr, g)
                    dve.wait_ge(nsb, 2 * g + 2)
                    norm_rows(rb, g + 1, 1 - u, nsb)
                choose(rb, g, u, bg_sb[:, :], csb)

            b1_dve(0, 0, False)
            with pairs(dve, 1, NG - 1) as g:
                b1_dve(g, 1, False)
                b1_dve(g + 1, 0, False)
            b1_dve(NG - 1, 1, True)
            dve.wait_ge(csb, NG)
            dve.wait_ge(nsb, 2 * NG)
            places(rb, 1, NSLOT0, bank[0], bank[1])

            def b2_dve(g, u):
                _, er = nc.values_load_multi_w_load_instructions(
                    tile_e[0:1, bass.ds(4 * g, 4)], engines=[DVE_ENGINE], min_val=0, max_val=E - 1,
                    skip_runtime_bounds_check_because="clamped to the last expert where it is computed")
                dve.wait_ge(b2_y, g + 1)
                if isinstance(g, int):
                    if g >= 2:
                        dve.wait_ge(b2_out[u], 16 * (g // 2))
                for j in range(4):
                    ins = dve.tensor_tensor(yo[u][:, j, :], bank[6 + u][:, j * P:(j + 1) * P],
                                            bd_sb[:, bass.ds(er[j] * D, D)], ALU.add)
                ins.then_inc(b2_yo, 1)

            b2_dve(0, 0)
            b2_dve(1, 1)
            with dve.Fori(1, NB2 // 2) as h:
                for u in range(2):
                    dve.wait_ge(b2_out[u], 16 * h)
                    b2_dve(2 * h + u, u)
            for g in range(NX):
                dve.wait_ge(s_gath[0][g], 16 * 8)
                for t in range(8 * g, 8 * g + 8):
                    dve.scalar_tensor_tensor(X[:, t, :], XN[:, t, :], GT[:, 0, t:t + 1], X[:, t, :], ALU.mult,
                                             ALU.add).then_inc(b3_x, 1)
                for t in range(8 * g, 8 * g + 8):
                    dve.wait_ge(b3_x, t + 1)
                    dve.bn_stats(ST[:, t, :], X[:, t, :]).then_inc(b3_t, 1)

            dve.wait_ge(b3_t, NTILE)
            ln_finish()
            L(dve.tensor_tensor(lb_sb[:, :], bih_sb[:, :], bhh_sb[:, :], ALU.add))
            nsg = sem("g_norm_step")
            pe_rs = bga_sb
            with pairs(dve, 0, NG) as g0:
                for u in range(2):
                    g = g0 + u
                    dve.wait_ge(c1_ax, g0)
                    norm_steps(g, 4, xn[u][:, 0:4, :], c1_xn, nsg, g)
                for u in range(2):
                    g = g0 + u
                    dve.wait_ge(c1_h, g + 1)
                    dve.wait_ge(c1_hr, g0)
                    dve.tensor_tensor(hb[u].rearrange("p (b n) -> p b n", n=N),
                                      bank[4 * u + 1][:, :].rearrange("p (b n) -> p b n", n=N),
                                      bcast(bga_sb[:, :], 1, 2), ALU.add).then_inc(c1_hb, 1)
                for u in range(2):
                    g = g0 + u
                    dve.wait_ge(c1_z, g + 1)
                    dve.wait_ge(c1_g, g0)
                    dve.tensor_tensor(zs[u], bank[4 * u + 2][:, :].rearrange("p (a b) -> p a b", b=P),
                                      bcast(g1b_sb[:, :], 1, 4), ALU.add).then_inc(c1_zc, 1)

            per = [3 if st[1] == 0 else 4 for st in lstm_steps]
            tot_act = sum(per)
            with dve.Fori(0, LB) as it:
                seen = 0
                for n, (p, t, s, b0, nb) in enumerate(lstm_steps):
                    nw = N // p
                    c = nb * nw
                    gi, gf, gg, go = (gb[s][k][:, 0:c] for k in range(GATES))
                    cc, tc = cst[s][:, 0:c], tcs[s][:, 0:c]
                    dve.wait_ge(l_act, it * tot_act + seen + 2)
                    if t == 0:
                        dve.tensor_tensor(cc, gi, gg, ALU.mult).then_inc(l_c, 1)
                    else:
                        dve.tensor_tensor(gi, gi, gg, ALU.mult).then_inc(l_ig, 1)
                        dve.wait_ge(l_act, it * tot_act + seen + 3)
                        dve.tensor_tensor(gf, gf, cc, ALU.mult).then_inc(l_ig, 1)
                        nt = sum(2 for q in lstm_steps[:n] if q[1] > 0)
                        ntot = sum(2 for q in lstm_steps if q[1] > 0)
                        dve.wait_ge(l_ig, it * ntot + nt + 2)
                        dve.tensor_tensor(cc, gi, gf, ALU.add).then_inc(l_c, 1)
                    seen += per[n]
                    dve.wait_ge(l_act, it * tot_act + seen)
                    dve.wait_ge(l_tc, it * NL + n + 1)
                    if t == p - 1:
                        dst = F[:, bass.ds(it * (2 * NSUP * N) + b0 * N, nb * N)].rearrange(
                            "p (b n) -> p b n", n=N)[:, :, t:t + (nw - 1) * p + 1:p]
                        dve.tensor_tensor(dst, go.rearrange("p (b n) -> p b n", n=nw),
                                          tc.rearrange("p (b n) -> p b n", n=nw), ALU.mult).then_inc(l_h, 1)
                    else:
                        dve.tensor_tensor(hst[s][:, 0:c], go, tc, ALU.mult).then_inc(l_h, 1)

            with pairs(dve, 0, NG) as g0:
                for u in range(2):
                    g = g0 + u
                    dve.wait_ge(t_tr, g + 1)
                    xv = X[:, bass.ds(4 * g, 4), :]
                    dve.tensor_tensor(xv, bank[u][:, :].rearrange("p (a b) -> p a b", b=P), xv, ALU.add).then_inc(t_x, 1)
                    dve.wait_ge(t_x, g + 1)
                    for j in range(4):
                        ins = dve.bn_stats(ST[:, bass.ds(4 * g + j, 1), :].rearrange("p a k -> p (a k)"),
                                           X[:, bass.ds(4 * g + j, 1), :].rearrange("p a k -> p (a k)"))
                    ins.then_inc(t_ln, 1)
            dve.wait_ge(t_ln, NG)
            ln_finish()
            nsd, csd = sem("d1_norm_step"), sem("d1_choose_step")
            norm_rows(rd, 0, 0, nsd)

            def d1_dve(g, u, last):
                if not last:
                    if not (isinstance(g, int) and g < 1):
                        dve.wait_ge(rd.tr, g)
                    dve.wait_ge(nsd, 2 * g + 2)
                    norm_rows(rd, g + 1, 1 - u, nsd)
                choose(rd, g, u, None, csd)

            d1_dve(0, 0, False)
            with pairs(dve, 1, NG - 1) as g:
                d1_dve(g, 1, False)
                d1_dve(g + 1, 0, False)
            d1_dve(NG - 1, 1, True)
            dve.wait_ge(csd, NG)
            dve.wait_ge(nsd, 2 * NG)
            places(rd, 2, NSLOT1, bank[0], bank[1])

            def d2_dve(g, u, first):
                early = isinstance(g, int) and g == 0
                for j in range(10):
                    if j < 8:
                        i = 8 * g + j
                        dve.wait_ge(d2_silu, i + 1)
                        if not (early and j < 2):
                            dve.wait_ge(d2_tt, i - 1)
                        dve.tensor_tensor(hm[j % 2], sl[j % 2], bank[3 + 2 * (j % 2)][:, 0:UP], ALU.mult).then_inc(d2_m, 1)
                    if j >= 2:
                        i = 8 * g + j - 2
                        dve.wait_ge(d2_y, i + 1)
                        dve.tensor_copy(yo[u][:, j - 2, :], bank[7][:, ((j - 2) % 4) * P:((j - 2) % 4 + 1) * P]).then_inc(d2_yo, 1)

            d2_dve(0, 0, True)
            d2_dve(1, 1, False)
            nb = (ND2 - 2) // 2
            with dve.Fori(1, 1 + nb) as h:
                for u in range(2):
                    dve.wait_ge(d2_out[u], 16 * h)
                    d2_dve(2 * h + u, u, False)
            for g in range(2 + 2 * nb, ND2):
                dve.wait_ge(d2_out[g % 2], 16 * (g // 2))
                d2_dve(g, g % 2, False)
            for g in range(NX):
                dve.wait_ge(s_gath[1][g], 16 * 16)
                for k in range(2):
                    src = XN if k == 0 else Y1
                    for t in range(8 * g, 8 * g + 8):
                        if k == 1:
                            dve.wait_ge(d3_x, 16 * g + t % 8 + 1)
                        dve.scalar_tensor_tensor(X[:, t, :], src[:, t, :], GT[:, k, t:t + 1], X[:, t, :], ALU.mult,
                                                 ALU.add).then_inc(d3_x, 1)


def layouts(i):
    import numpy as np
    c = np.ascontiguousarray
    N = i["adj"].shape[0]
    E, H, C = i["L1_ffn_w1"].shape
    S, G4, Dh = i["L1_gnn_Wih"].shape
    x = c(i["x"].reshape(-1, i["x"].shape[-1]))
    return dict(
        x=x, adj_t=c(i["adj"].T),
        bias_io=c(np.concatenate([i["L0_gnn_bias_in"], i["L0_gnn_bias_out"]], axis=1)),
        gate_w=c(np.concatenate([i["L0_gnn_gate_w_in"], i["L0_gnn_gate_w_out"], i["L0_gnn_loop_gate"]], axis=1)),
        gate_b=c(np.concatenate([i["L0_gnn_gate_b_in"], i["L0_gnn_gate_b_out"],
                                 np.zeros((N, 1), i["L0_gnn_gate_b_in"].dtype)], axis=1)),
        w1=c(i["L0_ffn_W1"]), b1=c(i["L0_ffn_b1"].reshape(-1, 128).T), wg=c(i["L0_ffn_Wg"]), bg=c(i["L0_ffn_bg"]),
        wd=c(np.transpose(i["L0_ffn_Wd"], (1, 0, 2)).reshape(i["L0_ffn_Wd"].shape[1], -1)),
        bd=c(i["L0_ffn_bd"].reshape(-1)),
        g0_w=c(i["L1_gnn_Wg0"]), g0_b=c(i["L1_gnn_bg0"].reshape(-1, 1)), g1_w=c(i["L1_gnn_Wg1"]), g1_b=c(i["L1_gnn_bg1"]),
        wih_t=c(np.transpose(i["L1_gnn_Wih"], (0, 2, 1))), whh_t=c(np.transpose(i["L1_gnn_Whh"], (0, 2, 1))),
        bih=c(i["L1_gnn_bih"].reshape(-1, 128).T), bhh=c(i["L1_gnn_bhh"].reshape(-1, 128).T),
        router_t=c(i["L1_ffn_router_w"].T),
        up_t=c(np.concatenate([np.transpose(i["L1_ffn_w1"], (0, 2, 1)), np.transpose(i["L1_ffn_w3"], (0, 2, 1))], axis=2)),
        down_t=c(np.transpose(i["L1_ffn_w2"], (0, 2, 1))),
    )


def kernel(**inputs):
    import concourse.bacc as bacc
    import numpy as np
    from concourse.bass_utils import run_bass_kernel_spmd

    shape = inputs["x"].shape
    arrays = layouts({name: np.asarray(a) for name, a in inputs.items()})
    nc = bacc.Bacc("TRN2", target_bir_lowering=False, num_devices=1)
    aps = [nc.dram_tensor(name, a.shape, mybir.dt.from_np(a.dtype), kind="ExternalInput").ap()
           for name, a in arrays.items()]
    out = nc.dram_tensor("out", arrays["x"].shape, F32, kind="ExternalOutput").ap()
    build(nc, *aps, out)
    result = run_bass_kernel_spmd(nc, [arrays], core_ids=[0])
    return result.results[0]["out"].reshape(shape)
```

```python
from contextlib import ExitStack, contextmanager

import concourse.bass as bass
from concourse import mybir

P = 128
F32 = mybir.dt.float32
I32 = mybir.dt.int32
U32 = mybir.dt.uint32
ALU = mybir.AluOpType
ACT = mybir.ActivationFunctionType
AX_X = mybir.AxisListType.X
PE_ENGINE = mybir.EngineType.PE
DVE_ENGINE = mybir.EngineType.DVE
LN_EPS = 1e-5
RSQRT_MAGIC = 0x5F3759DF
TOPK_EPS = 1e-9
BANK = 512


def bcast(ap, axis, n):
    v = ap.unsqueeze(axis)
    shape = list(v.shape)
    shape[axis] = n
    return v.broadcast_to(shape)


class HiddenSems:

    def __init__(self, tr, xt, h, act, lg):
        self.tr, self.xt, self.h, self.act, self.lg = tr, xt, h, act, lg


class RouteSems(HiddenSems):

    def __init__(self, xn, tr, xt, h, act, lg, st, mx, ix, copied, flat, ranks, places, mask, tiles):
        super().__init__(tr, xt, h, act, lg)
        self.xn, self.st, self.mx, self.ix, self.copied = xn, st, mx, ix, copied
        self.flat, self.ranks, self.places, self.mask, self.tiles = flat, ranks, places, mask, tiles


@contextmanager
def pairs(eng, first, end):
    with eng.Fori(0, (end - first) // 2) as h:
        yield 2 * h + first


def build(nc, x, adj_t, bias_io, gate_w, gate_b, w1, b1, wg, bg, wd, bd, g0_w, g0_b, g1_w, g1_b, wih_t, whh_t, bih, bhh,
          router_t, up_t, down_t, out):
    TOK, D = x.shape
    NTILE = TOK // P
    N = adj_t.shape[0]
    MC = N // P
    E = router_t.shape[1]
    HID = w1.shape[1]
    KH = HID // P
    UP = up_t.shape[2] // 2
    KU = -(-UP // P)
    MAX_SKIP = wih_t.shape[0]
    GATES = 4
    assert D == P and E == 8 and MC == 2 and MAX_SKIP == 4

    HALVES = 2
    NH = NTILE // HALVES
    NSLOT0 = -(-(NH + E - 1) // 4) * 4
    NSLOT1 = -(-(2 * NH + E - 1) // 8) * 8

    with ExitStack() as ctx:
        def sb(name, shape, dt=F32):
            return ctx.enter_context(nc.sbuf_tensor("sb_" + name, shape, dt))

        def sem(name):
            return ctx.enter_context(nc.semaphore(name))

        sorted_in = [nc.dram_tensor(f"sorted_in{h}", [NSLOT1 * P, D], F32, kind="Internal").ap() for h in range(HALVES)]
        sorted_out = [nc.dram_tensor(f"sorted_out{h}", [NSLOT1 * P, D], F32, kind="Internal").ap() for h in range(HALVES)]

        X = sb("X", [P, NTILE, D])
        R1 = sb("R1", [P, NTILE * D])
        R2 = sb("R2", [P, NTILE * D])
        R3 = sb("R3", [P, 6 * BANK])
        XN = R1[:, :].rearrange("p (t d) -> p t d", d=D)
        xn = [sb(f"xn{u}", [P, 8, D]) for u in range(2)]
        xs = [sb(f"xs{u}", [P, 8, D]) for u in range(2)]
        xt = [sb(f"xt{u}", [P, 8 * P]) for u in range(2)]
        ident = sb("ident", [P, P])
        before = sb("before", [P, P])
        ones = sb("ones", [P, P])
        ones_row = sb("ones_row", [P, BANK])
        iota_e = sb("iota_e", [P, E])
        iota_t = sb("iota_t", [P, NH])
        iota_s = sb("iota_s", [1, NSLOT1])
        adj_sb = sb("adj_sb", [P, MC, N])
        bias_sb = sb("bias_sb", [P, MC, 2, D])
        gw_sb = sb("gw_sb", [P, 3])
        gb_sb = sb("gb_sb", [P, MC, 3])
        w1_sb = sb("w1_sb", [P, HID])
        b1_sb = sb("b1_sb", [P, KH])
        wg_sb = sb("wg_sb", [P, KH, E])
        bg_sb = sb("bg_sb", [P, E])
        BIG = sb("BIG", [P, E * (2 * UP + KU * D)])
        wd_sb = BIG[:, 0:KH * E * D].rearrange("p (k n) -> p k n", k=KH)
        bd_sb = BIG[:, KH * E * D:(KH + 1) * E * D]
        up_sb = BIG[:, 0:E * 2 * UP]
        down_sb = BIG[:, E * 2 * UP:E * (2 * UP + KU * D)]
        g0_sb = sb("g0_sb", [P, D])
        g1_sb = sb("g1_sb", [P, D])
        g0b_sb = sb("g0b_sb", [P, 1])
        g1b_sb = sb("g1b_sb", [P, D])
        bga_sb = sb("bga_sb", [P, N])
        wih_sb = sb("wih_sb", [P, MAX_SKIP, GATES * P])
        whh_sb = sb("whh_sb", [P, MAX_SKIP, GATES * P])
        bih_sb = sb("bih_sb", [P, MAX_SKIP * GATES])
        bhh_sb = sb("bhh_sb", [P, MAX_SKIP * GATES])
        lb_sb = sb("lb_sb", [P, MAX_SKIP * GATES])
        rt_sb = sb("rt_sb", [P, E])
        ST = sb("ST", [P, NTILE, 6])
        MEAN = sb("MEAN", [P, NTILE])
        RSTD = sb("RSTD", [P, NTILE])
        ln_t = sb("ln_t", [P, 4, NTILE])
        ln_i = sb("ln_i", [P, 2, NTILE], I32)
        MX = sb("MX", [P, NTILE, E])
        IX = sb("IX", [P, NTILE, E])
        lg_st = [sb(f"lg_st{u}", [P, 4, E]) for u in range(2)]
        mx_st = [sb(f"mx_st{u}", [P, 4, E]) for u in range(2)]
        ix_st = [sb(f"ix_st{u}", [P, 4, E], U32) for u in range(2)]
        wait_c = [sb(f"wait_c{u}", [P, 2]) for u in range(2)]
        GT = sb("GT", [P, 2, NTILE])
        dest_i = sb("dest_i", [P, 2, NTILE], I32)
        tile_e = sb("tile_e", [1, HALVES, NSLOT1], I32)

        bank = [ctx.enter_context(nc.psum_tensor(f"bank{i}", [P, BANK], F32)) for i in range(8)]

        def view(region, at, *shape):
            n = 1
            for s in shape:
                n *= s
            names = "abcd"[:len(shape)]
            v = region[:, at:at + n]
            if len(shape) == 1:
                return v
            return v.rearrange(f"p ({' '.join(names)}) -> p {' '.join(names)}", **dict(zip(names, shape)))

        block = ctx.enter_context(nc.Block())

        NX = 8
        x_in = [sem(f"x_in{i}") for i in range(NX)]
        wa_in, w_in = sem("wa_in"), sem("w_in")
        up_in = sem("up_in")
        const_ready = sem("const_ready")
        zero_ready = sem("zero_ready")
        zeroed = sem("zeroed")

        loads_w = [
            (adj_sb[:, :, :], adj_t.rearrange("(c p) n -> p c n", p=P)),
            (bias_sb[:, :, :, :].rearrange("p c i d -> p c (i d)"), bias_io.rearrange("(c p) n -> p c n", p=P)),
            (gw_sb[:, :], gate_w),
            (gb_sb[:, :, :], gate_b.rearrange("(c p) n -> p c n", p=P)),
            (w1_sb[:, :], w1),
            (b1_sb[:, :], b1),
            (wg_sb[:, :, :], wg.rearrange("(k p) e -> p k e", p=P)),
            (bg_sb[:, :], bg.partition_broadcast(P)),
            (wd_sb, wd.rearrange("(k p) n -> p k n", p=P)),
            (bd_sb, bd.partition_broadcast(P)),
            (g0_sb[:, :], g0_w), (g1_sb[:, :], g1_w), (g0b_sb[:, :], g0_b),
            (g1b_sb[:, :], g1_b.partition_broadcast(P)),
            (wih_sb[:, :, :], wih_t.rearrange("s p n -> p s n")),
            (whh_sb[:, :, :], whh_t.rearrange("s p n -> p s n")),
            (bih_sb[:, :], bih), (bhh_sb[:, :], bhh), (rt_sb[:, :], router_t),
        ]
        loads_a, loads_w = loads_w[:4], loads_w[4:]
        WA_ALL, W_ALL = 16 * len(loads_a), 16 * len(loads_w)

        NA = NTILE // 8
        a_xn, a_tr, a_xt, a_z, a_ax, a_zb, a_th, a_s, a_us, a_c2, a_c3, a_q, a_mul, a_t1, a_x, a_ns, a_st, a_st2 = (
            sem("a_" + n) for n in ("normed transposed copied z mixed zbias tanh gate gate_sum gated_out gated_loop bias "
                                    "scaled summed done norm_step stats stats2").split())
        zb = [view(R2, u * 24, 8, 3) for u in range(2)]
        th = [view(R2, 64 + u * 24, 8, 3) for u in range(2)]
        sg = [view(R2, 128 + u * 24, 8, 3) for u in range(2)]
        us = [view(R2, 192 + u * 8, 8) for u in range(2)]
        q1, q2, q3 = ([view(R2, 512 + (2 * i + u) * 8 * D, 8, D) for u in range(2)] for i in range(3))
        t1 = view(R3, 0, 8, D)
        ZW = 9 * D
        zero = view(R2, 512 + 6 * 8 * D, ZW)

        row_sums = sem("row_sums")
        dve_step = sem("dve_step")
        pool_step = sem("pool_step")
        n_dve = [0]
        n_pool = [0]

        def link(eng, ins):
            ins.then_inc(dve_step, 1)
            n_dve[0] += 1
            eng.wait_ge(dve_step, n_dve[0])

        def route_sems(tag):
            return RouteSems(*(sem(f"{tag}_{n}") for n in (
                "normed", "transposed", "copied", "hidden", "gelu", "logits", "staged", "sorted", "chosen", "indexed",
                "softmax", "ranks", "places", "mask", "tiles")))

        rb, rd = route_sems("b1"), route_sems("d1")
        NG = NTILE // 4
        Ht = [view(R2, u * KH * BANK, KH, BANK) for u in range(2)]
        RW = 2 * KH * BANK
        EH = E * NH
        oh = [view(R2, RW + k * EH, E, NH) for k in range(2)]
        mask = view(R2, RW + 2 * EH, E, NH)
        tot = view(R2, RW + 3 * EH, E, NH)
        cum = view(R2, RW + 4 * EH, E, NH)
        rw1 = view(R2, RW + 5 * EH, E, NH)
        rw2 = view(R2, RW + 6 * EH, E, NH)
        small = view(R2, RW + 7 * EH, 16, E)
        dest_f = view(R2, RW + 7 * EH + 128, 2, NH)
        tcmp = view(R2, RW + 8 * EH, NSLOT1, E)
        te = view(R2, RW + 8 * EH + NSLOT1 * E, NSLOT1)

        s_scat = {l: [sem(f"{'bd'[l]}_scattered{h}") for h in range(HALVES)] for l in range(2)}
        s_gath = {0: [sem(f"b_gathered{i}") for i in range(NX)], 1: [sem(f"d_gathered{i}") for i in range(NX)]}
        b2_in = [sem("b2_in0"), sem("b2_in1")]
        b2_tr, b2_xt, b2_h, b2_act, b2_y, b2_yo = (sem("b2_" + n) for n in "tr xt h act y yo".split())
        r2 = HiddenSems(b2_tr, b2_xt, b2_h, b2_act, b2_y)
        nsb, csb, nsd, csd, nsg = (sem(n) for n in (
            "b1_norm_step", "b1_choose_step", "d1_norm_step", "d1_choose_step", "g_norm_step"))
        b2_out = [sem("b2_out0"), sem("b2_out1")]
        NB2 = HALVES * NSLOT0 // 4
        yb = [view(R3, u * BANK, 4, D) for u in range(2)]
        b3_x, b3_t = sem("b3_x"), sem("b3_t")

        c1_xn, c1_ax, c1_axc, c1_h, c1_hb, c1_hr, c1_z, c1_zc, c1_g, c1_f = (
            sem("g_" + n) for n in "normed mixed mixed_sb h0 h0_biased h0_relu z1 z1_sb h1 done".split())
        F = R2
        WK = NH * P
        axt = [view(R2, WK + u * BANK, BANK) for u in range(2)]
        hb = [view(R2, WK + (2 + u) * BANK, BANK) for u in range(2)]
        h1 = [view(R2, WK + (4 + u) * BANK, BANK) for u in range(2)]
        zs = [view(R2, WK + (6 + u) * BANK, 4, P) for u in range(2)]

        l_x, l_g, l_act, l_ig, l_fc, l_c, l_tc, l_h = (sem("l_" + n) for n in "x g act ig fc c tc h".split())
        gb = [[view(R2, WK + (u * GATES + k) * BANK, BANK) for k in range(GATES)] for u in range(2)]
        cst = [view(R3, u * BANK, BANK) for u in range(2)]
        tcs = [view(R3, (2 + u) * BANK, BANK) for u in range(2)]
        hst = [view(R3, (4 + u) * BANK, BANK) for u in range(2)]

        t_st, t_tr, t_x, t_ln = (sem("t_" + n) for n in "st tr x ln".split())

        ND2 = HALVES * NSLOT1 // 8
        d2_in = [sem("d2_in0"), sem("d2_in1")]
        d2_tr, d2_xt, d2_h, d2_silu, d2_m, d2_tt, d2_tc, d2_y, d2_yo = (
            sem("d2_" + n) for n in "tr xt h silu m tt tc y yo".split())
        d2_out = [sem("d2_out0"), sem("d2_out1")]
        sl = [view(R3, u * KU * P, UP) for u in range(2)]
        hm = [view(R3, (2 + u) * KU * P, UP) for u in range(2)]
        ht = [view(R3, (4 + u) * KU * P, KU, P) for u in range(2)]
        yd = [view(R2, u * 8 * D, 8, D) for u in range(2)]
        Y1 = [view(R2, WK * (1 - h), NH, D) for h in range(HALVES)]
        d3_x, d3_t = sem("d3_x"), sem("d3_t")
        out_sem = sem("out_sem")

        lstm_steps = []
        NSUP = 4
        for half in range(2):
            for s in range(2):
                lstm_steps.append((1, 0, s, NSUP * s + 2 * half, 2))
        for p in range(2, MAX_SKIP + 1):
            for t in range(p):
                for s in range(2):
                    lstm_steps.append((p, t, s, NSUP * s, NSUP))
        NL = len(lstm_steps)
        acts_before = [0]
        for step in lstm_steps:
            acts_before.append(acts_before[-1] + (GATES if step[1] > 0 else GATES - 1))
        acts_body = acts_before[-1]
        LB = TOK // (2 * NSUP * N)
        LBH = LB // HALVES

        def sweep(eng, first, end, body):
            body(first, first // 2, first % 2, True, False)
            mid = first + 1
            n = (end - 1 - mid) // 2
            with eng.Fori(0, n) as h:
                for j in range(2):
                    body(2 * h + (mid + j), h + (mid + j) // 2, (mid + j) % 2, False, False)
            for g in range(mid + 2 * n, end):
                body(g, g // 2, g % 2, False, g == end - 1)

        def run_pairs(eng, first, end, body):
            at = first
            if at % 2:
                body(at, at // 2, 1)
                at += 1
            n = (end - at) // 2
            with eng.Fori(0, n) as h:
                for j in range(2):
                    body(2 * h + (at + j), h + at // 2, j)
            if (end - at) % 2:
                body(end - 1, (end - 1) // 2, 0)

        def known_below(g, n):
            return isinstance(g, int) and g < n

        NGH = NG // HALVES
        NXH = NX // HALVES
        B2H = NB2 // HALVES
        D2H = ND2 // HALVES
        ZEROS = 16 * HALVES * (NSLOT1 * D // ZW)

        @block.sync
        def _(sp):
            for g in range(NX):
                sp.dma_start(X[:, 8 * g:8 * g + 8, :],
                             x.rearrange("(t p) d -> p t d", p=P)[:, 8 * g:8 * g + 8, :]).then_inc(x_in[g], 16)
                if g == 0:
                    for dst, src in loads_a:
                        sp.dma_start(dst, src).then_inc(wa_in, 16)
            for dst, src in loads_w:
                sp.dma_start(dst, src).then_inc(w_in, 16)
            sp.wait_ge(zero_ready, 1)
            for rows in sorted_in:
                zv = rows.rearrange("(p n) d -> p (n d)", p=P)
                for i in range(NSLOT1 * D // ZW):
                    sp.dma_start(zv[:, i * ZW:(i + 1) * ZW], zero).then_inc(zeroed, 16)

            def rows_of(rows, g, n):
                return rows[bass.ds(g * (n * P), n * P), :].rearrange("(t p) d -> p t d", p=P)

            def b2_store(g, k, u):
                half = b2_half[1]
                sp.wait_ge(b2_yo, g + 1)
                sp.dma_start(rows_of(sorted_out[half], g - half * B2H, 4), yb[u]).then_inc(b2_out[u], 16)

            def b2_load(g, u):
                half = b2_half[0]
                if not known_below(g, 2):
                    sp.wait_ge(b2_tr, g - 1)
                sp.dma_start(xs[u][:, 0:4, :], rows_of(sorted_in[half], g - half * B2H, 4)).then_inc(b2_in[u], 16)

            b2_half = [0, 0]

            def b2_both(g, k, u):
                b2_load(g, u)
                b2_store(g - 2, k - 1, u)

            sp.wait_ge(s_scat[0][0], 16 * NH)
            b2_load(0, 0)
            b2_load(1, 1)
            for half in range(HALVES):
                first = half * B2H
                if half > 0:
                    sp.wait_ge(s_scat[0][half], 16 * NH)
                    b2_half[0] = half
                    for g in range(first, first + 2):
                        b2_both(g, g // 2, g % 2)
                b2_half[1] = half
                run_pairs(sp, first + 2, first + B2H, b2_both)
            for g in range(NB2 - 2, NB2):
                b2_store(g, g // 2, g % 2)

            sp.wait_ge(b2_y, NB2)
            sp.wait_ge(b2_yo, NB2)
            sp.dma_start(up_sb, up_t.rearrange("e p n -> p e n")).then_inc(up_in, 16)
            dv = down_sb.rearrange("p (e k d) -> p e k d", k=KU, d=D)
            for k in range(KU):
                kk = min(P, UP - k * P)
                sp.dma_start(dv[0:kk, :, k, :],
                             down_t[:, k * P:k * P + kk, :].rearrange("e p d -> p e d")).then_inc(up_in, 16)

            d2_half = [0, 0]

            def d2_load(g, u):
                if not known_below(g, 2):
                    sp.wait_ge(d2_tr, g - 1)
                sp.dma_start(xs[u][:, :, :], rows_of(sorted_in[d2_half[0]], g - d2_half[0] * D2H, 8)).then_inc(d2_in[u], 16)

            def d2_store(g, u):
                half = d2_half[1]
                sp.wait_ge(d2_yo, 8 * g + 8)
                sp.dma_start(rows_of(sorted_out[half], g - half * D2H, 8), yd[u]).then_inc(d2_out[u], 16)

            def d2_both(g, k, u):
                d2_load(g, u)
                d2_store(g - 2, u)

            sp.wait_ge(s_scat[1][0], 32 * NH)
            d2_load(0, 0)
            d2_load(1, 1)
            for half in range(HALVES):
                first = half * D2H
                if half > 0:
                    sp.wait_ge(s_scat[1][half], 32 * NH)
                    d2_half[0] = half
                    for g in range(first, first + 2):
                        d2_both(g, g // 2, g % 2)
                d2_half[1] = half
                run_pairs(sp, first + 2, first + D2H, d2_both)
            for g in range(ND2 - 2, ND2):
                d2_store(g, g % 2)
            for g in range(NX):
                sp.wait_ge(d3_x, 16 * (g + 1))
                sp.dma_start(out.rearrange("(t p) d -> p t d", p=P)[:, 8 * g:8 * g + 8, :],
                             X[:, 8 * g:8 * g + 8, :]).then_inc(out_sem, 16)
            sp.wait_ge(out_sem, 16 * NX)

        @block.gpsimd
        def _(pool):
            def step(ins):
                ins.then_inc(pool_step, 1)
                n_pool[0] += 1
                pool.wait_ge(pool_step, n_pool[0])

            pool.memset(zero, 0.0).then_inc(zero_ready, 1)
            step(pool.memset(ident[:, :], 0.0))
            step(pool.affine_select(out=ident[:, :], in_=ident[:, :], compare_op=ALU.not_equal, fill=1.0, base=0,
                                    pattern=[[-1, P]], channel_multiplier=1))
            pool.memset(ones_row[:, :], 1.0)
            step(pool.memset(ones[:, :], 1.0))
            step(pool.affine_select(out=before[:, :], in_=ones[:, :], compare_op=ALU.is_gt, fill=0.0, base=0,
                                    pattern=[[1, P]], channel_multiplier=-1))
            pool.iota(iota_e[:, :], [[1, E]], base=0, channel_multiplier=0, allow_small_or_imprecise_dtypes=True)
            pool.iota(iota_t[:, :], [[P, NH]], base=0, channel_multiplier=0, allow_small_or_imprecise_dtypes=True)
            pool.iota(iota_s[:, :], [[1, NSLOT1]], base=0, channel_multiplier=0,
                      allow_small_or_imprecise_dtypes=True).then_inc(const_ready, 1)

            pool.wait_ge(wa_in, WA_ALL)
            p0 = n_pool[0]

            def a_pool(g, k, u):
                pool.wait_ge(a_s, g + 1)
                if not known_below(g, 2):
                    pool.wait_ge(a_t1, g - 1)
                pool.tensor_tensor(
                    q1[u].rearrange("p (b c) d -> p b c d", c=MC), bcast(bias_sb[:, :, 0, :], 1, 8 // MC),
                    bcast(sg[u][:, :, 0].rearrange("p (b c) -> p b c", c=MC), 3, D), ALU.mult).then_inc(pool_step, 1)
                pool.wait_ge(pool_step, p0 + 2 * g + 1)
                pool.wait_ge(a_c2, g + 1)
                pool.tensor_tensor(q1[u], q1[u], q2[u], ALU.add).then_inc(pool_step, 1)
                pool.wait_ge(pool_step, p0 + 2 * g + 2)
                pool.wait_ge(a_c3, g + 1)
                pool.tensor_tensor(q1[u], q1[u], q3[u], ALU.add).then_inc(a_q, 1)

            a_pool(0, 0, 0)
            a_pool(1, 0, 1)
            run_pairs(pool, 2, NA, a_pool)

            def scatter(layer, half, r, K):
                pool.wait_ge(r.places, half + 1)
                if layer == 0 and half == 0:
                    pool.wait_ge(zeroed, ZEROS)
                for t in range(half * NH, (half + 1) * NH):
                    for k in range(K):
                        pool.indirect_dma_start(
                            out=sorted_in[half], out_offset=bass.IndirectOffsetOnAxis(ap=dest_i[:, k, t:t + 1], axis=0),
                            in_=XN[:, t, :], in_offset=None).then_inc(s_scat[layer][half], 16)

            def gather(layer, half, outs, groups, nslot, K):
                done = (half + 1) * groups
                pool.wait_ge(outs[0], 16 * (done - done // 2))
                pool.wait_ge(outs[1], 16 * (done // 2))
                pool.wait_ge(s_scat[layer][half], 16 * K * NH)
                for t in range(half * NH, (half + 1) * NH):
                    for k in range(K):
                        dst = XN[:, t, :] if k == 0 else Y1[half][:, t - half * NH, :]
                        pool.indirect_dma_start(
                            out=dst, out_offset=None, in_=sorted_out[half][0:nslot * P, :],
                            in_offset=bass.IndirectOffsetOnAxis(ap=dest_i[:, k, t:t + 1], axis=0)).then_inc(
                                s_gath[layer][t // 8], 16)

            for half in range(HALVES):
                scatter(0, half, rb, 1)
            for half in range(HALVES):
                gather(0, half, b2_out, B2H, NSLOT0, 1)
            for half in range(HALVES):
                scatter(1, half, rd, 2)
            for half in range(HALVES):
                gather(1, half, d2_out, D2H, NSLOT1, 2)

        @block.scalar
        def _(act):
            act.wait_ge(wa_in, WA_ALL)

            def a_act(g, k, u):
                act.wait_ge(a_tr, g + 1)
                if not known_below(g, 2):
                    act.wait_ge(a_z, g - 1)
                for h in range(2):
                    ins = act.activation(xt[u][:, h * BANK:(h + 1) * BANK], bank[h][:, :], ACT.Copy)
                ins.then_inc(a_xt, 1)
                act.wait_ge(a_zb, g + 1)
                act.activation(th[u], zb[u], ACT.Tanh, scale=0.5).then_inc(a_th, 1)
                act.wait_ge(a_s, g + 1)
                if not known_below(g, 2):
                    act.wait_ge(a_q, g - 1)
                for j in range(8):
                    ins = act.activation(q2[u][:, j, :], bias_sb[:, j % MC, 1, :], ACT.Copy, scale=sg[u][:, j, 1:2])
                ins.then_inc(a_c2, 1)
                for j in range(8):
                    ins = act.activation(q3[u][:, j, :], xn[u][:, j, :], ACT.Copy, scale=sg[u][:, j, 2:3])
                ins.then_inc(a_c3, 1)

            a_act(0, 0, 0)
            a_act(1, 0, 1)
            run_pairs(act, 2, NA, a_act)
            act.wait_ge(w_in, W_ALL)

            def hidden_body(r):
                def body(g, k, u, first, last):
                    for c in range(KH):
                        act.wait_ge(r.h, KH * g + c + 1)
                        if c == 0 and not known_below(g, 2):
                            act.wait_ge(r.lg, g - 1)
                        act.activation(Ht[u][:, c, :], bank[2 + c][:, :], ACT.Gelu, bias=b1_sb[:, c:c + 1]).then_inc(r.act, 1)
                    if not last:
                        copy_xt(r, g + 1, 1 - u)
                return body

            def copy_xt(r, g, u):
                act.wait_ge(r.tr, g + 1)
                act.activation(xt[u][:, 0:BANK], bank[u][:, :], ACT.Copy).then_inc(r.xt, 1)

            def softmax_exp(r, half):
                act.wait_ge(r.flat, 2 * half + 1)
                act.activation(rw1, rw2, ACT.Exp).then_inc(r.flat, 1)

            for half in range(HALVES):
                copy_xt(rb, half * NGH, 0)
                sweep(act, half * NGH, (half + 1) * NGH, hidden_body(rb))
                softmax_exp(rb, half)
            copy_xt(r2, 0, 0)
            sweep(act, 0, NB2, hidden_body(r2))

            for half in range(HALVES):
                act.wait_ge(b3_x, (half + 1) * NH)

                def g_act(h0):
                    g0 = 2 * h0 + half * NGH
                    for u in range(2):
                        act.wait_ge(c1_ax, g0 + u + 1)
                        act.activation(axt[u], bank[4 * u][:, :], ACT.Copy).then_inc(c1_axc, 1)
                    for u in range(2):
                        act.wait_ge(c1_hb, g0 + u + 1)
                        act.activation(h1[u], hb[u], ACT.Relu).then_inc(c1_hr, 1)
                    for u in range(2):
                        act.wait_ge(c1_g, g0 + u + 1)
                        act.activation(F[:, bass.ds((2 * h0 + u) * BANK, BANK)], bank[4 * u + 3][:, :], ACT.Relu).then_inc(c1_f, 1)

                with act.Fori(0, NGH // 2) as h0:
                    g_act(h0)

                funcs = (ACT.Sigmoid, ACT.Sigmoid, ACT.Tanh, ACT.Sigmoid)
                with act.Fori(0, LBH) as itl:
                    it = itl + half * LBH
                    for n, (p, t, s, b0, nb) in enumerate(lstm_steps):
                        c = nb * (N // p)
                        act.wait_ge(l_g, it * NL + n + 1)
                        act.wait_ge(l_h, it * NL + (n - 1 if n >= 2 else 0))
                        for k in (0, 2, 1, 3):
                            if k == 1 and t == 0:
                                continue
                            act.activation(gb[s][k][:, 0:c], bank[4 * s + k][:, 0:c], funcs[k],
                                           bias=lb_sb[:, (p - 1) * GATES + k:(p - 1) * GATES + k + 1]).then_inc(l_act, 1)
                        act.wait_ge(l_c, it * NL + n + 1)
                        act.activation(tcs[s][:, 0:c], cst[s][:, 0:c], ACT.Tanh).then_inc(l_tc, 1)

                act.wait_ge(l_h, (half + 1) * LBH * NL)
                with act.Fori(0, NGH // 2) as h0:
                    g0 = 2 * h0 + half * NGH
                    for u in range(2):
                        act.wait_ge(t_tr, g0)
                        act.activation(xt[u][:, 0:BANK], F[:, bass.ds((2 * h0 + u) * BANK, BANK)], ACT.Copy).then_inc(t_st, 1)

                act.wait_ge(t_x, (half + 1) * NGH)
                with act.Fori(0, NGH // 2) as h0:
                    g0 = 2 * h0 + half * NGH
                    for u in range(2):
                        act.wait_ge(rd.tr, g0 + u + 1)
                        act.wait_ge(rd.lg, g0)
                        act.activation(xt[u][:, 0:BANK], bank[u][:, :], ACT.Copy).then_inc(rd.xt, 1)
                softmax_exp(rd, half)

            def d2_rows(g, u):
                act.wait_ge(d2_tr, g + 1)
                if not known_below(g, 1):
                    act.wait_ge(d2_h, 8 * g)
                for h in range(2):
                    ins = act.activation(xt[u][:, h * BANK:(h + 1) * BANK], bank[h][:, :], ACT.Copy)
                ins.then_inc(d2_xt, 1)

            def d2_act(g, k, u, first, last):
                for j in range(9):
                    if j < 8:
                        i = 8 * g + j
                        act.wait_ge(d2_h, i + 1)
                        if not (known_below(g, 1) and j < 2):
                            act.wait_ge(d2_m, i - 1)
                        act.activation(sl[j % 2], bank[2 + 2 * (j % 2)][:, 0:UP], ACT.Silu).then_inc(d2_silu, 1)
                    if j >= 1:
                        i = 8 * g + j - 1
                        act.wait_ge(d2_tt, i + 1)
                        if not (known_below(g, 1) and j < 3):
                            act.wait_ge(d2_y, i - 1)
                        kf = UP // P
                        dst = ht[(j - 1) % 2]
                        act.activation(dst[:, 0:kf, :], bank[6][:, 0:kf * P].rearrange("p (k n) -> p k n", n=P), ACT.Copy)
                        act.activation(dst[0:UP - kf * P, kf, :], bank[6][0:UP - kf * P, kf * P:(kf + 1) * P],
                                       ACT.Copy).then_inc(d2_tc, 1)
                if not last:
                    d2_rows(g + 1, 1 - u)

            act.wait_ge(rd.places, HALVES)
            d2_rows(0, 0)
            sweep(act, 0, ND2, d2_act)

        @block.tensor
        def _(pe):
            tile_list = tile_e[:, :, :].rearrange("a h s -> a (h s)")

            def load_experts(first, n):
                _, r = nc.values_load_multi_w_load_instructions(
                    tile_list[0:1, bass.ds(first, n)], engines=[PE_ENGINE], min_val=0, max_val=E - 1,
                    skip_runtime_bounds_check_because="clamped to the last expert where it is computed")
                return r

            pe.wait_ge(const_ready, 1)
            pe.wait_ge(wa_in, WA_ALL)
            for m in range(MC):
                mm = pe.matmul(bank[3][:, 0:N], ones[:, :], adj_sb[:, m, :], start=(m == 0), stop=(m == MC - 1))
            mm.then_inc(row_sums, 1)

            def a_pe(g, k, u):
                pe.wait_ge(a_xn, g + 1)
                if not known_below(g, 1):
                    pe.wait_ge(a_xt, g)
                for j in range(8):
                    tr = pe.transpose(bank[j // 4][:, (j % 4) * P:(j % 4 + 1) * P], xn[u][:, j, :], ident[:, :])
                tr.then_inc(a_tr, 1)
                xv = xn[u][:, :, :].rearrange("p (b c) d -> p b c d", c=MC)
                if not known_below(g, 2):
                    pe.wait_ge(a_mul, g - 1)
                for nch in range(MC):
                    for m in range(MC):
                        mm = pe.matmul(bank[4 + 2 * u + nch][:, :].rearrange("p (b d) -> p b d", d=D),
                                       adj_sb[:, m, nch * P:(nch + 1) * P], xv[:, :, m, :],
                                       start=(m == 0), stop=(m == MC - 1))
                mm.then_inc(a_ax, 1)
                pe.wait_ge(a_xt, g + 1)
                if not known_below(g, 1):
                    pe.wait_ge(a_zb, g)
                for j in range(8):
                    mm = pe.matmul(bank[2][:, 3 * j:3 * j + 3], xt[u][:, j * P:(j + 1) * P], gw_sb[:, :],
                                   start=True, stop=True)
                mm.then_inc(a_z, 1)

            a_pe(0, 0, 0)
            a_pe(1, 0, 1)
            run_pairs(pe, 2, NA, a_pe)

            def transposes4(g, u, r, rows, ready):
                pe.wait_ge(*ready)
                if not known_below(g, 2):
                    pe.wait_ge(r.xt, g - 1)
                for j in range(4):
                    tr = pe.transpose(bank[u][:, j * P:(j + 1) * P], rows[u][:, j, :], ident[:, :])
                tr.then_inc(r.tr, 1)

            def hidden(r, g, u):
                pe.wait_ge(r.xt, g + 1)
                for c in range(KH):
                    if not known_below(g, 1):
                        pe.wait_ge(r.act, KH * (g - 1) + c + 1)
                    pe.matmul(bank[2 + c][:, :], w1_sb[:, c * P:(c + 1) * P], xt[u][:, 0:BANK],
                              start=True, stop=True).then_inc(r.h, 1)

            def b1_pe(g, k, u, first, last):
                hidden(rb, g, u)
                if not last:
                    transposes4(g + 1, 1 - u, rb, xn, (rb.xn, g + 2))
                if not known_below(g, 2):
                    pe.wait_ge(rb.st, g - 1)
                for c in range(KH):
                    pe.wait_ge(rb.act, KH * g + c + 1)
                    for j in range(4):
                        mm = pe.matmul(bank[6 + u][:, j * E:(j + 1) * E], Ht[u][:, c, j * P:(j + 1) * P], wg_sb[:, c, :],
                                       start=(c == 0 and j == 0), stop=(c == KH - 1), skip_group_check=True)
                mm.then_inc(rb.lg, 1)

            def rank(r, half):
                pe.wait_ge(r.mask, half + 1)
                flat = mask.rearrange("p e t -> p (e t)")
                pe.matmul(bank[0][:, 0:EH], before[:, :], flat, start=True, stop=True)
                pe.matmul(bank[1][:, 0:EH], ones[:, :], flat, start=True, stop=True).then_inc(r.ranks, 1)

            pe.wait_ge(a_x, NA)
            pe.wait_ge(w_in, W_ALL)
            for half in range(HALVES):
                if half > 0:
                    pe.wait_ge(rb.places, half)
                transposes4(half * NGH, 0, rb, xn, (rb.xn, half * NGH + 1))
                sweep(pe, half * NGH, (half + 1) * NGH, b1_pe)
                rank(rb, half)

            def b2_pe(g, k, u, first, last):
                hidden(r2, g, u)
                if not last:
                    transposes4(g + 1, 1 - u, r2, xs, (b2_in[1 - u], 16 * (k + (1 if u == 0 else 2))))
                er = load_experts(4 * g, 4)
                if not known_below(g, 2):
                    pe.wait_ge(b2_yo, g - 1)
                for c in range(KH):
                    pe.wait_ge(b2_act, KH * g + c + 1)
                    for j in range(4):
                        mm = pe.matmul(bank[6 + u][:, j * P:(j + 1) * P], Ht[u][:, c, j * P:(j + 1) * P],
                                       wd_sb[:, c, bass.ds(er[j] * D, D)],
                                       start=(c == 0 and j == 0), stop=(c == KH - 1), skip_group_check=True)
                mm.then_inc(b2_y, 1)

            pe.wait_ge(rb.tiles, HALVES)
            transposes4(0, 0, r2, xs, (b2_in[0], 16))
            sweep(pe, 0, NB2, b2_pe)

            for half in range(HALVES):
                if half == 0:
                    pe.wait_ge(b2_yo, NB2)
                else:
                    pe.wait_ge(rd.places, half)
                with pe.Fori(0, NGH // 2) as h0:
                    g0 = 2 * h0 + half * NGH
                    for u in range(2):
                        pe.wait_ge(c1_xn, g0 + u + 1)
                        for b in range(2):
                            for m in range(MC):
                                mm = pe.matmul(bank[4 * u][:, b * N:(b + 1) * N], xn[u][:, MC * b + m, :], adj_sb[:, m, :],
                                               start=(m == 0), stop=(m == MC - 1))
                        mm.then_inc(c1_ax, 1)
                    for u in range(2):
                        pe.wait_ge(c1_axc, g0 + u + 1)
                        pe.matmul(bank[4 * u + 1][:, :], g0_sb[:, :], axt[u], start=True, stop=True).then_inc(c1_h, 1)
                    for u in range(2):
                        pe.wait_ge(c1_hr, g0 + u + 1)
                        for j in range(4):
                            mm = pe.matmul(bank[4 * u + 2][:, j * P:(j + 1) * P], h1[u][:, j * P:(j + 1) * P], g1_sb[:, :],
                                           start=True, stop=True)
                        mm.then_inc(c1_z, 1)
                    for u in range(2):
                        pe.wait_ge(c1_zc, g0 + u + 1)
                        pe.wait_ge(c1_f, g0)
                        for b in range(2):
                            for m in range(MC):
                                mm = pe.matmul(bank[4 * u + 3][:, b * N:(b + 1) * N], zs[u][:, MC * b + m, :], adj_sb[:, m, :],
                                               start=(m == 0), stop=(m == MC - 1))
                        mm.then_inc(c1_g, 1)

                pe.wait_ge(c1_f, (half + 1) * NGH)
                pe.wait_ge(c1_zc, (half + 1) * NGH)
                with pe.Fori(0, LBH) as itl:
                    it = itl + half * LBH
                    for n, (p, t, s, b0, nb) in enumerate(lstm_steps):
                        nw = N // p
                        c = nb * nw
                        xin = F[:, bass.ds(itl * (2 * NSUP * N) + b0 * N, nb * N)].rearrange(
                            "p (b n) -> p b n", n=N)[:, :, t:t + (nw - 1) * p + 1:p]
                        gates = [k for k in range(GATES) if k != 1 or t > 0]
                        if t == 0:
                            pe.wait_ge(l_h, it * NL + (n - 1 if n >= 2 else 0))
                        else:
                            pe.wait_ge(l_act, it * acts_body + acts_before[n - 1])
                        for k in gates:
                            mm = pe.matmul(bank[4 * s + k][:, 0:c].rearrange("p (b n) -> p b n", n=nw),
                                           wih_sb[:, p - 1, k * P:(k + 1) * P], xin, start=True, stop=(t == 0))
                        if t > 0:
                            pe.wait_ge(l_h, it * NL + n - 1)
                            for k in gates:
                                mm = pe.matmul(bank[4 * s + k][:, 0:c], whh_sb[:, p - 1, k * P:(k + 1) * P],
                                               hst[s][:, 0:c], start=False, stop=True)
                        mm.then_inc(l_g, 1)

                with pe.Fori(0, NGH // 2) as h0:
                    g0 = 2 * h0 + half * NGH
                    for u in range(2):
                        pe.wait_ge(t_st, g0 + u + 1)
                        pe.wait_ge(t_x, g0)
                        for j in range(4):
                            tr = pe.transpose(bank[u][:, j * P:(j + 1) * P], xt[u][:, j * P:(j + 1) * P], ident[:, :])
                        tr.then_inc(t_tr, 1)
                pe.wait_ge(t_x, (half + 1) * NGH)
                with pe.Fori(0, NGH // 2) as h0:
                    g0 = 2 * h0 + half * NGH
                    for u in range(2):
                        g = g0 + u
                        pe.wait_ge(rd.xn, g + 1)
                        pe.wait_ge(rd.xt, g0)
                        for j in range(4):
                            tr = pe.transpose(bank[u][:, j * P:(j + 1) * P], xn[u][:, j, :], ident[:, :])
                        tr.then_inc(rd.tr, 1)
                    for u in range(2):
                        g = g0 + u
                        pe.wait_ge(rd.xt, g + 1)
                        pe.wait_ge(rd.st, g0)
                        for j in range(4):
                            mm = pe.matmul(bank[6 + u][:, j * E:(j + 1) * E], xt[u][:, j * P:(j + 1) * P], rt_sb[:, :],
                                           start=True, stop=True)
                        mm.then_inc(rd.lg, 1)
                rank(rd, half)

            def d2_transposes(g, u, n_in):
                pe.wait_ge(d2_in[u], 16 * n_in)
                if not known_below(g, 1):
                    pe.wait_ge(d2_xt, g)
                for j in range(8):
                    tr = pe.transpose(bank[j // 4][:, (j % 4) * P:(j % 4 + 1) * P], xs[u][:, j, :], ident[:, :])
                tr.then_inc(d2_tr, 1)

            def d2_pe(g, k, u, first, last):
                er = load_experts(8 * g, 8)
                pe.wait_ge(d2_xt, g + 1)
                for j in range(10):
                    if j < 8:
                        i = 8 * g + j
                        if not (known_below(g, 1) and j < 2):
                            pe.wait_ge(d2_m, i - 1)
                        for part in range(2):
                            mm = pe.matmul(bank[2 + 2 * (j % 2) + part][:, 0:UP], xt[u][:, j * P:(j + 1) * P],
                                           up_sb[:, bass.ds(er[j] * (2 * UP) + part * UP, UP)], start=True, stop=True)
                        mm.then_inc(d2_h, 1)
                    if 1 <= j < 9:
                        i = 8 * g + j - 1
                        pe.wait_ge(d2_m, i + 1)
                        if not (known_below(g, 1) and j == 1):
                            pe.wait_ge(d2_tc, i)
                        for c in range(KU):
                            kk = min(P, UP - c * P)
                            mm = pe.transpose(bank[6][0:kk, c * P:(c + 1) * P], hm[(j - 1) % 2][:, c * P:c * P + kk],
                                              ident[:, :])
                        mm.then_inc(d2_tt, 1)
                    if j >= 2:
                        i = 8 * g + j - 2
                        pe.wait_ge(d2_tc, i + 1)
                        pe.wait_ge(d2_yo, i)
                        for c in range(KU):
                            kk = min(P, UP - c * P)
                            mm = pe.matmul(bank[7][:, (j % 4) * P:(j % 4 + 1) * P], ht[j % 2][0:kk, c, :],
                                           down_sb[0:kk, bass.ds(er[j - 2] * (KU * D) + c * D, D)],
                                           start=(c == 0), stop=(c == KU - 1))
                        mm.then_inc(d2_y, 1)
                    if j == 8 and not last:
                        d2_transposes(g + 1, 1 - u, k + (1 if u == 0 else 2))

            pe.wait_ge(rd.tiles, HALVES)
            pe.wait_ge(up_in, 16 * (1 + KU))
            d2_transposes(0, 0, 1)
            sweep(pe, 0, ND2, d2_pe)

        @block.vector
        def _(dve):
            def L(ins):
                link(dve, ins)

            def ln_finish(lo, hi):
                me, ve, mo, vo = (ST[:, lo:hi, i] for i in (1, 2, 4, 5))
                s, d, v, t = (ln_t[:, i, 0:hi - lo] for i in range(4))
                L(dve.tensor_tensor(s, me, mo, ALU.add))
                L(dve.tensor_tensor(d, me, mo, ALU.subtract))
                L(dve.tensor_tensor(v, ve, vo, ALU.add))
                L(dve.tensor_scalar(MEAN[:, lo:hi], s, 0.5, None, ALU.mult))
                L(dve.tensor_scalar(v, v, 1.0 / D, LN_EPS, ALU.mult, ALU.add))
                L(dve.tensor_tensor(d, d, d, ALU.mult))
                L(dve.scalar_tensor_tensor(v, d, 0.25, v, ALU.mult, ALU.add))
                bits, guess = (ln_i[:, i, 0:hi - lo] for i in range(2))
                L(dve.tensor_scalar(bits, v.bitcast(I32), 1, None, ALU.arith_shift_right))
                L(dve.tensor_scalar(guess, bits, -1.0, float(RSQRT_MAGIC), ALU.mult, ALU.add))
                y = guess.bitcast(F32)
                for i in range(3):
                    L(dve.tensor_tensor(t, y, y, ALU.mult))
                    L(dve.scalar_tensor_tensor(t, t, -0.5, v, ALU.mult, ALU.mult))
                    L(dve.scalar_tensor_tensor(RSTD[:, lo:hi], t, 1.5, y, ALU.add, ALU.mult))
                    y = RSTD[:, lo:hi]

            def normalise(g, n, dst, done, step_sem, count):
                dve.tensor_tensor(dst, X[:, bass.ds(g * n, n), :], bcast(MEAN[:, bass.ds(g * n, n)], 2, D),
                                  ALU.subtract).then_inc(step_sem, 1)
                dve.wait_ge(step_sem, count + 1)
                dve.tensor_tensor(dst, dst, bcast(RSTD[:, bass.ds(g * n, n)], 2, D), ALU.mult).then_inc(done, 1)

            dve.wait_ge(const_ready, 1)
            for g in range(NX):
                dve.wait_ge(x_in[g], 16)
                for t in range(8 * g, 8 * g + 8):
                    dve.bn_stats(ST[:, t, :], X[:, t, :]).then_inc(a_st, 1)
            dve.wait_ge(a_st, NTILE)
            ln_finish(0, NTILE)
            dve.wait_ge(wa_in, WA_ALL)
            normalise(0, 8, xn[0][:, :, :], a_xn, a_ns, 0)

            def a_gate(g, u):
                dve.wait_ge(a_z, g + 1)
                dve.tensor_tensor(zb[u].rearrange("p (b c) k -> p b c k", c=MC),
                                  bank[2][:, 0:24].rearrange("p (b c k) -> p b c k", c=MC, k=3),
                                  bcast(gb_sb[:, :, :], 1, 4), ALU.add).then_inc(a_zb, 1)
                dve.wait_ge(a_th, g + 1)
                dve.tensor_scalar(sg[u], th[u], 0.5, 0.5, ALU.mult, ALU.add).then_inc(a_s, 1)
                dve.wait_ge(a_s, g + 1)
                dve.tensor_tensor(us[u], sg[u][:, :, 0], sg[u][:, :, 1], ALU.add).then_inc(a_us, 1)

            def a_finish(g, u):
                dve.wait_ge(a_ax, g + 1)
                dve.wait_ge(a_us, g + 1)
                uv = us[u].rearrange("p (b c) -> p b c", c=MC)
                tv = t1.rearrange("p (b c) d -> p b c d", c=MC)
                for c in range(MC):
                    ins = dve.tensor_tensor(tv[:, :, c, :], bank[4 + 2 * u + c][:, :].rearrange("p (b d) -> p b d", d=D),
                                            bcast(uv[:, :, c], 2, D), ALU.mult)
                ins.then_inc(a_mul, 1)
                dve.wait_ge(a_mul, g + 1)
                dve.wait_ge(a_q, g + 1)
                dve.tensor_tensor(t1, t1, q1[u], ALU.add).then_inc(a_t1, 1)
                dve.wait_ge(a_t1, g + 1)
                xv = X[:, bass.ds(8 * g, 8), :]
                dve.scalar_tensor_tensor(xv, t1, 0.0, xv, ALU.max, ALU.add).then_inc(a_x, 1)
                dve.wait_ge(a_x, g + 1)
                for j in range(8):
                    ins = dve.bn_stats(ST[:, bass.ds(8 * g + j, 1), :].rearrange("p a k -> p (a k)"),
                                       X[:, bass.ds(8 * g + j, 1), :].rearrange("p a k -> p (a k)"))
                ins.then_inc(a_st2, 1)

            def a_dve(g, k, u, first, last):
                if not last:
                    if not known_below(g, 1):
                        dve.wait_ge(a_z, g)
                        dve.wait_ge(a_c3, g)
                    normalise(g + 1, 8, xn[1 - u][:, :, :], a_xn, a_ns, g + 1)
                a_gate(g, u)
                if not first:
                    a_finish(g - 1, 1 - u)

            a_dve(0, 0, 0, True, False)
            sweep(dve, 1, NA, lambda g, k, u, first, last: a_dve(g, k, u, False, last))
            a_finish(NA - 1, (NA - 1) % 2)
            dve.wait_ge(w_in, W_ALL)
            dve.wait_ge(row_sums, 1)
            L(dve.tensor_scalar(bga_sb[:, :], bank[3][:, 0:N], g0b_sb[:, 0:1], None, ALU.mult))
            L(dve.tensor_tensor(lb_sb[:, :], bih_sb[:, :], bhh_sb[:, :], ALU.add))
            dve.wait_ge(a_st2, NA)

            def norm_rows(r, g, u, ns):
                normalise(g, 4, xn[u][:, 0:4, :], r.xn, ns, 2 * g)
                dve.wait_ge(r.xn, g + 1)
                dve.tensor_copy(XN[:, bass.ds(4 * g, 4), :], xn[u][:, 0:4, :]).then_inc(ns, 1)

            def choose(r, g, u, bias, cs):
                dve.wait_ge(r.lg, g + 1)
                src = bank[6 + u][:, 0:4 * E].rearrange("p (j e) -> p j e", e=E)
                if bias is not None:
                    dve.tensor_tensor(lg_st[u][:, :, :], src, bcast(bias, 1, 4), ALU.add).then_inc(r.st, 1)
                else:
                    dve.tensor_copy(lg_st[u][:, :, :], src).then_inc(r.st, 1)
                dve.wait_ge(r.st, g + 1)
                dve.tensor_copy(wait_c[u][:, 0:1], lg_st[u][:, 0, 0:1])
                for j in range(4):
                    dve.max(mx_st[u][:, j, :], lg_st[u][:, j, :]).then_inc(r.mx, 1)
                dve.wait_ge(r.mx, 4 * g + 4)
                dve.tensor_copy(wait_c[u][:, 1:2], mx_st[u][:, 0, 0:1])
                for j in range(4):
                    dve.max_index(ix_st[u][:, j, :], mx_st[u][:, j, :], lg_st[u][:, j, :]).then_inc(r.copied, 1)
                dve.tensor_copy(MX[:, bass.ds(4 * g, 4), :], mx_st[u][:, :, :]).then_inc(cs, 1)
                dve.wait_ge(r.copied, 4 * g + 4)
                dve.tensor_copy(IX[:, bass.ds(4 * g, 4), :], ix_st[u][:, :, :]).then_inc(r.ix, 1)

            def route(r, half, bias, ns, cs):
                g0 = half * NGH
                norm_rows(r, g0, 0, ns)

                def body(g, k, u, first, last):
                    if not last:
                        if not known_below(g, 1):
                            dve.wait_ge(r.tr, g)
                        dve.wait_ge(ns, 2 * g + 2)
                        norm_rows(r, g + 1, 1 - u, ns)
                    choose(r, g, u, bias, cs)

                sweep(dve, g0, g0 + NGH, body)
                dve.wait_ge(cs, g0 + NGH)
                dve.wait_ge(ns, 2 * (g0 + NGH))

            def places(r, half, K, nslot):
                lo, hi = half * NH, (half + 1) * NH
                dve.wait_ge(r.ix, (half + 1) * NGH)
                for k in range(K):
                    L(dve.tensor_tensor(oh[k], bcast(iota_e[:, :], 2, NH), bcast(IX[:, lo:hi, k], 1, E), ALU.is_equal))
                if K == 2:
                    ins = dve.tensor_tensor(mask, oh[0], oh[1], ALU.add)
                else:
                    ins = dve.tensor_copy(mask, oh[0])
                ins.then_inc(r.mask, 1)

                def by_token(v):
                    return v.rearrange("p e t -> p (e t)").rearrange("p (t e) -> p t e", e=E)

                def flat(v):
                    return v.rearrange("p e t -> p (e t)")

                dve.tensor_tensor(by_token(rw2), MX[:, lo:hi, :], bcast(MX[:, lo:hi, 0], 2, E), ALU.subtract).then_inc(r.flat, 1)
                dve.wait_ge(r.ranks, half + 1)
                L(dve.tensor_copy(flat(tot), bank[1][:, 0:EH]))
                L(dve.tensor_tensor_scan(flat(cum), ones_row[:, 0:EH], flat(tot), 0.0, ALU.mult, ALU.add))
                start, count, ntile, end, corr, tmp = (small[:, i, :] for i in range(6))
                L(dve.tensor_tensor(start, cum[:, :, 0], tot[:, :, 0], ALU.subtract))
                L(dve.tensor_tensor(count, cum[:, :, NH - 1], start, ALU.subtract))
                dve.wait_ge(r.flat, 2 * half + 2)
                ex = by_token(rw1)
                den, p1, p2, dn = (ln_t[:, i, 0:NH] for i in range(4))
                L(dve.tensor_reduce(den, ex, AX_X, ALU.add))
                L(dve.reciprocal(p1, den))
                if K == 1:
                    L(dve.tensor_copy(GT[:, 0, lo:hi], p1))
                else:
                    L(dve.tensor_tensor(p2, ex[:, :, 1], p1, ALU.mult))
                    L(dve.scalar_tensor_tensor(dn, p1, TOPK_EPS, p2, ALU.add, ALU.add))
                    L(dve.reciprocal(den, dn))
                    L(dve.tensor_tensor(GT[:, 0, lo:hi], p1, den, ALU.mult))
                    L(dve.tensor_tensor(GT[:, 1, lo:hi], p2, den, ALU.mult))
                L(dve.tensor_tensor(rw2, bcast(count, 2, NH), bcast(iota_t[:, :], 1, E), ALU.is_gt))
                L(dve.tensor_reduce(ntile, rw2, AX_X, ALU.add))
                L(dve.tensor_tensor_scan(end, ones_row[:, 0:E], ntile, 0.0, ALU.mult, ALU.add))
                L(dve.tensor_tensor(tmp, end, ntile, ALU.subtract))
                L(dve.scalar_tensor_tensor(corr, tmp, float(P), start, ALU.mult, ALU.subtract))
                L(dve.tensor_tensor(rw1, cum, tot, ALU.subtract))
                L(dve.tensor_tensor(rw1, rw1, bcast(corr, 2, NH), ALU.add))
                L(dve.tensor_tensor(flat(rw1), bank[0][:, 0:EH], flat(rw1), ALU.add))
                for k in range(K):
                    L(dve.tensor_tensor(rw2, oh[k], rw1, ALU.mult))
                    L(dve.tensor_reduce(dest_f[:, k, :], rw2.rearrange("p e t -> p t e"), AX_X, ALU.add))
                dve.tensor_copy(dest_i[:, 0:K, lo:hi], dest_f[:, 0:K, :]).then_inc(r.places, 1)
                L(dve.tensor_tensor(tcmp[0:1, 0:nslot, :], bcast(iota_s[0:1, 0:nslot], 2, E),
                                    bcast(end[0:1, :], 1, nslot), ALU.is_ge))
                L(dve.tensor_reduce(te[0:1, 0:nslot], tcmp[0:1, 0:nslot, :], AX_X, ALU.add))
                tl = tile_e[:, :, :].rearrange("a h s -> a (h s)")[:, half * nslot:(half + 1) * nslot]
                dve.tensor_scalar(tl, te[0:1, 0:nslot], float(E - 1), None, ALU.min).then_inc(r.tiles, 1)
                dve.wait_ge(r.tiles, half + 1)

            ln_finish(0, NTILE)
            dve.wait_ge(zeroed, ZEROS)
            for half in range(HALVES):
                route(rb, half, bg_sb[:, :], nsb, csb)
                places(rb, half, 1, NSLOT0)

            def b2_dve(g, k, u, first, last):
                tile_list = tile_e[:, :, :].rearrange("a h s -> a (h s)")
                _, er = nc.values_load_multi_w_load_instructions(
                    tile_list[0:1, bass.ds(4 * g, 4)], engines=[DVE_ENGINE], min_val=0, max_val=E - 1,
                    skip_runtime_bounds_check_because="clamped to the last expert where it is computed")
                dve.wait_ge(b2_y, g + 1)
                if not known_below(g, 2):
                    dve.wait_ge(b2_out[u], 16 * k)
                for j in range(4):
                    ins = dve.tensor_tensor(yb[u][:, j, :], bank[6 + u][:, j * P:(j + 1) * P],
                                            bd_sb[:, bass.ds(er[j] * D, D)], ALU.add)
                ins.then_inc(b2_yo, 1)

            b2_dve(0, 0, 0, True, False)
            sweep(dve, 1, NB2, b2_dve)

            for half in range(HALVES):
                for g in range(half * NXH, (half + 1) * NXH):
                    dve.wait_ge(s_gath[0][g], 16 * 8)
                    for t in range(8 * g, 8 * g + 8):
                        dve.scalar_tensor_tensor(X[:, t, :], XN[:, t, :], GT[:, 0, t:t + 1], X[:, t, :], ALU.mult,
                                                 ALU.add).then_inc(b3_x, 1)
                    for t in range(8 * g, 8 * g + 8):
                        dve.wait_ge(b3_x, t + 1)
                        dve.bn_stats(ST[:, t, :], X[:, t, :]).then_inc(b3_t, 1)
                dve.wait_ge(b3_t, (half + 1) * NH)
                ln_finish(half * NH, (half + 1) * NH)

                with dve.Fori(0, NGH // 2) as h0:
                    g0 = 2 * h0 + half * NGH
                    for u in range(2):
                        dve.wait_ge(c1_ax, g0)
                        normalise(g0 + u, 4, xn[u][:, 0:4, :], c1_xn, nsg, g0 + u)
                    for u in range(2):
                        dve.wait_ge(c1_h, g0 + u + 1)
                        dve.wait_ge(c1_hr, g0)
                        dve.tensor_tensor(hb[u].rearrange("p (b n) -> p b n", n=N),
                                          bank[4 * u + 1][:, :].rearrange("p (b n) -> p b n", n=N),
                                          bcast(bga_sb[:, :], 1, 2), ALU.add).then_inc(c1_hb, 1)
                    for u in range(2):
                        dve.wait_ge(c1_z, g0 + u + 1)
                        dve.wait_ge(c1_g, g0)
                        dve.tensor_tensor(zs[u], bank[4 * u + 2][:, :].rearrange("p (a b) -> p a b", b=P),
                                          bcast(g1b_sb[:, :], 1, 4), ALU.add).then_inc(c1_zc, 1)

                for u in range(2):
                    dve.wait_ge(b2_out[u], 16 * (NB2 // 2))
                with dve.Fori(0, LBH) as itl:
                    it = itl + half * LBH
                    for n, (p, t, s, b0, nb) in enumerate(lstm_steps):
                        nw = N // p
                        c = nb * nw
                        gi, gf, gg, go = (gb[s][k][:, 0:c] for k in range(GATES))
                        cc, tc = cst[s][:, 0:c], tcs[s][:, 0:c]
                        seen = it * acts_body + acts_before[n]
                        dve.wait_ge(l_act, seen + 2)
                        if t == 0:
                            dve.tensor_tensor(cc, gi, gg, ALU.mult).then_inc(l_c, 1)
                        else:
                            late = [q[1] > 0 for q in lstm_steps]
                            dve.tensor_tensor(gi, gi, gg, ALU.mult).then_inc(l_ig, 1)
                            dve.wait_ge(l_act, seen + 3)
                            dve.tensor_tensor(gf, gf, cc, ALU.mult).then_inc(l_ig, 1)
                            dve.wait_ge(l_ig, it * (2 * sum(late)) + 2 * sum(late[:n]) + 2)
                            dve.tensor_tensor(cc, gi, gf, ALU.add).then_inc(l_c, 1)
                        dve.wait_ge(l_act, it * acts_body + acts_before[n + 1])
                        dve.wait_ge(l_tc, it * NL + n + 1)
                        if t == p - 1:
                            dst = F[:, bass.ds(itl * (2 * NSUP * N) + b0 * N, nb * N)].rearrange(
                                "p (b n) -> p b n", n=N)[:, :, t:t + (nw - 1) * p + 1:p]
                            dve.tensor_tensor(dst, go.rearrange("p (b n) -> p b n", n=nw),
                                              tc.rearrange("p (b n) -> p b n", n=nw), ALU.mult).then_inc(l_h, 1)
                        else:
                            dve.tensor_tensor(hst[s][:, 0:c], go, tc, ALU.mult).then_inc(l_h, 1)

                with dve.Fori(0, NGH // 2) as h0:
                    g0 = 2 * h0 + half * NGH
                    for u in range(2):
                        g = g0 + u
                        dve.wait_ge(t_tr, g + 1)
                        xv = X[:, bass.ds(4 * g, 4), :]
                        dve.tensor_tensor(xv, bank[u][:, :].rearrange("p (a b) -> p a b", b=P), xv, ALU.add).then_inc(t_x, 1)
                        dve.wait_ge(t_x, g + 1)
                        for j in range(4):
                            ins = dve.bn_stats(ST[:, bass.ds(4 * g + j, 1), :].rearrange("p a k -> p (a k)"),
                                               X[:, bass.ds(4 * g + j, 1), :].rearrange("p a k -> p (a k)"))
                        ins.then_inc(t_ln, 1)
                dve.wait_ge(t_ln, (half + 1) * NGH)
                ln_finish(half * NH, (half + 1) * NH)
                route(rd, half, None, nsd, csd)
                places(rd, half, 2, NSLOT1)

            def d2_dve(g, k, u, first, last):
                if not known_below(g, 2):
                    dve.wait_ge(d2_out[u], 16 * k)
                for j in range(10):
                    if j < 8:
                        i = 8 * g + j
                        dve.wait_ge(d2_silu, i + 1)
                        if not (known_below(g, 1) and j < 2):
                            dve.wait_ge(d2_tt, i - 1)
                        dve.tensor_tensor(hm[j % 2], sl[j % 2], bank[3 + 2 * (j % 2)][:, 0:UP], ALU.mult).then_inc(d2_m, 1)
                    if j >= 2:
                        i = 8 * g + j - 2
                        dve.wait_ge(d2_y, i + 1)
                        dve.tensor_copy(yd[u][:, j - 2, :], bank[7][:, (j % 4) * P:(j % 4 + 1) * P]).then_inc(d2_yo, 1)

            d2_dve(0, 0, 0, True, False)
            sweep(dve, 1, ND2, d2_dve)
            for g in range(NX):
                dve.wait_ge(s_gath[1][g], 16 * 16)
                for k in range(2):
                    for t in range(8 * g, 8 * g + 8):
                        src = XN[:, t, :] if k == 0 else Y1[t // NH][:, t % NH, :]
                        if k == 1:
                            dve.wait_ge(d3_x, 16 * g + t % 8 + 1)
                        dve.scalar_tensor_tensor(X[:, t, :], src, GT[:, k, t:t + 1], X[:, t, :], ALU.mult,
                                                 ALU.add).then_inc(d3_x, 1)


def layouts(i):
    import numpy as np
    c = np.ascontiguousarray
    N = i["adj"].shape[0]
    E, H, C = i["L1_ffn_w1"].shape
    S, G4, Dh = i["L1_gnn_Wih"].shape
    x = c(i["x"].reshape(-1, i["x"].shape[-1]))
    return dict(
        x=x, adj_t=c(i["adj"].T),
        bias_io=c(np.concatenate([i["L0_gnn_bias_in"], i["L0_gnn_bias_out"]], axis=1)),
        gate_w=c(np.concatenate([i["L0_gnn_gate_w_in"], i["L0_gnn_gate_w_out"], i["L0_gnn_loop_gate"]], axis=1)),
        gate_b=c(np.concatenate([i["L0_gnn_gate_b_in"], i["L0_gnn_gate_b_out"],
                                 np.zeros((N, 1), i["L0_gnn_gate_b_in"].dtype)], axis=1)),
        w1=c(i["L0_ffn_W1"]), b1=c(i["L0_ffn_b1"].reshape(-1, 128).T), wg=c(i["L0_ffn_Wg"]), bg=c(i["L0_ffn_bg"]),
        wd=c(np.transpose(i["L0_ffn_Wd"], (1, 0, 2)).reshape(i["L0_ffn_Wd"].shape[1], -1)),
        bd=c(i["L0_ffn_bd"].reshape(-1)),
        g0_w=c(i["L1_gnn_Wg0"]), g0_b=c(i["L1_gnn_bg0"].reshape(-1, 1)), g1_w=c(i["L1_gnn_Wg1"]), g1_b=c(i["L1_gnn_bg1"]),
        wih_t=c(np.transpose(i["L1_gnn_Wih"], (0, 2, 1))), whh_t=c(np.transpose(i["L1_gnn_Whh"], (0, 2, 1))),
        bih=c(i["L1_gnn_bih"].reshape(-1, 128).T), bhh=c(i["L1_gnn_bhh"].reshape(-1, 128).T),
        router_t=c(i["L1_ffn_router_w"].T),
        up_t=c(np.concatenate([np.transpose(i["L1_ffn_w1"], (0, 2, 1)), np.transpose(i["L1_ffn_w3"], (0, 2, 1))], axis=2)),
        down_t=c(np.transpose(i["L1_ffn_w2"], (0, 2, 1))),
    )


def kernel(**inputs):
    import concourse.bacc as bacc
    import numpy as np
    from concourse.bass_utils import run_bass_kernel_spmd

    shape = inputs["x"].shape
    arrays = layouts({name: np.asarray(a) for name, a in inputs.items()})
    nc = bacc.Bacc("TRN2", target_bir_lowering=False, num_devices=1)
    aps = [nc.dram_tensor(name, a.shape, mybir.dt.from_np(a.dtype), kind="ExternalInput").ap()
           for name, a in arrays.items()]
    out = nc.dram_tensor("out", arrays["x"].shape, F32, kind="ExternalOutput").ap()
    build(nc, *aps, out)
    result = run_bass_kernel_spmd(nc, [arrays], core_ids=[0])
    return result.results[0]["out"].reshape(shape)
```

```python
from contextlib import ExitStack

import concourse.bass as bass
from concourse import mybir

P = 128
F32 = mybir.dt.float32
I32 = mybir.dt.int32
U32 = mybir.dt.uint32
ALU = mybir.AluOpType
ACT = mybir.ActivationFunctionType
AX_X = mybir.AxisListType.X
PE_ENGINE = mybir.EngineType.PE
DVE_ENGINE = mybir.EngineType.DVE
LN_EPS = 1e-5
RSQRT_MAGIC = 0x5F3759DF
TOPK_EPS = 1e-9
BANK = 512


def bcast(ap, axis, n):
    v = ap.unsqueeze(axis)
    shape = list(v.shape)
    shape[axis] = n
    return v.broadcast_to(shape)


class HiddenSems:

    def __init__(self, tr, xt, h, act, lg):
        self.tr, self.xt, self.h, self.act, self.lg = tr, xt, h, act, lg


class RouteSems(HiddenSems):

    def __init__(self, xn, tr, xt, h, act, lg, st, mx, ix, copied, flat, ranks, ranks_sb, mask, tiles):
        super().__init__(tr, xt, h, act, lg)
        self.xn, self.st, self.mx, self.ix, self.copied = xn, st, mx, ix, copied
        self.flat, self.ranks, self.ranks_sb, self.mask, self.tiles = flat, ranks, ranks_sb, mask, tiles


def build(nc, x, adj_t, bias_io, gate_w, gate_b, w1, b1, wg, bg, wd, bd, g0_w, g0_b, g1_w, g1_b, wih_t, whh_t, bih, bhh,
          router_t, up_t, down_t, out):
    TOK, D = x.shape
    NTILE = TOK // P
    N = adj_t.shape[0]
    MC = N // P
    E = router_t.shape[1]
    HID = w1.shape[1]
    KH = HID // P
    UP = up_t.shape[2] // 2
    KU = -(-UP // P)
    MAX_SKIP = wih_t.shape[0]
    GATES = 4
    assert D == P and E == 8 and MC == 2 and MAX_SKIP == 4

    HALVES = 2
    NH = NTILE // HALVES
    NSLOT0 = -(-(NH + E - 1) // 4) * 4
    NSLOT1 = -(-(2 * NH + E - 1) // 8) * 8

    with ExitStack() as ctx:
        def sb(name, shape, dt=F32):
            return ctx.enter_context(nc.sbuf_tensor("sb_" + name, shape, dt))

        def sem(name):
            return ctx.enter_context(nc.semaphore(name))

        sorted_in = [nc.dram_tensor(f"sorted_in{h}", [NSLOT1 * P, D], F32, kind="Internal").ap() for h in range(HALVES)]
        sorted_out = [nc.dram_tensor(f"sorted_out{h}", [NSLOT1 * P, D], F32, kind="Internal").ap() for h in range(HALVES)]

        X = sb("X", [P, NTILE, D])
        R1 = sb("R1", [P, NTILE * D])
        R2 = sb("R2", [P, NTILE * D])
        R3 = sb("R3", [P, 6 * BANK])
        XN = R1[:, :].rearrange("p (t d) -> p t d", d=D)
        xn = [sb(f"xn{u}", [P, 8, D]) for u in range(2)]
        XS = sb("XS", [P, 2 * 8 * D])
        xt = [sb(f"xt{u}", [P, 8 * P]) for u in range(2)]
        ident = sb("ident", [P, P])
        before = sb("before", [P, P])
        ones = sb("ones", [P, P])
        ones_row = sb("ones_row", [P, E * NH])
        iota_e = sb("iota_e", [P, E])
        iota_t = sb("iota_t", [P, NH])
        iota_s = sb("iota_s", [1, NSLOT1])
        adj_sb = sb("adj_sb", [P, MC, N])
        bias_sb = sb("bias_sb", [P, MC, 2, D])
        gw_sb = sb("gw_sb", [P, 3])
        gb_sb = sb("gb_sb", [P, MC, 3])
        w1_sb = sb("w1_sb", [P, HID])
        b1_sb = sb("b1_sb", [P, KH])
        wg_sb = sb("wg_sb", [P, KH, E])
        bg_sb = sb("bg_sb", [P, E])
        BIG = sb("BIG", [P, E * (2 * UP + KU * D)])
        wd_sb = BIG[:, 0:KH * E * D].rearrange("p (k n) -> p k n", k=KH)
        bd_sb = BIG[:, KH * E * D:(KH + 1) * E * D]
        up_sb = BIG[:, 0:E * 2 * UP]
        down_sb = BIG[:, E * 2 * UP:E * (2 * UP + KU * D)]
        g0_sb = sb("g0_sb", [P, D])
        g1_sb = sb("g1_sb", [P, D])
        g0b_sb = sb("g0b_sb", [P, 1])
        g1b_sb = sb("g1b_sb", [P, D])
        bga_sb = sb("bga_sb", [P, N])
        wih_sb = sb("wih_sb", [P, MAX_SKIP, GATES * P])
        whh_sb = sb("whh_sb", [P, MAX_SKIP, GATES * P])
        bih_sb = sb("bih_sb", [P, MAX_SKIP * GATES])
        bhh_sb = sb("bhh_sb", [P, MAX_SKIP * GATES])
        lb_sb = sb("lb_sb", [P, MAX_SKIP * GATES])
        rt_sb = sb("rt_sb", [P, E])
        ST = sb("ST", [P, NTILE, 6])
        MEAN = sb("MEAN", [P, NTILE])
        RSTD = sb("RSTD", [P, NTILE])
        ln_t = sb("ln_t", [P, 4, NTILE])
        ln_i = sb("ln_i", [P, 2, NTILE], I32)
        MX = sb("MX", [P, NTILE, E])
        IX = sb("IX", [P, NTILE, E])
        lg_st = [sb(f"lg_st{u}", [P, 4, E]) for u in range(2)]
        mx_st = [sb(f"mx_st{u}", [P, 4, E]) for u in range(2)]
        ix_st = [sb(f"ix_st{u}", [P, 4, E], U32) for u in range(2)]
        wait_c = [sb(f"wait_c{u}", [P, 2]) for u in range(2)]
        GT = sb("GT", [P, 2, NTILE])
        dest_i = sb("dest_i", [P, 2, NTILE], I32)
        tile_e = sb("tile_e", [1, HALVES, NSLOT1], I32)

        bank = [ctx.enter_context(nc.psum_tensor(f"bank{i}", [P, BANK], F32)) for i in range(8)]

        def view(region, at, *shape):
            n = 1
            for s in shape:
                n *= s
            names = "abcd"[:len(shape)]
            v = region[:, at:at + n]
            if len(shape) == 1:
                return v
            return v.rearrange(f"p ({' '.join(names)}) -> p {' '.join(names)}", **dict(zip(names, shape)))

        block = ctx.enter_context(nc.Block())

        NX = 8
        x_in = [sem(f"x_in{i}") for i in range(NX)]
        wa_in, w_in = sem("wa_in"), sem("w_in")
        up_in = sem("up_in")
        const_ready = sem("const_ready")
        zero_ready = sem("zero_ready")
        zeroed = sem("zeroed")

        loads_w = [
            (adj_sb[:, :, :], adj_t.rearrange("(c p) n -> p c n", p=P)),
            (bias_sb[:, :, :, :].rearrange("p c i d -> p c (i d)"), bias_io.rearrange("(c p) n -> p c n", p=P)),
            (gw_sb[:, :], gate_w),
            (gb_sb[:, :, :], gate_b.rearrange("(c p) n -> p c n", p=P)),
            (w1_sb[:, :], w1),
            (b1_sb[:, :], b1),
            (wg_sb[:, :, :], wg.rearrange("(k p) e -> p k e", p=P)),
            (bg_sb[:, :], bg.partition_broadcast(P)),
            (wd_sb, wd.rearrange("(k p) n -> p k n", p=P)),
            (bd_sb, bd.partition_broadcast(P)),
            (g0_sb[:, :], g0_w), (g1_sb[:, :], g1_w), (g0b_sb[:, :], g0_b),
            (g1b_sb[:, :], g1_b.partition_broadcast(P)),
            (wih_sb[:, :, :], wih_t.rearrange("s p n -> p s n")),
            (whh_sb[:, :, :], whh_t.rearrange("s p n -> p s n")),
            (bih_sb[:, :], bih), (bhh_sb[:, :], bhh), (rt_sb[:, :], router_t),
        ]
        loads_a, loads_w = loads_w[:4], loads_w[4:]
        WA_ALL, W_ALL = 16 * len(loads_a), 16 * len(loads_w)

        NA = NTILE // 8
        a_xn, a_tr, a_xt, a_z, a_ax, a_zb, a_th, a_s, a_us, a_c2, a_c3, a_q, a_mul, a_t1, a_x, a_ns, a_st, a_st2 = (
            sem("a_" + n) for n in ("normed transposed copied z mixed zbias tanh gate gate_sum gated_out gated_loop bias "
                                    "scaled summed done norm_step stats stats2").split())
        zb = [view(R2, u * 24, 8, 3) for u in range(2)]
        th = [view(R2, 64 + u * 24, 8, 3) for u in range(2)]
        sg = [view(R2, 128 + u * 24, 8, 3) for u in range(2)]
        us = [view(R2, 192 + u * 8, 8) for u in range(2)]
        q1, q2, q3 = ([view(R2, 512 + (2 * i + u) * 8 * D, 8, D) for u in range(2)] for i in range(3))
        t1 = view(R3, 0, 8, D)
        ZW = 9 * D
        zero = view(R2, 512 + 6 * 8 * D, ZW)

        row_sums = sem("row_sums")
        dve_step = sem("dve_step")
        pool_step = sem("pool_step")
        n_dve = [0]
        n_pool = [0]

        def link(eng, ins):
            ins.then_inc(dve_step, 1)
            n_dve[0] += 1
            eng.wait_ge(dve_step, n_dve[0])

        def route_sems(tag):
            return RouteSems(*(sem(f"{tag}_{n}") for n in (
                "normed", "transposed", "copied", "hidden", "gelu", "logits", "staged", "sorted", "chosen", "indexed",
                "softmax", "ranks", "ranks_copied", "mask", "tiles")))

        rb, rd = route_sems("b1"), route_sems("d1")
        NG = NTILE // 4
        Ht = [view(R2, u * KH * BANK, KH, BANK) for u in range(2)]
        EH = E * NH

        class RouteSpace:
            def __init__(self, region, at):
                self.oh = [view(region, at + k * EH, E, NH) for k in range(2)]
                self.mask, self.tot, self.cum, self.rank, self.w1, self.w2 = (
                    view(region, at + k * EH, E, NH) for k in range(2, 8))
                self.tcmp = view(region, at, NSLOT1, E)

        space = {(0, 0): RouteSpace(R2, 2 * KH * BANK), (0, 1): RouteSpace(R2, 2 * KH * BANK),
                 (1, 0): RouteSpace(XS, 0), (1, 1): RouteSpace(R2, 2 * KH * BANK)}
        small = sb("small", [P, 6, E])
        wts = sb("wts", [P, 4, NH])
        dest_f = sb("dest_f", [P, 2, NH])
        te = sb("te", [1, NSLOT1])

        def by_token(v):
            return v.rearrange("p e t -> p (e t)").rearrange("p (t e) -> p t e", e=E)

        def flat(v):
            return v.rearrange("p e t -> p (e t)")

        s_scat = {l: [sem(f"{'bd'[l]}_scattered{h}") for h in range(HALVES)] for l in range(2)}
        s_gath = {0: [sem(f"b_gathered{i}") for i in range(NX)], 1: [sem(f"d_gathered{i}") for i in range(NX)]}
        b2_in = [sem("b2_in0"), sem("b2_in1")]
        b2_tr, b2_xt, b2_h, b2_act, b2_y, b2_yo = (sem("b2_" + n) for n in "tr xt h act y yo".split())
        r2 = HiddenSems(b2_tr, b2_xt, b2_h, b2_act, b2_y)
        nsb, csb, nsd, csd, nsg = (sem(n) for n in (
            "b1_norm_step", "b1_choose_step", "d1_norm_step", "d1_choose_step", "g_norm_step"))
        b2_out = [sem("b2_out0"), sem("b2_out1")]
        NB2 = HALVES * NSLOT0 // 4
        xs = [view(XS, u * 8 * D, 8, D) for u in range(2)]
        yb = [view(R3, u * BANK, 4, D) for u in range(2)]
        b3_x, b3_t = sem("b3_x"), sem("b3_t")

        c1_xn, c1_ax, c1_axc, c1_h, c1_hb, c1_hr, c1_z, c1_zc, c1_g, c1_f = (
            sem("g_" + n) for n in "normed mixed mixed_sb h0 h0_biased h0_relu z1 z1_sb h1 done".split())
        F = R2
        WK = NH * P
        axt = [view(R2, WK + u * BANK, BANK) for u in range(2)]
        hb = [view(R2, WK + (2 + u) * BANK, BANK) for u in range(2)]
        h1 = [view(R2, WK + (4 + u) * BANK, BANK) for u in range(2)]
        zs = [view(R2, WK + (6 + u) * BANK, 4, P) for u in range(2)]

        l_x, l_g, l_act, l_ig, l_fc, l_c, l_tc, l_h = (sem("l_" + n) for n in "x g act ig fc c tc h".split())
        gb = [[view(R2, WK + (u * GATES + k) * BANK, BANK) for k in range(GATES)] for u in range(2)]
        cst = [view(R3, u * BANK, BANK) for u in range(2)]
        tcs = [view(R3, (2 + u) * BANK, BANK) for u in range(2)]
        hst = [view(R3, (4 + u) * BANK, BANK) for u in range(2)]

        t_st, t_tr, t_x, t_ln = (sem("t_" + n) for n in "st tr x ln".split())

        ND2 = HALVES * NSLOT1 // 8
        d2_in = [sem("d2_in0"), sem("d2_in1")]
        d2_tr, d2_xt, d2_h, d2_silu, d2_m, d2_tt, d2_tc, d2_y, d2_yo = (
            sem("d2_" + n) for n in "tr xt h silu m tt tc y yo".split())
        d2_out = [sem("d2_out0"), sem("d2_out1")]
        sl = [view(R3, u * KU * P, UP) for u in range(2)]
        hm = [view(R3, (2 + u) * KU * P, UP) for u in range(2)]
        ht = [view(R3, (4 + u) * KU * P, KU, P) for u in range(2)]
        yd = [view(R2, u * 8 * D, 8, D) for u in range(2)]
        Y1 = [view(R2, WK * (1 - h), NH, D) for h in range(HALVES)]
        d3_x, d3_t = sem("d3_x"), sem("d3_t")
        out_sem = sem("out_sem")

        GH = NH // MC
        lstm_steps = []
        for p, nb in ((1, 2), (2, 4), (3, 4), (4, 8)):
            for b0 in range(0, GH, 2 * nb):
                for t in range(p):
                    for s in range(2):
                        lstm_steps.append((p, t, s, b0 + s * nb, nb))
        NL = len(lstm_steps)
        assert GH % 16 == 0 and all(nb * (N // p) <= BANK for p, t, s, b0, nb in lstm_steps)

        def gates_of(t):
            return (0, 2, 1, 3) if t > 0 else (0, 2, 3)

        gates_before, sums_before = [0], [0]
        for step in lstm_steps:
            gates_before.append(gates_before[-1] + len(gates_of(step[1])))
            sums_before.append(sums_before[-1] + (step[1] > 0))

        def inputs_done(n):
            p, t, s, b0, nb = lstm_steps[n]
            done = [m + 1 for m in range(n) if lstm_steps[m][0] == p - 1 and lstm_steps[m][1] == p - 2
                    and lstm_steps[m][3] < b0 + nb and b0 < lstm_steps[m][3] + lstm_steps[m][4]]
            return max(done) if done else 0

        def sweep(eng, first, end, body, ahead=2, more=False, behind=1):
            for g in range(first, first + ahead):
                body(g, g // 2, g % 2, g == first, False)
            mid = first + ahead
            n = (end - behind - mid) // 2
            if n > 0:
                with eng.Fori(0, n) as h:
                    for j in range(2):
                        body(2 * h + (mid + j), h + (mid + j) // 2, (mid + j) % 2, False, False)
            for g in range(mid + 2 * n, end):
                body(g, g // 2, g % 2, False, g == end - 1 and not more)

        def run_pairs(eng, first, end, body):
            at = first
            if at % 2:
                body(at, at // 2, 1)
                at += 1
            n = (end - at) // 2
            with eng.Fori(0, n) as h:
                for j in range(2):
                    body(2 * h + (at + j), h + at // 2, j)
            if (end - at) % 2:
                body(end - 1, (end - 1) // 2, 0)

        def wait_from(eng, semaphore, value):
            if not (isinstance(value, int) and value == 0):
                eng.wait_ge(semaphore, value)

        def turns(eng, half, body):
            straight = 1 if half == 0 else 0
            if straight:
                body(0, 0)
            with eng.Fori(0, NGH // 2 - straight) as h:
                h0 = h + straight
                body(2 * h + (2 * straight + half * NGH), h0)

        def known_below(g, n):
            return isinstance(g, int) and g < n

        NGH = NG // HALVES
        B2H = NB2 // HALVES
        D2H = ND2 // HALVES
        ZEROS = 16 * HALVES * (NSLOT1 * D // ZW)

        @block.sync
        def _(sp):
            for g in range(NX):
                sp.dma_start(X[:, 8 * g:8 * g + 8, :],
                             x.rearrange("(t p) d -> p t d", p=P)[:, 8 * g:8 * g + 8, :]).then_inc(x_in[g], 16)
                if g == 0:
                    for dst, src in loads_a:
                        sp.dma_start(dst, src).then_inc(wa_in, 16)
            for dst, src in loads_w:
                sp.dma_start(dst, src).then_inc(w_in, 16)
            sp.wait_ge(zero_ready, 1)
            for rows in sorted_in:
                zv = rows.rearrange("(p n) d -> p (n d)", p=P)
                for i in range(NSLOT1 * D // ZW):
                    sp.dma_start(zv[:, i * ZW:(i + 1) * ZW], zero).then_inc(zeroed, 16)

            def rows_of(rows, g, n):
                return rows[bass.ds(g * (n * P), n * P), :].rearrange("(t p) d -> p t d", p=P)

            def b2_store(g, k, u):
                half = b2_half[1]
                sp.wait_ge(b2_yo, g + 1)
                sp.dma_start(rows_of(sorted_out[half], g - half * B2H, 4), yb[u]).then_inc(b2_out[u], 16)

            def b2_load(g, u):
                half = b2_half[0]
                if not known_below(g, 2):
                    sp.wait_ge(b2_tr, g - 1)
                sp.dma_start(xs[u][:, 0:4, :], rows_of(sorted_in[half], g - half * B2H, 4)).then_inc(b2_in[u], 16)

            b2_half = [0, 0]

            def b2_both(g, k, u):
                b2_load(g, u)
                b2_store(g - 2, k - 1, u)

            sp.wait_ge(s_scat[0][0], 16 * NH)
            b2_load(0, 0)
            b2_load(1, 1)
            for half in range(HALVES):
                first = half * B2H
                if half > 0:
                    sp.wait_ge(s_scat[0][half], 16 * NH)
                    b2_half[0] = half
                    for g in range(first, first + 2):
                        b2_both(g, g // 2, g % 2)
                b2_half[1] = half
                run_pairs(sp, first + 2, first + B2H, b2_both)
            for g in range(NB2 - 2, NB2):
                b2_store(g, g // 2, g % 2)

            sp.wait_ge(b2_y, NB2)
            sp.wait_ge(b2_yo, NB2)
            sp.dma_start(up_sb, up_t.rearrange("e p n -> p e n")).then_inc(up_in, 16)
            dv = down_sb.rearrange("p (e k d) -> p e k d", k=KU, d=D)
            for k in range(KU):
                kk = min(P, UP - k * P)
                sp.dma_start(dv[0:kk, :, k, :],
                             down_t[:, k * P:k * P + kk, :].rearrange("e p d -> p e d")).then_inc(up_in, 16)

            d2_half = [0, 0]

            def d2_load(g, u):
                if not known_below(g, 2):
                    sp.wait_ge(d2_tr, g - 1)
                sp.dma_start(xs[u][:, :, :], rows_of(sorted_in[d2_half[0]], g - d2_half[0] * D2H, 8)).then_inc(d2_in[u], 16)

            def d2_store(g, u):
                half = d2_half[1]
                sp.wait_ge(d2_yo, 8 * g + 8)
                sp.dma_start(rows_of(sorted_out[half], g - half * D2H, 8), yd[u]).then_inc(d2_out[u], 16)

            def d2_both(g, k, u):
                d2_load(g, u)
                d2_store(g - 2, u)

            sp.wait_ge(s_scat[1][0], 32 * NH)
            d2_load(0, 0)
            d2_load(1, 1)
            for half in range(HALVES):
                first = half * D2H
                if half > 0:
                    sp.wait_ge(s_scat[1][half], 32 * NH)
                    d2_half[0] = half
                    for g in range(first, first + 2):
                        d2_both(g, g // 2, g % 2)
                d2_half[1] = half
                run_pairs(sp, first + 2, first + D2H, d2_both)
            for g in range(ND2 - 2, ND2):
                d2_store(g, g % 2)
            for g in range(NX):
                sp.wait_ge(d3_x, 16 * (g + 1))
                sp.dma_start(out.rearrange("(t p) d -> p t d", p=P)[:, 8 * g:8 * g + 8, :],
                             X[:, 8 * g:8 * g + 8, :]).then_inc(out_sem, 16)
            sp.wait_ge(out_sem, 16 * NX)

        @block.gpsimd
        def _(pool):
            def step(ins):
                ins.then_inc(pool_step, 1)
                n_pool[0] += 1
                pool.wait_ge(pool_step, n_pool[0])

            pool.memset(zero, 0.0).then_inc(zero_ready, 1)
            step(pool.memset(ident[:, :], 0.0))
            step(pool.affine_select(out=ident[:, :], in_=ident[:, :], compare_op=ALU.not_equal, fill=1.0, base=0,
                                    pattern=[[-1, P]], channel_multiplier=1))
            pool.memset(ones_row[:, :], 1.0)
            step(pool.memset(ones[:, :], 1.0))
            step(pool.affine_select(out=before[:, :], in_=ones[:, :], compare_op=ALU.is_gt, fill=0.0, base=0,
                                    pattern=[[1, P]], channel_multiplier=-1))
            pool.iota(iota_e[:, :], [[1, E]], base=0, channel_multiplier=0, allow_small_or_imprecise_dtypes=True)
            pool.iota(iota_t[:, :], [[P, NH]], base=0, channel_multiplier=0, allow_small_or_imprecise_dtypes=True)
            pool.iota(iota_s[:, :], [[1, NSLOT1]], base=0, channel_multiplier=0,
                      allow_small_or_imprecise_dtypes=True).then_inc(const_ready, 1)

            pool.wait_ge(wa_in, WA_ALL)
            p0 = n_pool[0]

            def a_pool(g, k, u):
                pool.wait_ge(a_s, g + 1)
                if not known_below(g, 2):
                    pool.wait_ge(a_t1, g - 1)
                pool.tensor_tensor(
                    q1[u].rearrange("p (b c) d -> p b c d", c=MC), bcast(bias_sb[:, :, 0, :], 1, 8 // MC),
                    bcast(sg[u][:, :, 0].rearrange("p (b c) -> p b c", c=MC), 3, D), ALU.mult).then_inc(pool_step, 1)
                pool.wait_ge(pool_step, p0 + 2 * g + 1)
                pool.wait_ge(a_c2, g + 1)
                pool.tensor_tensor(q1[u], q1[u], q2[u], ALU.add).then_inc(pool_step, 1)
                pool.wait_ge(pool_step, p0 + 2 * g + 2)
                pool.wait_ge(a_c3, g + 1)
                pool.tensor_tensor(q1[u], q1[u], q3[u], ALU.add).then_inc(a_q, 1)

            a_pool(0, 0, 0)
            a_pool(1, 0, 1)
            run_pairs(pool, 2, NA, a_pool)
            n_pool[0] += 2 * NA

            def scatter(layer, half, r, K):
                pool.wait_ge(r.tiles, half + 1)
                if layer == 0 and half == 0:
                    pool.wait_ge(zeroed, ZEROS)
                for t in range(half * NH, (half + 1) * NH):
                    for k in range(K):
                        pool.indirect_dma_start(
                            out=sorted_in[half], out_offset=bass.IndirectOffsetOnAxis(ap=dest_i[:, k, t:t + 1], axis=0),
                            in_=XN[:, t, :], in_offset=None).then_inc(s_scat[layer][half], 16)

            def gather(layer, half, outs, groups, nslot, K):
                done = (half + 1) * groups
                pool.wait_ge(outs[0], 16 * (done - done // 2))
                pool.wait_ge(outs[1], 16 * (done // 2))
                pool.wait_ge(s_scat[layer][half], 16 * K * NH)
                for t in range(half * NH, (half + 1) * NH):
                    for k in range(K):
                        dst = XN[:, t, :] if k == 0 else Y1[half][:, t - half * NH, :]
                        pool.indirect_dma_start(
                            out=dst, out_offset=None, in_=sorted_out[half][0:nslot * P, :],
                            in_offset=bass.IndirectOffsetOnAxis(ap=dest_i[:, k, t:t + 1], axis=0)).then_inc(
                                s_gath[layer][t // 8], 16)

            for half in range(HALVES):
                scatter(0, half, rb, 1)
            for half in range(HALVES):
                gather(0, half, b2_out, B2H, NSLOT0, 1)
            for half in range(HALVES):
                scatter(1, half, rd, 2)
            for half in range(HALVES):
                gather(1, half, d2_out, D2H, NSLOT1, 2)

        @block.scalar
        def _(act):
            act.wait_ge(wa_in, WA_ALL)

            def a_act(g, k, u):
                act.wait_ge(a_tr, g + 1)
                if not known_below(g, 2):
                    act.wait_ge(a_z, g - 1)
                for h in range(2):
                    ins = act.activation(xt[u][:, h * BANK:(h + 1) * BANK], bank[h][:, :], ACT.Copy)
                ins.then_inc(a_xt, 1)
                act.wait_ge(a_zb, g + 1)
                act.activation(th[u], zb[u], ACT.Tanh, scale=0.5).then_inc(a_th, 1)
                act.wait_ge(a_s, g + 1)
                if not known_below(g, 2):
                    act.wait_ge(a_q, g - 1)
                for j in range(8):
                    ins = act.activation(q2[u][:, j, :], bias_sb[:, j % MC, 1, :], ACT.Copy, scale=sg[u][:, j, 1:2])
                ins.then_inc(a_c2, 1)
                for j in range(8):
                    ins = act.activation(q3[u][:, j, :], xn[u][:, j, :], ACT.Copy, scale=sg[u][:, j, 2:3])
                ins.then_inc(a_c3, 1)

            a_act(0, 0, 0)
            a_act(1, 0, 1)
            run_pairs(act, 2, NA, a_act)
            act.wait_ge(w_in, W_ALL)

            def hidden_body(r, routed):
                def body(g, k, u, first, last):
                    for c in range(KH):
                        act.wait_ge(r.h, KH * g + c + 1)
                        if c == 0 and not known_below(g, 2):
                            act.wait_ge(r.lg, g - 1)
                        act.activation(Ht[u][:, c, :], bank[2 + c][:, :], ACT.Gelu, bias=b1_sb[:, c:c + 1]).then_inc(r.act, 1)
                    if first and routed >= 0:
                        route_act(0, rb, routed)
                    if not last:
                        copy_xt(r, g + 1, 1 - u)
                    elif r is rb:
                        copy_xt(r2, 0, 0)
                return body

            def copy_xt(r, g, u):
                act.wait_ge(r.tr, g + 1)
                act.activation(xt[u][:, 0:BANK], bank[u][:, :], ACT.Copy).then_inc(r.xt, 1)

            def route_act(layer, r, half):
                w = space[layer, half]
                act.wait_ge(r.ranks, half + 1)
                act.activation(flat(w.rank), bank[1][:, 0:EH], ACT.Copy)
                act.activation(flat(w.tot), bank[1][:, EH:2 * EH], ACT.Copy).then_inc(r.ranks_sb, 1)
                act.wait_ge(r.flat, 2 * half + 1)
                act.activation(w.w1, w.w2, ACT.Exp).then_inc(r.flat, 1)

            copy_xt(rb, 0, 0)
            for half in range(HALVES):
                sweep(act, half * NGH, (half + 1) * NGH, hidden_body(rb, half - 1), more=half < HALVES - 1)
            sweep(act, 0, NB2, hidden_body(r2, HALVES - 1))

            for half in range(HALVES):
                act.wait_ge(b3_x, (half + 1) * NH)

                def g_act(g0, h0):
                    for u in range(2):
                        act.wait_ge(c1_ax, g0 + u + 1)
                        act.activation(axt[u], bank[4 * u][:, :], ACT.Copy).then_inc(c1_axc, 1)
                    for u in range(2):
                        act.wait_ge(c1_hb, g0 + u + 1)
                        act.activation(h1[u], hb[u], ACT.Relu).then_inc(c1_hr, 1)
                    for u in range(2):
                        act.wait_ge(c1_g, g0 + u + 1)
                        act.activation(F[:, bass.ds((2 * h0 + u) * BANK, BANK)], bank[4 * u + 3][:, :], ACT.Relu).then_inc(c1_f, 1)

                turns(act, half, g_act)

                funcs = (ACT.Sigmoid, ACT.Sigmoid, ACT.Tanh, ACT.Sigmoid)
                for n, (p, t, s, b0, nb) in enumerate(lstm_steps):
                    c = nb * (N // p)
                    steps0, gates0 = half * NL, half * gates_before[NL]
                    if n >= 2:
                        act.wait_ge(l_h, steps0 + n - 1)
                    for i, k in enumerate(gates_of(t)):
                        act.wait_ge(l_g, gates0 + gates_before[n] + i + 1)
                        act.activation(gb[s][k][:, 0:c], bank[4 * s + k][:, 0:c], funcs[k],
                                       bias=lb_sb[:, (p - 1) * GATES + k:(p - 1) * GATES + k + 1]).then_inc(l_act, 1)
                    act.wait_ge(l_c, steps0 + n + 1)
                    act.activation(tcs[s][:, 0:c], cst[s][:, 0:c], ACT.Tanh).then_inc(l_tc, 1)

                act.wait_ge(l_h, (half + 1) * NL)
                def turn(g0, h0):
                    for u in range(2):
                        wait_from(act, t_tr, g0)
                        act.activation(xt[u][:, 0:BANK], F[:, bass.ds((2 * h0 + u) * BANK, BANK)], ACT.Copy).then_inc(t_st, 1)

                turns(act, half, turn)

                act.wait_ge(t_x, (half + 1) * NGH)
                def turn(g0, h0):
                    for u in range(2):
                        act.wait_ge(rd.tr, g0 + u + 1)
                        wait_from(act, rd.lg, g0)
                        act.activation(xt[u][:, 0:BANK], bank[u][:, :], ACT.Copy).then_inc(rd.xt, 1)

                turns(act, half, turn)
                route_act(1, rd, half)

            def d2_rows(g, u):
                act.wait_ge(d2_tr, g + 1)
                if not known_below(g, 2):
                    act.wait_ge(d2_h, 8 * (g - 1))
                for h in range(2):
                    ins = act.activation(xt[u][:, h * BANK:(h + 1) * BANK], bank[h][:, :], ACT.Copy)
                ins.then_inc(d2_xt, 1)

            def d2_hidden_columns(i, j, straight):
                act.wait_ge(d2_tt, i + 1)
                if not straight:
                    act.wait_ge(d2_y, i - 1)
                kf = UP // P
                dst = ht[j % 2]
                act.activation(dst[:, 0:kf, :], bank[6][:, 0:kf * P].rearrange("p (k n) -> p k n", n=P), ACT.Copy)
                act.activation(dst[0:UP - kf * P, kf, :], bank[6][0:UP - kf * P, kf * P:(kf + 1) * P],
                               ACT.Copy).then_inc(d2_tc, 1)

            def d2_act(g, k, u, first, last):
                for j in range(8):
                    i = 8 * g + j
                    act.wait_ge(d2_h, i + 1)
                    if not (first and j < 2):
                        act.wait_ge(d2_m, i - 1)
                    act.activation(sl[j % 2], bank[2 + 2 * (j % 2)][:, 0:UP], ACT.Silu).then_inc(d2_silu, 1)
                    if not (first and j < 1):
                        d2_hidden_columns(i - 1, j - 1, first and j < 3)
                    if j == 5 and not last:
                        d2_rows(g + 1, 1 - u)
                if last:
                    d2_hidden_columns(8 * g + 7, 7, False)

            d2_rows(0, 0)
            sweep(act, 0, ND2, d2_act)

        @block.tensor
        def _(pe):
            tile_list = tile_e[:, :, :].rearrange("a h s -> a (h s)")

            def load_experts(first, n):
                _, r = nc.values_load_multi_w_load_instructions(
                    tile_list[0:1, bass.ds(first, n)], engines=[PE_ENGINE], min_val=0, max_val=E - 1,
                    skip_runtime_bounds_check_because="clamped to the last expert where it is computed")
                return r

            pe.wait_ge(const_ready, 1)
            pe.wait_ge(wa_in, WA_ALL)
            for m in range(MC):
                mm = pe.matmul(bank[3][:, 0:N], ones[:, :], adj_sb[:, m, :], start=(m == 0), stop=(m == MC - 1))
            mm.then_inc(row_sums, 1)

            def a_pe(g, k, u):
                pe.wait_ge(a_xn, g + 1)
                if not known_below(g, 1):
                    pe.wait_ge(a_xt, g)
                for j in range(8):
                    tr = pe.transpose(bank[j // 4][:, (j % 4) * P:(j % 4 + 1) * P], xn[u][:, j, :], ident[:, :])
                tr.then_inc(a_tr, 1)
                xv = xn[u][:, :, :].rearrange("p (b c) d -> p b c d", c=MC)
                if not known_below(g, 2):
                    pe.wait_ge(a_mul, g - 1)
                for nch in range(MC):
                    for m in range(MC):
                        mm = pe.matmul(bank[4 + 2 * u + nch][:, :].rearrange("p (b d) -> p b d", d=D),
                                       adj_sb[:, m, nch * P:(nch + 1) * P], xv[:, :, m, :],
                                       start=(m == 0), stop=(m == MC - 1))
                mm.then_inc(a_ax, 1)
                pe.wait_ge(a_xt, g + 1)
                if not known_below(g, 1):
                    pe.wait_ge(a_zb, g)
                for j in range(8):
                    mm = pe.matmul(bank[2][:, 3 * j:3 * j + 3], xt[u][:, j * P:(j + 1) * P], gw_sb[:, :],
                                   start=True, stop=True)
                mm.then_inc(a_z, 1)

            a_pe(0, 0, 0)
            a_pe(1, 0, 1)
            run_pairs(pe, 2, NA, a_pe)

            def transposes4(g, u, r, rows, ready):
                pe.wait_ge(*ready)
                if not known_below(g, 2):
                    pe.wait_ge(r.xt, g - 1)
                for j in range(4):
                    tr = pe.transpose(bank[u][:, j * P:(j + 1) * P], rows[u][:, j, :], ident[:, :])
                tr.then_inc(r.tr, 1)

            def hidden(r, g, u):
                pe.wait_ge(r.xt, g + 1)
                for c in range(KH):
                    if not known_below(g, 1):
                        pe.wait_ge(r.act, KH * (g - 1) + c + 1)
                    pe.matmul(bank[2 + c][:, :], w1_sb[:, c * P:(c + 1) * P], xt[u][:, 0:BANK],
                              start=True, stop=True).then_inc(r.h, 1)

            def rank(layer, r, half):
                m = flat(space[layer, half].mask)
                pe.wait_ge(r.mask, half + 1)
                pe.matmul(bank[1][:, 0:EH], before[:, :], m, start=True, stop=True)
                pe.matmul(bank[1][:, EH:2 * EH], ones[:, :], m, start=True, stop=True).then_inc(r.ranks, 1)

            def b1_pe(g, k, u, first, last):
                hidden(rb, g, u)
                if first and not known_below(g, 1):
                    rank(0, rb, 0)
                    pe.wait_ge(rb.ranks_sb, 1)
                if not last:
                    transposes4(g + 1, 1 - u, rb, xn, (rb.xn, g + 2))
                else:
                    transposes4(0, 0, r2, xs, (b2_in[0], 16))
                if not known_below(g, 2):
                    pe.wait_ge(rb.st, g - 1)
                for c in range(KH):
                    pe.wait_ge(rb.act, KH * g + c + 1)
                    for j in range(4):
                        mm = pe.matmul(bank[6 + u][:, j * E:(j + 1) * E], Ht[u][:, c, j * P:(j + 1) * P], wg_sb[:, c, :],
                                       start=(c == 0 and j == 0), stop=(c == KH - 1), skip_group_check=True)
                mm.then_inc(rb.lg, 1)

            pe.wait_ge(a_x, NA)
            pe.wait_ge(w_in, W_ALL)
            transposes4(0, 0, rb, xn, (rb.xn, 1))
            for half in range(HALVES):
                sweep(pe, half * NGH, (half + 1) * NGH, b1_pe, more=half < HALVES - 1)

            def b2_pe(g, k, u, first, last):
                hidden(r2, g, u)
                if first:
                    rank(0, rb, HALVES - 1)
                    pe.wait_ge(rb.ranks_sb, HALVES)
                    pe.wait_ge(rb.tiles, 1)
                if not last:
                    transposes4(g + 1, 1 - u, r2, xs, (b2_in[1 - u], 16 * (k + (1 if u == 0 else 2))))
                er = load_experts(4 * g, 4)
                if not known_below(g, 2):
                    pe.wait_ge(b2_yo, g - 1)
                for c in range(KH):
                    pe.wait_ge(b2_act, KH * g + c + 1)
                    for j in range(4):
                        mm = pe.matmul(bank[6 + u][:, j * P:(j + 1) * P], Ht[u][:, c, j * P:(j + 1) * P],
                                       wd_sb[:, c, bass.ds(er[j] * D, D)],
                                       start=(c == 0 and j == 0), stop=(c == KH - 1), skip_group_check=True)
                mm.then_inc(b2_y, 1)

            sweep(pe, 0, NB2, b2_pe)

            for half in range(HALVES):
                if half == 0:
                    pe.wait_ge(b2_yo, NB2)
                def turn(g0, h0):
                    for u in range(2):
                        pe.wait_ge(c1_xn, g0 + u + 1)
                        for b in range(2):
                            for m in range(MC):
                                mm = pe.matmul(bank[4 * u][:, b * N:(b + 1) * N], xn[u][:, MC * b + m, :], adj_sb[:, m, :],
                                               start=(m == 0), stop=(m == MC - 1))
                        mm.then_inc(c1_ax, 1)
                    for u in range(2):
                        pe.wait_ge(c1_axc, g0 + u + 1)
                        pe.matmul(bank[4 * u + 1][:, :], g0_sb[:, :], axt[u], start=True, stop=True).then_inc(c1_h, 1)
                    for u in range(2):
                        pe.wait_ge(c1_hr, g0 + u + 1)
                        for j in range(4):
                            mm = pe.matmul(bank[4 * u + 2][:, j * P:(j + 1) * P], h1[u][:, j * P:(j + 1) * P], g1_sb[:, :],
                                           start=True, stop=True)
                        mm.then_inc(c1_z, 1)
                    for u in range(2):
                        pe.wait_ge(c1_zc, g0 + u + 1)
                        wait_from(pe, c1_f, g0)
                        for b in range(2):
                            for m in range(MC):
                                mm = pe.matmul(bank[4 * u + 3][:, b * N:(b + 1) * N], zs[u][:, MC * b + m, :], adj_sb[:, m, :],
                                               start=(m == 0), stop=(m == MC - 1))
                        mm.then_inc(c1_g, 1)

                turns(pe, half, turn)

                pe.wait_ge(c1_f, (half + 1) * NGH)
                pe.wait_ge(c1_zc, (half + 1) * NGH)
                for n, (p, t, s, b0, nb) in enumerate(lstm_steps):
                    nw = N // p
                    c = nb * nw
                    steps0, gates0 = half * NL, half * gates_before[NL]
                    xin = F[:, b0 * N:(b0 + nb) * N].rearrange("p (b n) -> p b n", n=N)[:, :, t:t + (nw - 1) * p + 1:p]
                    if n >= 2:
                        pe.wait_ge(l_act, gates0 + gates_before[n - 1])
                    if t == 0 and inputs_done(n) > 0:
                        pe.wait_ge(l_h, steps0 + inputs_done(n))
                    for k in gates_of(t):
                        mm = pe.matmul(bank[4 * s + k][:, 0:c].rearrange("p (b n) -> p b n", n=nw),
                                       wih_sb[:, p - 1, k * P:(k + 1) * P], xin, start=True, stop=(t == 0))
                        if t == 0:
                            mm.then_inc(l_g, 1)
                    if t > 0:
                        pe.wait_ge(l_h, steps0 + n - 1)
                        for k in gates_of(t):
                            pe.matmul(bank[4 * s + k][:, 0:c], whh_sb[:, p - 1, k * P:(k + 1) * P],
                                      hst[s][:, 0:c], start=False, stop=True).then_inc(l_g, 1)

                def turn(g0, h0):
                    for u in range(2):
                        pe.wait_ge(t_st, g0 + u + 1)
                        wait_from(pe, t_x, g0)
                        for j in range(4):
                            tr = pe.transpose(bank[u][:, j * P:(j + 1) * P], xt[u][:, j * P:(j + 1) * P], ident[:, :])
                        tr.then_inc(t_tr, 1)

                turns(pe, half, turn)
                pe.wait_ge(t_x, (half + 1) * NGH)
                def turn(g0, h0):
                    for u in range(2):
                        g = g0 + u
                        pe.wait_ge(rd.xn, g + 1)
                        wait_from(pe, rd.xt, g0)
                        for j in range(4):
                            tr = pe.transpose(bank[u][:, j * P:(j + 1) * P], xn[u][:, j, :], ident[:, :])
                        tr.then_inc(rd.tr, 1)
                    for u in range(2):
                        g = g0 + u
                        pe.wait_ge(rd.xt, g + 1)
                        wait_from(pe, rd.st, g0)
                        for j in range(4):
                            mm = pe.matmul(bank[6 + u][:, j * E:(j + 1) * E], xt[u][:, j * P:(j + 1) * P], rt_sb[:, :],
                                           start=True, stop=True)
                        mm.then_inc(rd.lg, 1)

                turns(pe, half, turn)
                rank(1, rd, half)
                pe.wait_ge(rd.ranks_sb, half + 1)

            def d2_transposes(g, u, n_in):
                pe.wait_ge(d2_in[u], 16 * n_in)
                if not known_below(g, 1):
                    pe.wait_ge(d2_xt, g)
                for j in range(8):
                    tr = pe.transpose(bank[j // 4][:, (j % 4) * P:(j % 4 + 1) * P], xs[u][:, j, :], ident[:, :])
                tr.then_inc(d2_tr, 1)

            def d2_transpose_hidden(i, j, straight):
                pe.wait_ge(d2_m, i + 1)
                if not straight:
                    pe.wait_ge(d2_tc, i)
                for c in range(KU):
                    kk = min(P, UP - c * P)
                    mm = pe.transpose(bank[6][0:kk, c * P:(c + 1) * P], hm[j % 2][:, c * P:c * P + kk], ident[:, :])
                mm.then_inc(d2_tt, 1)

            def d2_down(i, j, expert):
                pe.wait_ge(d2_tc, i + 1)
                pe.wait_ge(d2_yo, i)
                for c in range(KU):
                    kk = min(P, UP - c * P)
                    mm = pe.matmul(bank[7][:, (j % 4) * P:(j % 4 + 1) * P], ht[j % 2][0:kk, c, :],
                                   down_sb[0:kk, bass.ds(expert * (KU * D) + c * D, D)],
                                   start=(c == 0), stop=(c == KU - 1))
                mm.then_inc(d2_y, 1)

            def d2_pe(g, k, u, first, last):
                back = 0 if first else 2
                er = load_experts(8 * g - back, 8 + back)
                pe.wait_ge(d2_xt, g + 1)
                for j in range(8):
                    i = 8 * g + j
                    if not (first and j < 2):
                        pe.wait_ge(d2_m, i - 1)
                    for part in range(2):
                        mm = pe.matmul(bank[2 + 2 * (j % 2) + part][:, 0:UP], xt[u][:, j * P:(j + 1) * P],
                                       up_sb[:, bass.ds(er[j + back] * (2 * UP) + part * UP, UP)], start=True, stop=True)
                    mm.then_inc(d2_h, 1)
                    if j == 5 and not last:
                        d2_transposes(g + 1, 1 - u, k + (1 if u == 0 else 2))
                    if not (first and j < 1):
                        d2_transpose_hidden(i - 1, j - 1, first and j == 1)
                    if not (first and j < 2):
                        d2_down(i - 2, j - 2, er[j + back - 2])
                if last:
                    d2_transpose_hidden(8 * g + 7, 7, False)
                    for j in (6, 7):
                        d2_down(8 * g + j, j, er[j + back])

            pe.wait_ge(rd.tiles, 1)
            pe.wait_ge(up_in, 16 * (1 + KU))
            d2_transposes(0, 0, 1)
            sweep(pe, 0, ND2, d2_pe)

        @block.vector
        def _(dve):
            def L(ins):
                link(dve, ins)

            def ln_finish(lo, hi):
                me, ve, mo, vo = (ST[:, lo:hi, i] for i in (1, 2, 4, 5))
                s, d, v, t = (ln_t[:, i, 0:hi - lo] for i in range(4))
                L(dve.tensor_tensor(s, me, mo, ALU.add))
                L(dve.tensor_tensor(d, me, mo, ALU.subtract))
                L(dve.tensor_tensor(v, ve, vo, ALU.add))
                L(dve.tensor_scalar(MEAN[:, lo:hi], s, 0.5, None, ALU.mult))
                L(dve.tensor_scalar(v, v, 1.0 / D, LN_EPS, ALU.mult, ALU.add))
                L(dve.tensor_tensor(d, d, d, ALU.mult))
                L(dve.scalar_tensor_tensor(v, d, 0.25, v, ALU.mult, ALU.add))
                bits, guess = (ln_i[:, i, 0:hi - lo] for i in range(2))
                L(dve.tensor_scalar(bits, v.bitcast(I32), 1, None, ALU.arith_shift_right))
                L(dve.tensor_scalar(guess, bits, -1.0, float(RSQRT_MAGIC), ALU.mult, ALU.add))
                y = guess.bitcast(F32)
                for i in range(3):
                    L(dve.tensor_tensor(t, y, y, ALU.mult))
                    L(dve.scalar_tensor_tensor(t, t, -0.5, v, ALU.mult, ALU.mult))
                    L(dve.scalar_tensor_tensor(RSTD[:, lo:hi], t, 1.5, y, ALU.add, ALU.mult))
                    y = RSTD[:, lo:hi]

            def normalise(g, n, dst, done, step_sem, count):
                dve.tensor_tensor(dst, X[:, bass.ds(g * n, n), :], bcast(MEAN[:, bass.ds(g * n, n)], 2, D),
                                  ALU.subtract).then_inc(step_sem, 1)
                dve.wait_ge(step_sem, count + 1)
                dve.tensor_tensor(dst, dst, bcast(RSTD[:, bass.ds(g * n, n)], 2, D), ALU.mult).then_inc(done, 1)

            dve.wait_ge(const_ready, 1)
            for g in range(NX):
                dve.wait_ge(x_in[g], 16)
                for t in range(8 * g, 8 * g + 8):
                    dve.bn_stats(ST[:, t, :], X[:, t, :]).then_inc(a_st, 1)
            dve.wait_ge(a_st, NTILE)
            ln_finish(0, NTILE)
            dve.wait_ge(wa_in, WA_ALL)
            normalise(0, 8, xn[0][:, :, :], a_xn, a_ns, 0)

            def a_gate(g, u):
                dve.wait_ge(a_z, g + 1)
                dve.tensor_tensor(zb[u].rearrange("p (b c) k -> p b c k", c=MC),
                                  bank[2][:, 0:24].rearrange("p (b c k) -> p b c k", c=MC, k=3),
                                  bcast(gb_sb[:, :, :], 1, 4), ALU.add).then_inc(a_zb, 1)
                dve.wait_ge(a_th, g + 1)
                dve.tensor_scalar(sg[u], th[u], 0.5, 0.5, ALU.mult, ALU.add).then_inc(a_s, 1)
                dve.wait_ge(a_s, g + 1)
                dve.tensor_tensor(us[u], sg[u][:, :, 0], sg[u][:, :, 1], ALU.add).then_inc(a_us, 1)

            def a_finish(g, u):
                dve.wait_ge(a_ax, g + 1)
                dve.wait_ge(a_us, g + 1)
                uv = us[u].rearrange("p (b c) -> p b c", c=MC)
                tv = t1.rearrange("p (b c) d -> p b c d", c=MC)
                for c in range(MC):
                    ins = dve.tensor_tensor(tv[:, :, c, :], bank[4 + 2 * u + c][:, :].rearrange("p (b d) -> p b d", d=D),
                                            bcast(uv[:, :, c], 2, D), ALU.mult)
                ins.then_inc(a_mul, 1)
                dve.wait_ge(a_mul, g + 1)
                dve.wait_ge(a_q, g + 1)
                dve.tensor_tensor(t1, t1, q1[u], ALU.add).then_inc(a_t1, 1)
                dve.wait_ge(a_t1, g + 1)
                xv = X[:, bass.ds(8 * g, 8), :]
                dve.scalar_tensor_tensor(xv, t1, 0.0, xv, ALU.max, ALU.add).then_inc(a_x, 1)
                dve.wait_ge(a_x, g + 1)
                for j in range(8):
                    ins = dve.bn_stats(ST[:, bass.ds(8 * g + j, 1), :].rearrange("p a k -> p (a k)"),
                                       X[:, bass.ds(8 * g + j, 1), :].rearrange("p a k -> p (a k)"))
                ins.then_inc(a_st2, 1)

            def a_dve(g, k, u, first, last):
                if not last:
                    if not known_below(g, 1):
                        dve.wait_ge(a_z, g)
                        dve.wait_ge(a_c3, g)
                    normalise(g + 1, 8, xn[1 - u][:, :, :], a_xn, a_ns, g + 1)
                a_gate(g, u)
                if not first:
                    a_finish(g - 1, 1 - u)

            a_dve(0, 0, 0, True, False)
            sweep(dve, 1, NA, lambda g, k, u, first, last: a_dve(g, k, u, False, last))
            a_finish(NA - 1, (NA - 1) % 2)
            dve.wait_ge(w_in, W_ALL)
            dve.wait_ge(row_sums, 1)
            L(dve.tensor_scalar(bga_sb[:, :], bank[3][:, 0:N], g0b_sb[:, 0:1], None, ALU.mult))
            L(dve.tensor_tensor(lb_sb[:, :], bih_sb[:, :], bhh_sb[:, :], ALU.add))
            dve.wait_ge(a_st2, NA)

            def norm_rows(r, g, u, ns):
                normalise(g, 4, xn[u][:, 0:4, :], r.xn, ns, 2 * g)
                dve.wait_ge(r.xn, g + 1)
                dve.tensor_copy(XN[:, bass.ds(4 * g, 4), :], xn[u][:, 0:4, :]).then_inc(ns, 1)

            def choose(r, g, u, bias, cs):
                dve.wait_ge(r.lg, g + 1)
                src = bank[6 + u][:, 0:4 * E].rearrange("p (j e) -> p j e", e=E)
                if bias is not None:
                    dve.tensor_tensor(lg_st[u][:, :, :], src, bcast(bias, 1, 4), ALU.add).then_inc(r.st, 1)
                else:
                    dve.tensor_copy(lg_st[u][:, :, :], src).then_inc(r.st, 1)
                dve.wait_ge(r.st, g + 1)
                dve.tensor_copy(wait_c[u][:, 0:1], lg_st[u][:, 0, 0:1])
                for j in range(4):
                    dve.max(mx_st[u][:, j, :], lg_st[u][:, j, :]).then_inc(r.mx, 1)
                dve.wait_ge(r.mx, 4 * g + 4)
                dve.tensor_copy(wait_c[u][:, 1:2], mx_st[u][:, 0, 0:1])
                for j in range(4):
                    dve.max_index(ix_st[u][:, j, :], mx_st[u][:, j, :], lg_st[u][:, j, :]).then_inc(r.copied, 1)
                dve.tensor_copy(MX[:, bass.ds(4 * g, 4), :], mx_st[u][:, :, :]).then_inc(cs, 1)
                dve.wait_ge(r.copied, 4 * g + 4)
                dve.tensor_copy(IX[:, bass.ds(4 * g, 4), :], ix_st[u][:, :, :]).then_inc(r.ix, 1)

            def route(r, half, bias, ns, cs, before_it, rows_from, rows_end):
                g0 = half * NGH
                for g in range(rows_from, g0 + 2):
                    norm_rows(r, g, g % 2, ns)

                def body(g, k, u, first, last):
                    if not last:
                        dve.wait_ge(r.tr, g + 1)
                        dve.wait_ge(ns, 2 * g + 2)
                        norm_rows(r, g + 2, u, ns)
                    choose(r, g, u, bias, cs)
                    if before_it is not None and known_below(g, g0 + 2):
                        before_it.part(2 * (g - g0))
                        before_it.part(2 * (g - g0) + 1)

                ahead = 2
                more = rows_end - 2 - g0
                if more < NGH:
                    sweep(dve, g0, g0 + more, body, ahead, more=True)
                    for g in range(g0 + more, g0 + NGH):
                        body(g, g // 2, g % 2, False, True)
                else:
                    sweep(dve, g0, g0 + NGH, body, ahead, more=True)
                dve.wait_ge(cs, g0 + NGH)

            class Places:

                def __init__(self, layer, half, r, K, nslot):
                    self.w, self.half, self.r, self.K, self.nslot = space[layer, half], half, r, K, nslot
                    self.lo, self.hi = half * NH, (half + 1) * NH

                def begin(self):
                    w, r, lo, hi, half = self.w, self.r, self.lo, self.hi, self.half
                    dve.wait_ge(r.ix, (half + 1) * NGH)
                    for k in range(self.K):
                        L(dve.tensor_tensor(w.oh[k], bcast(iota_e[:, :], 2, NH), bcast(IX[:, lo:hi, k], 1, E), ALU.is_equal))
                    if self.K == 2:
                        ins = dve.tensor_tensor(w.mask, w.oh[0], w.oh[1], ALU.add)
                    else:
                        ins = dve.tensor_copy(w.mask, w.oh[0])
                    ins.then_inc(r.mask, 1)
                    dve.tensor_tensor(by_token(w.w2), MX[:, lo:hi, :], bcast(MX[:, lo:hi, 0], 2, E),
                                      ALU.subtract).then_inc(r.flat, 1)

                def weights(self):
                    w, lo, hi = self.w, self.lo, self.hi
                    dve.wait_ge(self.r.flat, 2 * self.half + 2)
                    ex = by_token(w.w1)
                    den, p1, p2, dn = (wts[:, i, :] for i in range(4))
                    L(dve.tensor_reduce(den, ex, AX_X, ALU.add))
                    L(dve.reciprocal(p1, den))
                    if self.K == 1:
                        L(dve.tensor_copy(GT[:, 0, lo:hi], p1))
                    else:
                        L(dve.tensor_tensor(p2, ex[:, :, 1], p1, ALU.mult))
                        L(dve.scalar_tensor_tensor(dn, p1, TOPK_EPS, p2, ALU.add, ALU.add))
                        L(dve.reciprocal(den, dn))
                        L(dve.tensor_tensor(GT[:, 0, lo:hi], p1, den, ALU.mult))
                        L(dve.tensor_tensor(GT[:, 1, lo:hi], p2, den, ALU.mult))

                def counts(self):
                    w = self.w
                    start, count, ntile, end, corr, tmp = (small[:, i, :] for i in range(6))
                    dve.wait_ge(self.r.ranks_sb, self.half + 1)
                    L(dve.tensor_tensor_scan(flat(w.cum), ones_row[:, 0:EH], flat(w.tot), 0.0, ALU.mult, ALU.add))
                    L(dve.tensor_tensor(start, w.cum[:, :, 0], w.tot[:, :, 0], ALU.subtract))
                    L(dve.tensor_tensor(count, w.cum[:, :, NH - 1], start, ALU.subtract))
                    L(dve.tensor_tensor(w.w2, bcast(count, 2, NH), bcast(iota_t[:, :], 1, E), ALU.is_gt))
                    L(dve.tensor_reduce(ntile, w.w2, AX_X, ALU.add))
                    L(dve.tensor_tensor_scan(end, ones_row[:, 0:E], ntile, 0.0, ALU.mult, ALU.add))
                    L(dve.tensor_tensor(tmp, end, ntile, ALU.subtract))
                    L(dve.scalar_tensor_tensor(corr, tmp, float(P), start, ALU.mult, ALU.subtract))

                def places(self):
                    w = self.w
                    corr = small[:, 4, :]
                    L(dve.tensor_tensor(w.w1, w.cum, w.tot, ALU.subtract))
                    L(dve.tensor_tensor(w.w1, w.w1, bcast(corr, 2, NH), ALU.add))
                    L(dve.tensor_tensor(w.w1, w.rank, w.w1, ALU.add))
                    for k in range(self.K):
                        L(dve.tensor_tensor(w.w2, w.oh[k], w.w1, ALU.mult))
                        L(dve.tensor_reduce(dest_f[:, k, :], w.w2.rearrange("p e t -> p t e"), AX_X, ALU.add))

                def finish(self):
                    w, nslot, half, K = self.w, self.nslot, self.half, self.K
                    L(dve.tensor_copy(dest_i[:, 0:K, self.lo:self.hi], dest_f[:, 0:K, :]))
                    L(dve.tensor_tensor(w.tcmp[0:1, 0:nslot, :], bcast(iota_s[0:1, 0:nslot], 2, E),
                                        bcast(small[0:1, 3, :], 1, nslot), ALU.is_ge))
                    L(dve.tensor_reduce(te[0:1, 0:nslot], w.tcmp[0:1, 0:nslot, :], AX_X, ALU.add))
                    tl = tile_e[:, :, :].rearrange("a h s -> a (h s)")[:, half * nslot:(half + 1) * nslot]
                    dve.tensor_scalar(tl, te[0:1, 0:nslot], float(E - 1), None, ALU.min).then_inc(self.r.tiles, 1)
                    dve.wait_ge(self.r.tiles, half + 1)

                def part(self, i):
                    if i == 0:
                        self.weights()
                    elif i == 1:
                        self.counts()
                    elif i == 2:
                        self.places()
                    elif i == 3:
                        self.finish()

            in_b = [Places(0, half, rb, 1, NSLOT0) for half in range(HALVES)]
            assert NH <= NL - 3 and HALVES == 2
            in_d = [Places(1, half, rd, 2, NSLOT1) for half in range(HALVES)]

            ln_finish(0, NTILE)
            dve.wait_ge(zeroed, ZEROS)
            for half in range(HALVES):
                route(rb, half, bg_sb[:, :], nsb, csb, in_b[half - 1] if half > 0 else None,
                      half * NGH + (2 if half > 0 else 0), min((half + 1) * NGH + 2, NG))
                in_b[half].begin()

            def b3_tile(t):
                if t % 8 == 0:
                    dve.wait_ge(s_gath[0][t // 8], 16 * 8)
                dve.scalar_tensor_tensor(X[:, t, :], XN[:, t, :], GT[:, 0, t:t + 1], X[:, t, :], ALU.mult,
                                         ALU.add).then_inc(b3_x, 1)
                if t % 2 == 1:
                    dve.wait_ge(b3_x, t + 1)
                    for q in (t - 1, t):
                        dve.bn_stats(ST[:, q, :], X[:, q, :]).then_inc(b3_t, 1)

            def b3_finish(half):
                dve.wait_ge(b3_t, (half + 1) * NH)
                ln_finish(half * NH, (half + 1) * NH)

            def b2_dve(g, k, u, first, last):
                tile_list = tile_e[:, :, :].rearrange("a h s -> a (h s)")
                _, er = nc.values_load_multi_w_load_instructions(
                    tile_list[0:1, bass.ds(4 * g, 4)], engines=[DVE_ENGINE], min_val=0, max_val=E - 1,
                    skip_runtime_bounds_check_because="clamped to the last expert where it is computed")
                dve.wait_ge(b2_y, g + 1)
                if not known_below(g, 2):
                    dve.wait_ge(b2_out[u], 16 * k)
                for j in range(4):
                    ins = dve.tensor_tensor(yb[u][:, j, :], bank[6 + u][:, j * P:(j + 1) * P],
                                            bd_sb[:, bass.ds(er[j] * D, D)], ALU.add)
                ins.then_inc(b2_yo, 1)
                ahead_of_end = NB2 - g if isinstance(g, int) else NB2
                if ahead_of_end <= 4:
                    for t in range((4 - ahead_of_end) * NH // 4, (5 - ahead_of_end) * NH // 4):
                        b3_tile(t)
                if ahead_of_end == 1:
                    b3_finish(0)

            for i in range(4):
                in_b[HALVES - 1].part(i)
            sweep(dve, 0, NB2, b2_dve, 2, behind=4)

            for half in range(HALVES):
                def turn(g0, h0):
                    for u in range(2):
                        wait_from(dve, c1_ax, g0)
                        normalise(g0 + u, 4, xn[u][:, 0:4, :], c1_xn, nsg, g0 + u)
                    for u in range(2):
                        dve.wait_ge(c1_h, g0 + u + 1)
                        wait_from(dve, c1_hr, g0)
                        dve.tensor_tensor(hb[u].rearrange("p (b n) -> p b n", n=N),
                                          bank[4 * u + 1][:, :].rearrange("p (b n) -> p b n", n=N),
                                          bcast(bga_sb[:, :], 1, 2), ALU.add).then_inc(c1_hb, 1)
                    for u in range(2):
                        dve.wait_ge(c1_z, g0 + u + 1)
                        wait_from(dve, c1_g, g0)
                        dve.tensor_tensor(zs[u], bank[4 * u + 2][:, :].rearrange("p (a b) -> p a b", b=P),
                                          bcast(g1b_sb[:, :], 1, 4), ALU.add).then_inc(c1_zc, 1)

                turns(dve, half, turn)

                for u in range(2):
                    dve.wait_ge(b2_out[u], 16 * (NB2 // 2))
                for n, (p, t, s, b0, nb) in enumerate(lstm_steps):
                    nw = N // p
                    c = nb * nw
                    gi, gf, gg, go = (gb[s][k][:, 0:c] for k in range(GATES))
                    cc, tc = cst[s][:, 0:c], tcs[s][:, 0:c]
                    steps0, seen = half * NL, half * gates_before[NL] + gates_before[n]
                    dve.wait_ge(l_act, seen + 2)
                    if t == 0:
                        dve.tensor_tensor(cc, gi, gg, ALU.mult).then_inc(l_c, 1)
                    else:
                        dve.tensor_tensor(gi, gi, gg, ALU.mult).then_inc(l_ig, 1)
                        dve.wait_ge(l_act, seen + 3)
                        dve.tensor_tensor(gf, gf, cc, ALU.mult).then_inc(l_ig, 1)
                        dve.wait_ge(l_ig, 2 * (half * sums_before[NL] + sums_before[n]) + 2)
                        dve.tensor_tensor(cc, gi, gf, ALU.add).then_inc(l_c, 1)
                    dve.wait_ge(l_act, seen + len(gates_of(t)))
                    dve.wait_ge(l_tc, steps0 + n + 1)
                    if t == p - 1:
                        dst = F[:, b0 * N:(b0 + nb) * N].rearrange("p (b n) -> p b n", n=N)[:, :, t:t + (nw - 1) * p + 1:p]
                        dve.tensor_tensor(dst, go.rearrange("p (b n) -> p b n", n=nw),
                                          tc.rearrange("p (b n) -> p b n", n=nw), ALU.mult).then_inc(l_h, 1)
                    else:
                        dve.tensor_tensor(hst[s][:, 0:c], go, tc, ALU.mult).then_inc(l_h, 1)
                    if half > 0 and n % 2 == 1:
                        in_d[half - 1].part(n // 2)
                    if half == 0 and n < NH:
                        b3_tile(NH + n)
                    if half == 0 and n == NL - 3:
                        b3_finish(1)

                def turn(g0, h0):
                    for u in range(2):
                        g = g0 + u
                        dve.wait_ge(t_tr, g + 1)
                        xv = X[:, bass.ds(4 * g, 4), :]
                        dve.tensor_tensor(xv, bank[u][:, :].rearrange("p (a b) -> p a b", b=P), xv, ALU.add).then_inc(t_x, 1)
                        dve.wait_ge(t_x, g + 1)
                        for j in range(4):
                            ins = dve.bn_stats(ST[:, bass.ds(4 * g + j, 1), :].rearrange("p a k -> p (a k)"),
                                               X[:, bass.ds(4 * g + j, 1), :].rearrange("p a k -> p (a k)"))
                        ins.then_inc(t_ln, 1)

                turns(dve, half, turn)
                dve.wait_ge(t_ln, (half + 1) * NGH)
                ln_finish(half * NH, (half + 1) * NH)
                dve.wait_ge(t_x, (half + 1) * NGH)
                route(rd, half, None, nsd, csd, None, half * NGH, (half + 1) * NGH)
                in_d[half].begin()

            def d2_rows_out(i, u, j):
                dve.wait_ge(d2_y, i + 1)
                dve.tensor_copy(yd[u][:, j, :], bank[7][:, (j % 4) * P:(j % 4 + 1) * P]).then_inc(d2_yo, 1)

            def d2_dve(g, k, u, first, last):
                for j in range(8):
                    i = 8 * g + j
                    dve.wait_ge(d2_silu, i + 1)
                    if not (first and j < 2):
                        dve.wait_ge(d2_tt, i - 1)
                    dve.tensor_tensor(hm[j % 2], sl[j % 2], bank[3 + 2 * (j % 2)][:, 0:UP], ALU.mult).then_inc(d2_m, 1)
                    if j % 2 == 1 and first:
                        in_d[HALVES - 1].part(j // 2)
                    if j == 2 and not known_below(g, 2):
                        dve.wait_ge(d2_out[u], 16 * k)
                    if j >= 2:
                        d2_rows_out(i - 2, u, j - 2)
                    elif not first:
                        d2_rows_out(i - 2, 1 - u, j + 6)
                if last:
                    for j in (6, 7):
                        d2_rows_out(8 * g + j, u, j)

            sweep(dve, 0, ND2, d2_dve, 2)
            for g in range(NX):
                dve.wait_ge(s_gath[1][g], 16 * 16)
                for k in range(2):
                    for t in range(8 * g, 8 * g + 8):
                        src = XN[:, t, :] if k == 0 else Y1[t // NH][:, t % NH, :]
                        if k == 1:
                            dve.wait_ge(d3_x, 16 * g + t % 8 + 1)
                        dve.scalar_tensor_tensor(X[:, t, :], src, GT[:, k, t:t + 1], X[:, t, :], ALU.mult,
                                                 ALU.add).then_inc(d3_x, 1)


def layouts(i):
    import numpy as np
    c = np.ascontiguousarray
    N = i["adj"].shape[0]
    E, H, C = i["L1_ffn_w1"].shape
    S, G4, Dh = i["L1_gnn_Wih"].shape
    x = c(i["x"].reshape(-1, i["x"].shape[-1]))
    return dict(
        x=x, adj_t=c(i["adj"].T),
        bias_io=c(np.concatenate([i["L0_gnn_bias_in"], i["L0_gnn_bias_out"]], axis=1)),
        gate_w=c(np.concatenate([i["L0_gnn_gate_w_in"], i["L0_gnn_gate_w_out"], i["L0_gnn_loop_gate"]], axis=1)),
        gate_b=c(np.concatenate([i["L0_gnn_gate_b_in"], i["L0_gnn_gate_b_out"],
                                 np.zeros((N, 1), i["L0_gnn_gate_b_in"].dtype)], axis=1)),
        w1=c(i["L0_ffn_W1"]), b1=c(i["L0_ffn_b1"].reshape(-1, 128).T), wg=c(i["L0_ffn_Wg"]), bg=c(i["L0_ffn_bg"]),
        wd=c(np.transpose(i["L0_ffn_Wd"], (1, 0, 2)).reshape(i["L0_ffn_Wd"].shape[1], -1)),
        bd=c(i["L0_ffn_bd"].reshape(-1)),
        g0_w=c(i["L1_gnn_Wg0"]), g0_b=c(i["L1_gnn_bg0"].reshape(-1, 1)), g1_w=c(i["L1_gnn_Wg1"]), g1_b=c(i["L1_gnn_bg1"]),
        wih_t=c(np.transpose(i["L1_gnn_Wih"], (0, 2, 1))), whh_t=c(np.transpose(i["L1_gnn_Whh"], (0, 2, 1))),
        bih=c(i["L1_gnn_bih"].reshape(-1, 128).T), bhh=c(i["L1_gnn_bhh"].reshape(-1, 128).T),
        router_t=c(i["L1_ffn_router_w"].T),
        up_t=c(np.concatenate([np.transpose(i["L1_ffn_w1"], (0, 2, 1)), np.transpose(i["L1_ffn_w3"], (0, 2, 1))], axis=2)),
        down_t=c(np.transpose(i["L1_ffn_w2"], (0, 2, 1))),
    )


def kernel(**inputs):
    import concourse.bacc as bacc
    import numpy as np
    from concourse.bass_utils import run_bass_kernel_spmd

    shape = inputs["x"].shape
    arrays = layouts({name: np.asarray(a) for name, a in inputs.items()})
    nc = bacc.Bacc("TRN2", target_bir_lowering=False, num_devices=1)
    aps = [nc.dram_tensor(name, a.shape, mybir.dt.from_np(a.dtype), kind="ExternalInput").ap()
           for name, a in arrays.items()]
    out = nc.dram_tensor("out", arrays["x"].shape, F32, kind="ExternalOutput").ap()
    build(nc, *aps, out)
    result = run_bass_kernel_spmd(nc, [arrays], core_ids=[0])
    return result.results[0]["out"].reshape(shape)
```
